# Optimizing a Trainium2 kernel written in Bass

```python
import numpy as np
import jax
import jax.numpy as jnp

def _softmax(x, axis=-1):
    return jax.nn.softmax(x, axis=axis)

def _gelu(x):
    return jax.nn.gelu(x, approximate=True)

def _silu(x):
    return jax.nn.silu(x)

def _sigmoid(x):
    return jax.nn.sigmoid(x)

def _layernorm(x, axis=-1, eps=1e-05):
    m = jnp.mean(x, axis=axis, keepdims=True)
    v = jnp.var(x, axis=axis, keepdims=True)
    return (x - m) / jnp.sqrt(v + eps)

def _scatter_add(tgt, idx, src, axis=0):
    return tgt.at[idx].add(src)

def _segment_sum(src, seg, n):
    return jax.ops.segment_sum(src, seg, n)
kernel_name = 'mk_seq_preln_d2_jaxref_r8_099da6'

def setup_inputs(seed: int=0):
    np.random.seed(seed)
    _w = jnp.asarray

    def _L0_attn_setup():
        import jax, jax.numpy as jnp
        import numpy as np
        D_MODEL, D_STATE, D_CONV, EXPAND, NHEADS, NGROUPS = (128, 16, 4, 2, 8, 1)
        D_INNER = D_MODEL * EXPAND
        HEADDIM = D_INNER // NHEADS
        D_XBC = D_INNER + 2 * NGROUPS * D_STATE
        D_IN_PROJ = 3 * D_INNER + D_XBC + NHEADS
        BATCH, SEQLEN = (2, 256)
        LN_EPS = 1e-05

        def _silu(x):
            return x * jax.nn.sigmoid(x)
        key = jax.random.key(seed)
        ks = jax.random.split(key, 8)
        u = jax.random.normal(ks[0], (BATCH, SEQLEN, D_MODEL), dtype=jnp.float32)
        W_in = jax.random.normal(ks[1], (D_IN_PROJ, D_MODEL), jnp.float32) / np.sqrt(D_MODEL)
        conv_w = jax.random.normal(ks[2], (D_XBC, 1, D_CONV), jnp.float32) / np.sqrt(D_CONV)
        conv_b = jnp.zeros((D_XBC,), jnp.float32)
        dt = jnp.exp(jax.random.uniform(ks[3], (NHEADS,)) * (np.log(0.1) - np.log(0.001)) + np.log(0.001))
        dt_bias = dt + jnp.log(-jnp.expm1(-dt))
        A_log = jnp.log(jax.random.uniform(ks[4], (NHEADS,), minval=0.9, maxval=0.999))
        D_param = jnp.ones((NHEADS,), jnp.float32)
        ln_gamma = jnp.ones((D_INNER,), jnp.float32)
        ln_beta = jnp.zeros((D_INNER,), jnp.float32)
        W_gate = jax.random.normal(ks[5], (D_INNER, D_INNER), jnp.float32) / np.sqrt(D_INNER)
        b_gate = jnp.zeros((D_INNER,), jnp.float32)
        W_out = jax.random.normal(ks[6], (D_MODEL, 2 * D_INNER), jnp.float32) / np.sqrt(2 * D_INNER)
        return dict(u=u, W_in=W_in, conv_w=conv_w, conv_b=conv_b, dt_bias=dt_bias, A_log=A_log, D_param=D_param, ln_gamma=ln_gamma, ln_beta=ln_beta, W_gate=W_gate, b_gate=b_gate, W_out=W_out)
    _L0_attn_in = _L0_attn_setup()

    def _L0_ffn_setup():
        import jax, jax.numpy as jnp
        import numpy as np
        D_MODEL = 128
        N_HEADS = 16
        HEAD_DIM = D_MODEL // N_HEADS
        FFN_DIM = 512
        N_EXPERTS = 8
        TOP_K = 2
        BATCH = 4
        SEQ = 128

        def _layernorm(x, w, b, eps=1e-05):
            mu = jnp.mean(x, axis=-1, keepdims=True)
            var = jnp.mean(jnp.square(x - mu), axis=-1, keepdims=True)
            return (x - mu) * jax.lax.rsqrt(var + eps) * w + b

        def _causal_attention(nx, Wqkv, bqkv, Wo, bo):
            B, S, D = nx.shape
            qkv = nx @ Wqkv + bqkv
            q, k, v = jnp.split(qkv, 3, axis=-1)
            q = q.reshape(B, S, N_HEADS, HEAD_DIM)
            k = k.reshape(B, S, N_HEADS, HEAD_DIM)
            v = v.reshape(B, S, N_HEADS, HEAD_DIM)
            scores = jnp.einsum('bqhd,bkhd->bhqk', q, k) / jnp.sqrt(jnp.float32(HEAD_DIM))
            causal = jnp.tril(jnp.ones((S, S), bool))
            scores = jnp.where(causal, scores, jnp.finfo(scores.dtype).min)
            attn = jax.nn.softmax(scores, axis=-1)
            out = jnp.einsum('bhqk,bkhd->bqhd', attn, v).reshape(B, S, D)
            return out @ Wo + bo

        def _moe_ffn(nx, gate_W, fc1_w, fc1_b, fc2_w, fc2_b):
            gate_logits = nx @ gate_W
            topk_vals, topk_idx = jax.lax.top_k(gate_logits, TOP_K)
            gate_w = jax.nn.softmax(topk_vals, axis=-1)
            dense_gates = jnp.sum(jax.nn.one_hot(topk_idx, N_EXPERTS, dtype=nx.dtype) * gate_w[..., None], axis=-2)
            moe_out = jnp.zeros_like(nx)
            for e in range(N_EXPERTS):
                h = jax.nn.gelu(jnp.einsum('bsd,fd->bsf', nx, fc1_w[e]) + fc1_b[e], approximate=False)
                y = jnp.einsum('bsf,df->bsd', h, fc2_w[e]) + fc2_b[e]
                moe_out = moe_out + y * dense_gates[..., e:e + 1]
            return moe_out
        key = jax.random.key(seed)
        ks = jax.random.split(key, 12)
        s = lambda k, shape, scale: jax.random.normal(k, shape, dtype=jnp.float32) * scale
        inp = {'x': s(ks[0], (BATCH, SEQ, D_MODEL), 1.0), 'ln1_w': jnp.ones((D_MODEL,), jnp.float32), 'ln1_b': jnp.zeros((D_MODEL,), jnp.float32), 'ln2_w': jnp.ones((D_MODEL,), jnp.float32), 'ln2_b': jnp.zeros((D_MODEL,), jnp.float32), 'Wqkv': s(ks[1], (D_MODEL, 3 * D_MODEL), 0.02), 'bqkv': jnp.zeros((3 * D_MODEL,), jnp.float32), 'Wo': s(ks[2], (D_MODEL, D_MODEL), 0.02), 'bo': jnp.zeros((D_MODEL,), jnp.float32), 'gate_W': s(ks[3], (D_MODEL, N_EXPERTS), 0.02), 'fc1_w': s(ks[4], (N_EXPERTS, FFN_DIM, D_MODEL), (2.0 / D_MODEL) ** 0.5), 'fc1_b': jnp.zeros((N_EXPERTS, FFN_DIM), jnp.float32), 'fc2_w': s(ks[5], (N_EXPERTS, D_MODEL, FFN_DIM), (1.0 / FFN_DIM) ** 0.5), 'fc2_b': jnp.zeros((N_EXPERTS, D_MODEL), jnp.float32)}
        return inp
    _L0_ffn_in = _L0_ffn_setup()

    def _L1_attn_setup():
        import jax, jax.numpy as jnp
        import numpy as np
        D_MODEL, D_STATE, D_CONV, EXPAND = (128, 16, 4, 2)
        D_INNER = EXPAND * D_MODEL
        BATCH, LENGTH = (2, 128)

        def _mamba_fwd(x, in_proj_w, in_proj_b, conv_w, conv_b, x_proj_w, x_proj_b, dt_proj_w, dt_proj_b, D, out_proj_w, out_proj_b):
            batch, length, _ = x.shape
            d_inner = D.shape[0]
            d_state = dt_proj_w.shape[0]
            d_conv = conv_w.shape[-1]
            xz = x @ in_proj_w + in_proj_b
            xc, z = jnp.split(xz, 2, axis=-1)
            xc_bdl = jnp.transpose(xc, (0, 2, 1))
            xc_bdl = jax.lax.conv_general_dilated(xc_bdl, conv_w, window_strides=(1,), padding=[(d_conv - 1, 0)], dimension_numbers=('NCH', 'OIH', 'NCH'), feature_group_count=d_inner)
            xc_bdl = xc_bdl + conv_b[None, :, None]
            xc = jnp.transpose(xc_bdl, (0, 2, 1))
            xc = jax.nn.silu(xc)
            dBu = xc @ x_proj_w + x_proj_b
            delta_s, B, u = jnp.split(dBu, [d_state, 2 * d_state], axis=-1)
            delta = jax.nn.softplus(delta_s @ dt_proj_w + dt_proj_b)
            A = -jnp.arange(1, d_state + 1, dtype=x.dtype)
            deltaA = jnp.exp(delta[..., None] * A)
            deltaB_u = delta[..., None] * B[:, :, None, :] * u[..., None]
            dA_t = jnp.moveaxis(deltaA, 1, 0)
            dBu_t = jnp.moveaxis(deltaB_u, 1, 0)

            def step(h, inp):
                dA, dBu_ = inp
                h = dA * h + dBu_
                return (h, h.sum(-1))
            h0 = jnp.zeros((batch, d_inner, d_state), x.dtype)
            _, y_t = jax.lax.scan(step, h0, (dA_t, dBu_t))
            y = jnp.moveaxis(y_t, 0, 1)
            y = y + u * D
            y = y * jax.nn.silu(z)
            return y @ out_proj_w + out_proj_b
        key = jax.random.key(seed)
        ks = jax.random.split(key, 12)
        s = lambda fan_in: 1.0 / np.sqrt(fan_in)
        return {'x': jax.random.normal(ks[0], (BATCH, LENGTH, D_MODEL), jnp.float32), 'in_proj_w': jax.random.normal(ks[1], (D_MODEL, 2 * D_INNER), jnp.float32) * s(D_MODEL), 'in_proj_b': jax.random.normal(ks[2], (2 * D_INNER,), jnp.float32) * s(D_MODEL), 'conv_w': jax.random.normal(ks[3], (D_INNER, 1, D_CONV), jnp.float32) * s(D_CONV), 'conv_b': jax.random.normal(ks[4], (D_INNER,), jnp.float32) * s(D_CONV), 'x_proj_w': jax.random.normal(ks[5], (D_INNER, 2 * D_STATE + D_INNER), jnp.float32) * s(D_INNER), 'x_proj_b': jax.random.normal(ks[6], (2 * D_STATE + D_INNER,), jnp.float32) * s(D_INNER), 'dt_proj_w': jax.random.normal(ks[7], (D_STATE, D_INNER), jnp.float32) * s(D_STATE), 'dt_proj_b': jax.random.normal(ks[8], (D_INNER,), jnp.float32) * s(D_STATE), 'D': jnp.ones((D_INNER,), jnp.float32), 'out_proj_w': jax.random.normal(ks[9], (D_INNER, D_MODEL), jnp.float32) * s(D_INNER), 'out_proj_b': jax.random.normal(ks[10], (D_MODEL,), jnp.float32) * s(D_INNER)}
    _L1_attn_in = _L1_attn_setup()

    def _L1_ffn_setup():
        import jax, jax.numpy as jnp
        import numpy as np
        D_IN, D_HID = (128, 512)

        def _ternary(key, shape):
            return jax.random.randint(key, shape, -1, 2).astype(jnp.float32)

        def _tlin(x, w, s):
            return jnp.einsum('bsi,oi->bso', x, w) * s
        key = jax.random.key(seed)
        ks = jax.random.split(key, 12)
        inv = lambda fan: 1.0 / np.sqrt(fan).astype(np.float32)
        return {'x': jax.random.normal(ks[0], (4, 256, D_IN), dtype=jnp.float32), 'w1_w': _ternary(ks[1], (D_HID, D_IN)), 'w1_s': jax.random.uniform(ks[2], (D_HID,), dtype=jnp.float32) * inv(D_IN), 'w2_w': _ternary(ks[3], (D_HID, D_IN)), 'w2_s': jax.random.uniform(ks[4], (D_HID,), dtype=jnp.float32) * inv(D_IN), 'h1_w': _ternary(ks[5], (D_HID, D_HID)), 'h1_s': jax.random.uniform(ks[6], (D_HID,), dtype=jnp.float32) * inv(D_HID), 'h2_w': _ternary(ks[7], (D_HID, D_HID)), 'h2_s': jax.random.uniform(ks[8], (D_HID,), dtype=jnp.float32) * inv(D_HID), 'w3_w': _ternary(ks[9], (D_IN, D_HID)), 'w3_s': jax.random.uniform(ks[10], (D_IN,), dtype=jnp.float32) * inv(D_HID)}
    _L1_ffn_in = _L1_ffn_setup()
    _d = {'L0_attn_u': _L0_attn_in['u'], 'L0_attn_W_in': _L0_attn_in['W_in'], 'L0_attn_conv_w': _L0_attn_in['conv_w'], 'L0_attn_conv_b': _L0_attn_in['conv_b'], 'L0_attn_dt_bias': _L0_attn_in['dt_bias'], 'L0_attn_A_log': _L0_attn_in['A_log'], 'L0_attn_D_param': _L0_attn_in['D_param'], 'L0_attn_ln_gamma': _L0_attn_in['ln_gamma'], 'L0_attn_ln_beta': _L0_attn_in['ln_beta'], 'L0_attn_W_gate': _L0_attn_in['W_gate'], 'L0_attn_b_gate': _L0_attn_in['b_gate'], 'L0_attn_W_out': _L0_attn_in['W_out'], 'L0_ffn_ln1_w': _L0_ffn_in['ln1_w'], 'L0_ffn_ln1_b': _L0_ffn_in['ln1_b'], 'L0_ffn_ln2_w': _L0_ffn_in['ln2_w'], 'L0_ffn_ln2_b': _L0_ffn_in['ln2_b'], 'L0_ffn_Wqkv': _L0_ffn_in['Wqkv'], 'L0_ffn_bqkv': _L0_ffn_in['bqkv'], 'L0_ffn_Wo': _L0_ffn_in['Wo'], 'L0_ffn_bo': _L0_ffn_in['bo'], 'L0_ffn_gate_W': _L0_ffn_in['gate_W'], 'L0_ffn_fc1_w': _L0_ffn_in['fc1_w'], 'L0_ffn_fc1_b': _L0_ffn_in['fc1_b'], 'L0_ffn_fc2_w': _L0_ffn_in['fc2_w'], 'L0_ffn_fc2_b': _L0_ffn_in['fc2_b'], 'L1_attn_in_proj_w': _L1_attn_in['in_proj_w'], 'L1_attn_in_proj_b': _L1_attn_in['in_proj_b'], 'L1_attn_conv_w': _L1_attn_in['conv_w'], 'L1_attn_conv_b': _L1_attn_in['conv_b'], 'L1_attn_x_proj_w': _L1_attn_in['x_proj_w'], 'L1_attn_x_proj_b': _L1_attn_in['x_proj_b'], 'L1_attn_dt_proj_w': _L1_attn_in['dt_proj_w'], 'L1_attn_dt_proj_b': _L1_attn_in['dt_proj_b'], 'L1_attn_D': _L1_attn_in['D'], 'L1_attn_out_proj_w': _L1_attn_in['out_proj_w'], 'L1_attn_out_proj_b': _L1_attn_in['out_proj_b'], 'L1_ffn_w1_w': _L1_ffn_in['w1_w'], 'L1_ffn_w1_s': _L1_ffn_in['w1_s'], 'L1_ffn_w2_w': _L1_ffn_in['w2_w'], 'L1_ffn_w2_s': _L1_ffn_in['w2_s'], 'L1_ffn_h1_w': _L1_ffn_in['h1_w'], 'L1_ffn_h1_s': _L1_ffn_in['h1_s'], 'L1_ffn_h2_w': _L1_ffn_in['h2_w'], 'L1_ffn_h2_s': _L1_ffn_in['h2_s'], 'L1_ffn_w3_w': _L1_ffn_in['w3_w'], 'L1_ffn_w3_s': _L1_ffn_in['w3_s']}
    _x0 = _d['L0_attn_u']
    _d['L0_attn_u'] = jax.random.normal(jax.random.fold_in(jax.random.key(seed), 1), (1, 2048, 128), dtype=_x0.dtype)
    del _x0
    return _d

def reference(L0_attn_u, L0_attn_W_in, L0_attn_conv_w, L0_attn_conv_b, L0_attn_dt_bias, L0_attn_A_log, L0_attn_D_param, L0_attn_ln_gamma, L0_attn_ln_beta, L0_attn_W_gate, L0_attn_b_gate, L0_attn_W_out, L0_ffn_ln1_w, L0_ffn_ln1_b, L0_ffn_ln2_w, L0_ffn_ln2_b, L0_ffn_Wqkv, L0_ffn_bqkv, L0_ffn_Wo, L0_ffn_bo, L0_ffn_gate_W, L0_ffn_fc1_w, L0_ffn_fc1_b, L0_ffn_fc2_w, L0_ffn_fc2_b, L1_attn_in_proj_w, L1_attn_in_proj_b, L1_attn_conv_w, L1_attn_conv_b, L1_attn_x_proj_w, L1_attn_x_proj_b, L1_attn_dt_proj_w, L1_attn_dt_proj_b, L1_attn_D, L1_attn_out_proj_w, L1_attn_out_proj_b, L1_ffn_w1_w, L1_ffn_w1_s, L1_ffn_w2_w, L1_ffn_w2_s, L1_ffn_h1_w, L1_ffn_h1_s, L1_ffn_h2_w, L1_ffn_h2_s, L1_ffn_w3_w, L1_ffn_w3_s):

    def _L0_attn_ref(u, W_in, conv_w, conv_b, dt_bias, A_log, D_param, ln_gamma, ln_beta, W_gate, b_gate, W_out):
        import jax, jax.numpy as jnp
        import numpy as np
        D_MODEL, D_STATE, D_CONV, EXPAND, NHEADS, NGROUPS = (128, 16, 4, 2, 8, 1)
        D_INNER = D_MODEL * EXPAND
        HEADDIM = D_INNER // NHEADS
        D_XBC = D_INNER + 2 * NGROUPS * D_STATE
        D_IN_PROJ = 3 * D_INNER + D_XBC + NHEADS
        BATCH, SEQLEN = (2, 256)
        LN_EPS = 1e-05

        def _silu(x):
            return x * jax.nn.sigmoid(x)
        B, L, _ = u.shape
        zxbcdt = u @ W_in.T
        z0 = zxbcdt[..., :D_INNER]
        x0 = zxbcdt[..., D_INNER:2 * D_INNER]
        xBC = zxbcdt[..., 3 * D_INNER:3 * D_INNER + D_XBC]
        dt = jax.nn.softplus(zxbcdt[..., -NHEADS:] + dt_bias)
        A = -jnp.exp(A_log)
        xBC_c = jnp.transpose(xBC, (0, 2, 1))
        xBC_c = jax.lax.conv_general_dilated(xBC_c, conv_w, window_strides=(1,), padding=[(D_CONV - 1, 0)], dimension_numbers=('NCH', 'OIH', 'NCH'), feature_group_count=D_XBC)
        xBC = _silu(jnp.transpose(xBC_c, (0, 2, 1)) + conv_b)
        x = xBC[..., :D_INNER].reshape(B, L, NHEADS, HEADDIM)
        Bm = xBC[..., D_INNER:D_INNER + D_STATE]
        Cm = xBC[..., D_INNER + D_STATE:]

        def step(h, inp):
            x_t, B_t, C_t, dt_t = inp
            dA = jnp.exp(dt_t * A)[:, :, None, None]
            h = dA * h + dt_t[:, :, None, None] * x_t[..., None] * B_t[:, None, None, :]
            y_t = jnp.einsum('bhpn,bn->bhp', h, C_t) + D_param[None, :, None] * x_t
            return (h, y_t)
        h0 = jnp.zeros((B, NHEADS, HEADDIM, D_STATE), u.dtype)
        xs = (jnp.moveaxis(x, 1, 0), jnp.moveaxis(Bm, 1, 0), jnp.moveaxis(Cm, 1, 0), jnp.moveaxis(dt, 1, 0))
        _, y = jax.lax.scan(step, h0, xs)
        y = jnp.moveaxis(y, 0, 1).reshape(B, L, D_INNER)
        mu = y.mean(-1, keepdims=True)
        var = ((y - mu) ** 2).mean(-1, keepdims=True)
        y = (y - mu) * jax.lax.rsqrt(var + LN_EPS) * ln_gamma + ln_beta
        gate = jax.nn.sigmoid(y @ W_gate.T + b_gate)
        y = gate * y
        mlp_skip = _silu(z0) * x0
        return jnp.concatenate([mlp_skip, y], axis=-1) @ W_out.T

    def _L0_ffn_ref(x, ln1_w, ln1_b, ln2_w, ln2_b, Wqkv, bqkv, Wo, bo, gate_W, fc1_w, fc1_b, fc2_w, fc2_b):
        import jax, jax.numpy as jnp
        import numpy as np
        D_MODEL = 128
        N_HEADS = 16
        HEAD_DIM = D_MODEL // N_HEADS
        FFN_DIM = 512
        N_EXPERTS = 8
        TOP_K = 2
        BATCH = 4
        SEQ = 128

        def _layernorm(x, w, b, eps=1e-05):
            mu = jnp.mean(x, axis=-1, keepdims=True)
            var = jnp.mean(jnp.square(x - mu), axis=-1, keepdims=True)
            return (x - mu) * jax.lax.rsqrt(var + eps) * w + b

        def _causal_attention(nx, Wqkv, bqkv, Wo, bo):
            B, S, D = nx.shape
            qkv = nx @ Wqkv + bqkv
            q, k, v = jnp.split(qkv, 3, axis=-1)
            q = q.reshape(B, S, N_HEADS, HEAD_DIM)
            k = k.reshape(B, S, N_HEADS, HEAD_DIM)
            v = v.reshape(B, S, N_HEADS, HEAD_DIM)
            scores = jnp.einsum('bqhd,bkhd->bhqk', q, k) / jnp.sqrt(jnp.float32(HEAD_DIM))
            causal = jnp.tril(jnp.ones((S, S), bool))
            scores = jnp.where(causal, scores, jnp.finfo(scores.dtype).min)
            attn = jax.nn.softmax(scores, axis=-1)
            out = jnp.einsum('bhqk,bkhd->bqhd', attn, v).reshape(B, S, D)
            return out @ Wo + bo

        def _moe_ffn(nx, gate_W, fc1_w, fc1_b, fc2_w, fc2_b):
            gate_logits = nx @ gate_W
            topk_vals, topk_idx = jax.lax.top_k(gate_logits, TOP_K)
            gate_w = jax.nn.softmax(topk_vals, axis=-1)
            dense_gates = jnp.sum(jax.nn.one_hot(topk_idx, N_EXPERTS, dtype=nx.dtype) * gate_w[..., None], axis=-2)
            moe_out = jnp.zeros_like(nx)
            for e in range(N_EXPERTS):
                h = jax.nn.gelu(jnp.einsum('bsd,fd->bsf', nx, fc1_w[e]) + fc1_b[e], approximate=False)
                y = jnp.einsum('bsf,df->bsd', h, fc2_w[e]) + fc2_b[e]
                moe_out = moe_out + y * dense_gates[..., e:e + 1]
            return moe_out
        nx = _layernorm(x, ln1_w, ln1_b)
        attn_out = _causal_attention(nx, Wqkv, bqkv, Wo, bo)
        x = x + attn_out
        nx2 = _layernorm(x, ln2_w, ln2_b)
        moe_out = _moe_ffn(nx2, gate_W, fc1_w, fc1_b, fc2_w, fc2_b)
        return x + moe_out

    def _L1_attn_ref(x, in_proj_w, in_proj_b, conv_w, conv_b, x_proj_w, x_proj_b, dt_proj_w, dt_proj_b, D, out_proj_w, out_proj_b):
        import jax, jax.numpy as jnp
        import numpy as np
        D_MODEL, D_STATE, D_CONV, EXPAND = (128, 16, 4, 2)
        D_INNER = EXPAND * D_MODEL
        BATCH, LENGTH = (2, 128)

        def _mamba_fwd(x, in_proj_w, in_proj_b, conv_w, conv_b, x_proj_w, x_proj_b, dt_proj_w, dt_proj_b, D, out_proj_w, out_proj_b):
            batch, length, _ = x.shape
            d_inner = D.shape[0]
            d_state = dt_proj_w.shape[0]
            d_conv = conv_w.shape[-1]
            xz = x @ in_proj_w + in_proj_b
            xc, z = jnp.split(xz, 2, axis=-1)
            xc_bdl = jnp.transpose(xc, (0, 2, 1))
            xc_bdl = jax.lax.conv_general_dilated(xc_bdl, conv_w, window_strides=(1,), padding=[(d_conv - 1, 0)], dimension_numbers=('NCH', 'OIH', 'NCH'), feature_group_count=d_inner)
            xc_bdl = xc_bdl + conv_b[None, :, None]
            xc = jnp.transpose(xc_bdl, (0, 2, 1))
            xc = jax.nn.silu(xc)
            dBu = xc @ x_proj_w + x_proj_b
            delta_s, B, u = jnp.split(dBu, [d_state, 2 * d_state], axis=-1)
            delta = jax.nn.softplus(delta_s @ dt_proj_w + dt_proj_b)
            A = -jnp.arange(1, d_state + 1, dtype=x.dtype)
            deltaA = jnp.exp(delta[..., None] * A)
            deltaB_u = delta[..., None] * B[:, :, None, :] * u[..., None]
            dA_t = jnp.moveaxis(deltaA, 1, 0)
            dBu_t = jnp.moveaxis(deltaB_u, 1, 0)

            def step(h, inp):
                dA, dBu_ = inp
                h = dA * h + dBu_
                return (h, h.sum(-1))
            h0 = jnp.zeros((batch, d_inner, d_state), x.dtype)
            _, y_t = jax.lax.scan(step, h0, (dA_t, dBu_t))
            y = jnp.moveaxis(y_t, 0, 1)
            y = y + u * D
            y = y * jax.nn.silu(z)
            return y @ out_proj_w + out_proj_b
        return _mamba_fwd(x, in_proj_w, in_proj_b, conv_w, conv_b, x_proj_w, x_proj_b, dt_proj_w, dt_proj_b, D, out_proj_w, out_proj_b)

    def _L1_ffn_ref(x, w1_w, w1_s, w2_w, w2_s, h1_w, h1_s, h2_w, h2_s, w3_w, w3_s):
        import jax, jax.numpy as jnp
        import numpy as np
        D_IN, D_HID = (128, 512)

        def _ternary(key, shape):
            return jax.random.randint(key, shape, -1, 2).astype(jnp.float32)

        def _tlin(x, w, s):
            return jnp.einsum('bsi,oi->bso', x, w) * s
        h = jax.nn.silu(_tlin(x, w1_w, w1_s)) * _tlin(x, w2_w, w2_s)
        h = jax.nn.gelu(_tlin(h, h1_w, h1_s), approximate=False)
        h = jax.nn.gelu(_tlin(h, h2_w, h2_s), approximate=False)
        return _tlin(h, w3_w, w3_s)
    x = L0_attn_u
    x = x + _L0_attn_ref(_layernorm(x, axis=-1), L0_attn_W_in, L0_attn_conv_w, L0_attn_conv_b, L0_attn_dt_bias, L0_attn_A_log, L0_attn_D_param, L0_attn_ln_gamma, L0_attn_ln_beta, L0_attn_W_gate, L0_attn_b_gate, L0_attn_W_out)
    x = x + _L0_ffn_ref(_layernorm(x, axis=-1), L0_ffn_ln1_w, L0_ffn_ln1_b, L0_ffn_ln2_w, L0_ffn_ln2_b, L0_ffn_Wqkv, L0_ffn_bqkv, L0_ffn_Wo, L0_ffn_bo, L0_ffn_gate_W, L0_ffn_fc1_w, L0_ffn_fc1_b, L0_ffn_fc2_w, L0_ffn_fc2_b)
    x = x + _L1_attn_ref(_layernorm(x, axis=-1), L1_attn_in_proj_w, L1_attn_in_proj_b, L1_attn_conv_w, L1_attn_conv_b, L1_attn_x_proj_w, L1_attn_x_proj_b, L1_attn_dt_proj_w, L1_attn_dt_proj_b, L1_attn_D, L1_attn_out_proj_w, L1_attn_out_proj_b)
    x = x + _L1_ffn_ref(_layernorm(x, axis=-1), L1_ffn_w1_w, L1_ffn_w1_s, L1_ffn_w2_w, L1_ffn_w2_s, L1_ffn_h1_w, L1_ffn_h1_s, L1_ffn_h2_w, L1_ffn_h2_s, L1_ffn_w3_w, L1_ffn_w3_s)
    return x

_drawn_inputs = setup_inputs


def setup_inputs(seed=0):
    import zlib

    import numpy as np

    out = dict(_drawn_inputs(seed))
    spreads = {'L0_attn_conv_b': (0.0, 0.1),
     'L0_attn_D_param': (1.0, 0.2),
     'L0_attn_ln_gamma': (1.0, 0.2),
     'L0_attn_ln_beta': (0.0, 0.1),
     'L0_attn_b_gate': (0.0, 0.1),
     'L0_ffn_ln1_w': (1.0, 0.2),
     'L0_ffn_ln1_b': (0.0, 0.1),
     'L0_ffn_ln2_w': (1.0, 0.2),
     'L0_ffn_ln2_b': (0.0, 0.1),
     'L0_ffn_bqkv': (0.0, 0.1),
     'L0_ffn_bo': (0.0, 0.1),
     'L0_ffn_fc1_b': (0.0, 0.1),
     'L0_ffn_fc2_b': (0.0, 0.1),
     'L1_attn_D': (1.0, 0.2)}
    factors = {}
    for name, (base, spread) in spreads.items():
        noise = np.random.default_rng([zlib.crc32(name.encode()), seed]).standard_normal(out[name].shape)
        drawn = base * np.exp(spread * noise) if base else spread * noise
        out[name] = jnp.asarray(drawn.astype(out[name].dtype))
    for name, factor in factors.items():
        out[name] = (out[name] * factor).astype(out[name].dtype)
    return out
```

```python
from contextlib import ExitStack

import concourse.bass as bass
from concourse import mybir

F32 = mybir.dt.float32
F32R = mybir.dt.float32r
BF16 = mybir.dt.bfloat16
ALU = mybir.AluOpType
ACT = mybir.ActivationFunctionType
AX = mybir.AxisListType

P = 128
T = 2048
D = 128
BLK = 512
NB = T // BLK
TPB = BLK // P
NT = T // P
EPS = 1e-5
NEG = -1e30

H0, HD0, NS0, CONV = 8, 32, 16, 4
DI = 256
HA, HDA = 16, 8
NE, FF = 8, 512
FC = FF // P
NS1 = 16
HID = 512
HC = HID // P

XA, XB, BREP, CREP, DTREP, Z0A, Z0B, X0A, X0B = range(9)

_COLS = [
    ("conv0_w", 4 * CONV), ("conv0_b", 4), ("dt_bias", 1), ("a_log", 1), ("d0", 2), ("gamma", 2), ("beta", 2),
    ("b_gate", 2), ("ln1_w", 1), ("ln1_b", 1), ("ln2_w", 1), ("ln2_b", 1), ("bq", 1), ("bk", 1),
    ("fc1_b", NE * FC), ("in1_b", 4), ("conv1_w", 2 * CONV), ("conv1_b", 2), ("xu_b", 2), ("xd_b", 1),
    ("xB_b", 1), ("dt1_b", 2), ("d1", 2), ("w1_s", HC), ("w2_s", HC), ("h1_s", HC), ("h2_s", HC), ("w3_s", 1),
    ("out1_b", 1),
]
COL = {}
_n = 0
for _name, _w in _COLS:
    COL[_name] = _n
    _n += _w
NCOL = _n


class Order:

    def __init__(self, eng, sem):
        self.eng, self.sem, self.n = eng, sem, 0

    def did(self, ins):
        ins.then_inc(self.sem, 1)
        self.n += 1
        return self.n

    def wait(self, n=None):
        self.eng.wait_ge(self.sem, self.n if n is None else n)


class Ring:

    def __init__(self, eng, banks):
        self.eng, self.banks, self.emptied = eng, banks, []

    def take(self, *emptied_when):
        n = len(self.emptied)
        if n >= len(self.banks):
            for sem, value in self.emptied[n - len(self.banks)]:
                self.eng.wait_ge(sem, value)
        self.emptied.append(emptied_when)
        return self.banks[n % len(self.banks)]

    def drain(self):
        for uses in self.emptied[-len(self.banks):]:
            for sem, value in uses:
                self.eng.wait_ge(sem, value)


class Fillings:

    def __init__(self, banks, names, emptied):
        self.banks, self.names, self.emptied = banks, names, emptied
        self.at = {name: n for n, name in enumerate(names)}

    def bank(self, *name):
        return self.banks[self.at[name] % len(self.banks)]

    def take(self, pe, *name):
        n = self.at[name]
        if n >= len(self.banks):
            pe.wait_ge(*self.emptied(*self.names[n - len(self.banks)]))
        return self.bank(*name)


def build(nc, a):
    ctx = ExitStack()
    sems = {}

    def sem(name):
        if name not in sems:
            sems[name] = ctx.enter_context(nc.semaphore(name))
        return sems[name]

    free = [0]

    def sb(name, shape, dt, at=None):
        size = 4 if dt in (F32, F32R) else 2
        for s in shape[1:]:
            size *= s
        size = (size + 31) // 32 * 32
        if at is None:
            at = free[0]
            free[0] += size
        t = nc.alloc_sbuf_tensor_at(name, shape, dt, offset=at + BASE)
        t_end[name] = at + size
        return t

    t_end = {}
    BASE = (nc.sbuf_base + 31) // 32 * 32
    with ctx:
        x_tok = sb("x_tok", [P, NT, D], F32)
        cols = sb("cols", [P, NCOL], F32)
        ident = sb("ident", [P, P], F32)
        identb = sb("identb", [P, P], BF16)
        tri = sb("tri", [P, P], F32)
        tri_r = sb("tri_r", [P, P], F32R)
        negtri_r = sb("negtri_r", [P, P], F32R)
        maskneg = sb("maskneg", [P, P], BF16)
        headmask = sb("headmask", [P, H0, HD0], F32)
        mhalf = sb("mhalf", [P, 8], F32)
        one = sb("one", [P, 1], F32)
        a_neg = sb("a_neg", [P, 1], F32)
        ln_st = sb("ln_st", [P, TPB, 6], F32)
        ln_mv = sb("ln_mv", [P, TPB, 2], F32)
        ln_ve = sb("ln_ve", [P, 2, TPB], F32)
        ln_rs = sb("ln_rs", [P, 2, TPB], F32)
        xn = sb("xn", [P, TPB, D], F32)
        xT = [sb("xT_hi", [D, BLK], F32R), sb("xT_lo", [D, BLK], F32R)]
        SHARED = free[0]

        w_raw = sb("w_raw", [P, 9 * P], F32)
        win = [sb("win_hi", [P, 9, P], F32R), sb("win_lo", [P, 9, P], F32R)]
        wg_raw = sb("wg_raw", [P, 8, P], F32)
        wgo = [sb("wgo_hi", [P, 8, P], F32R), sb("wgo_lo", [P, 8, P], F32R)]
        convin = sb("convin", [P, 4, CONV - 1 + BLK], F32)
        cacc = sb("cacc", [P, 4, BLK], F32)
        xs = sb("xs", [P, 4, BLK], F32)
        dtv = sb("dtv", [P, BLK], F32)
        dta = sb("dta", [P, BLK], F32)
        dte = sb("dte", [P, BLK], F32)
        dt = sb("dt", [P, BLK], F32)
        dtA = sb("dtA", [P, BLK], F32)
        cs = sb("cs", [P, BLK], F32)
        ecs = sb("ecs", [P, BLK], F32)
        eb = sb("eb", [P, BLK], F32)
        cdec = sb("cdec", [P, BLK], F32)
        bdec = sb("bdec", [P, BLK], F32)
        sz = sb("sz", [P, 2, BLK], F32)
        skip = sb("skip", [P, 2, BLK], F32)
        cat = [sb("cat_hi", [P, 2, 2, BLK], F32R), sb("cat_lo", [P, 2, 2, BLK], F32R)]
        gy = [sb("gy_hi", [P, 2, BLK], F32R), sb("gy_lo", [P, 2, BLK], F32R)]
        dt_tok = sb("dt_tok", [P, 2, H0], F32)
        dA_tok = [sb("dA_hi", [P, 2, H0], F32R), sb("dA_lo", [P, 2, H0], F32R)]
        bd_tok = sb("bd_tok", [P, 2, P], F32)
        xdt = sb("xdt", [P, 2, H0, HD0], F32)
        edec = sb("edec", [P, 2, H0, P], F32)
        mdec = sb("mdec", [P, 2, H0, P], F32)
        state = sb("state", [P, 2, DI], F32)
        stmp = sb("stmp", [P, DI], F32)
        y_fm = sb("y_fm", [P, 2, BLK], F32)
        yn = sb("yn", [P, TPB, DI], F32)
        yst = sb("yst", [P, TPB, 6], F32)
        ymv = sb("ymv", [P, TPB, 2], F32)
        yg = sb("yg", [P, 2, BLK], F32)
        ygs = [sb("yg_hi", [P, 2, BLK], F32R), sb("yg_lo", [P, 2, BLK], F32R)]
        sg = sb("sg", [P, 2, BLK], F32)
        y2 = sb("y2", [P, 2, BLK], F32)

        A_END = free[0]

        wqkv_raw = sb("wqkv_raw", [P, 3, P], F32)
        wqkv = [sb("wqkv_hi", [P, 3, P], F32R), sb("wqkv_lo", [P, 3, P], F32R)]
        wo = sb("wo", [P, 4, D], F32)
        bv = sb("bv", [P, D], F32)
        bo = sb("bo", [P, D], F32)
        den_sel = sb("den_sel", [P, P], F32)
        W_END = free[0]

        free[0] = SHARED
        inner = sb("inner", [P, NT, D], F32)
        I_END = free[0]
        kz = sb("kz", [P, HA, T], BF16)
        qa = sb("qa", [P, HA // 2, T], BF16)
        VW = HA * (HDA + 1)
        v9 = sb("v9", [P, NT * VW + 32], F32)
        probs = sb("probs", [P, 2, 4, 2, BLK], F32)
        assert free[0] <= A_END, (free[0], A_END)
        free[0] = W_END
        nx = sb("nx", [P, BLK], F32)
        nxs = [sb("nx_hi", [P, BLK], F32R), sb("nx_lo", [P, BLK], F32R)]
        QK_AT = free[0]
        qk_f = sb("qk_f", [P, 2, BLK], F32)
        qk_r = sb("qk_r", [P, 2, BLK], F32)
        o_n = sb("o_n", [P, 4, BLK], F32, at=QK_AT)
        qk_parts = sb("qk_parts", [P, 2, 3, BLK], BF16)
        mx = sb("mx", [P, 16, 4], F32)
        mneg = sb("mneg", [P, 2, 16], F32)
        mrow = sb("mrow", [4, 2, 2, BLK], BF16)
        o_sb = sb("o_sb", [P, BLK], F32)
        rden = sb("rden", [P, BLK], F32)
        END = free[0]
        assert BASE + END <= nc.sbuf_usable_end, (END, nc.sbuf_usable_end)

        free[0] = I_END
        nx2 = [sb("nx2_hi", [P, T], F32R), sb("nx2_lo", [P, T], F32R)]
        gT = [sb("gT_hi", [P, T], F32R), sb("gT_lo", [P, T], F32R)]
        nx2f = sb("nx2f", [P, BLK], F32)
        ew_raw = sb("ew_raw", [P, 2, 8, P], F32)
        ew = [sb("ew_hi", [P, 2, 8, P], F32R), sb("ew_lo", [P, 2, 8, P], F32R)]
        hid = sb("hid", [P, 2, FC, BLK], F32)
        hids = [sb("hid_hi", [P, 2, FC, BLK], F32R), sb("hid_lo", [P, 2, FC, BLK], F32R)]
        gate_bc = sb("gate_bc", [P, 2, BLK], F32)
        moe_sb = sb("moe_sb", [P, 2, BLK], F32)
        sel8 = sb("sel8", [P, NE, P], F32R)
        b2_raw = sb("b2_raw", [P, D], F32)
        b2 = [sb("b2_hi", [P, D], F32R), sb("b2_lo", [P, D], F32R)]
        gw = sb("gw", [P, NE], F32)
        lower8 = sb("lower8", [P, NE, NE], F32)
        lg = sb("lg", [P, TPB, NE], F32)
        above = sb("above", [P, TPB, NE, NE], F32)
        equal = sb("equal", [P, TPB, NE, NE], F32)
        rank = sb("rank", [P, TPB, NE], F32)
        lgm = sb("lgm", [P, TPB, 1], F32)
        ex8 = sb("ex8", [P, TPB, NE], F32)
        gates = sb("gates", [P, TPB, P], F32)
        assert free[0] <= A_END, (free[0], A_END)

        free[0] = W_END
        sw_raw = sb("sw_raw", [P, 16, P], F32)
        sw = [sb("sw_hi", [P, 16, P], F32R), sb("sw_lo", [P, 16, P], F32R)]
        out1_b = sb("out1_b", [P, D], F32)
        assert BASE + free[0] <= nc.sbuf_usable_end

        free[0] = SHARED
        N_FFN = 2 * HC + 2 * HC * HC + HC
        fw_raw = sb("fw_raw", [P, 2, 4, P], F32)
        fw = [sb("fw_hi", [P, N_FFN, P], F32R), sb("fw_lo", [P, N_FFN, P], F32R)]
        SCAN_AT = free[0]
        cin1 = sb("cin1", [P, 2, CONV - 1 + BLK], F32)
        cacc1 = sb("cacc1", [P, 2, BLK], F32)
        xc = sb("xc", [P, 2, BLK], F32)
        xcs = [sb("xc_hi", [P, 2, BLK], F32R), sb("xc_lo", [P, 2, BLK], F32R)]
        sz1 = sb("sz1", [P, 2, BLK], F32)
        u1 = sb("u1", [P, 2, BLK], F32)
        dB = sb("dB", [P, 2, BLK], F32)
        dBs = [sb("dB_hi", [P, 2, BLK], F32R), sb("dB_lo", [P, 2, BLK], F32R)]
        dv1 = sb("dv1", [P, 2, BLK], F32)
        da1 = sb("da1", [P, 2, BLK], F32)
        delta = sb("delta", [P, 2, BLK], F32)
        du = sb("du", [P, 2, BLK], F32)
        b_bc = sb("b_bc", [P, 2, BLK], F32)
        decay = sb("decay", [P, 2, 2, BLK], F32)
        drive = sb("drive", [P, 2, 2, BLK], F32)
        hst = sb("hst", [P, 2, 2, BLK], F32)
        hlast = sb("hlast", [P, NS1, 2], F32)
        sel16 = sb("sel16", [P, NS1, P], F32R)
        y1s = [sb("y1_hi", [P, 2, BLK], F32R), sb("y1_lo", [P, 2, BLK], F32R)]
        assert free[0] <= W_END, (free[0], W_END)
        free[0] = SCAN_AT
        fa = sb("fa", [P, 2, BLK], F32)
        fh = sb("fh", [P, HC, BLK], F32)
        fhs = [sb("fh_hi", [P, 3, HC, BLK], F32R), sb("fh_lo", [P, 3, HC, BLK], F32R)]
        fo = sb("fo", [P, 2, BLK], F32)
        assert free[0] <= W_END, (free[0], W_END)
        psum = ctx.enter_context(nc.psum_tensor("psum", [P, 8, BLK], F32))
        bank = [psum[:, i, :] for i in range(8)]
        s_pair = [psum[:, 0:2, :], psum[:, 2:4, :]]

        S = {n: sem(n) for n in """
            ln_var ln_rstd ln_turned ln_xn xT_hi xT_lo w_split pj_act pj_dve pj_filled dec_done tok_dve turned
            m_done e_done arg_filled y_done state_done s_filled yn_done yt_filled yg_done yb_filled yg_split
            sg_done gate_filled skip_split gy_split x_mixed out_filled conv_hist dt_done skip_done conv_done
            xs_ready dt_lnd cs_done ecs_done eb_done dA_hi y_var y_rstd nx_ready nx_split qkv_split qk_evac
            qk_filled v_done v_filled parts_done inner_ready parts_saved qk_zero kz_ready parts_loaded mx_read
            mrow_done rden_done att_done mx_filled mneg_done mrow_filled p_done s_scores pv_done o_copied
            den_filled on_done att_filled gbc_done gelu_done moe_added nx2_ready lg_done lg_filled gates_done
            gT_done gT_filled nx2_split lgm_done ex8_done ew_split gbc_filled hid_filled hid_split down_done
            hid_gated hid_hi ew_split_hi moe_consts moe_copied moe_turned moe_pool_consts in_moe sw_split
            c_in_read c_u_read c_db_read c_dt_read bbc_done c_mixed c_in_filled xc_split c_u_filled c_db_filled
            dB_split c_dt_filled y1_split xc_ready bbc_filled drive_done delta_ready scanned y1_read summed
            decay_done hlast_done c_out_filled sel16_done in_out1_b x1_done f_a_done f_prod f_g_hi f_o_done
            f_added fw_split f_filled f_split f_turned f_hi fw_hi in_x in_cols in_win in_wg in_qkv in_wo in_sw
            stored pool_order consts bo_added act_order a_ready dve_order consts_r
            """.split()}

        def C(name, j=0, w=1):
            return cols[:, COL[name] + j:COL[name] + j + w]

        def ln_stats_dve(o, dve, u, src, double=False):
            for i in range(TPB):
                o.did(dve.bn_stats(ln_st[:, i, :], src[:, i, :]))
            o.wait()
            for i in range(TPB):
                o.did(dve.bn_aggr(ln_mv[:, i, :], ln_st[:, i, :]))
            o.wait()
            if double:
                o.did(dve.tensor_scalar(ln_ve[:, 1, :], ln_mv[:, :, 1], 1.0 + EPS, EPS * EPS, ALU.mult, ALU.add))
            dve.tensor_scalar(ln_ve[:, 0, :], ln_mv[:, :, 1], EPS, None, ALU.add).then_inc(S["ln_var"], 1)
            dve.wait_ge(S["ln_rstd"], u + 1)

        def ln_apply_dve(dve, u, src, dst, which):
            if u >= 1:
                dve.wait_ge(S["ln_turned"], u)
            for i in range(TPB):
                ins = dve.tensor_scalar(dst[:, i, :], src[:, i, :], ln_mv[:, i, 0:1], ln_rs[:, which, i:i + 1],
                                        ALU.subtract, ALU.mult)
            ins.then_inc(S["ln_xn"], 1)

        def ln_pool(pool, u, double=False):
            pool.wait_ge(S["ln_var"], u + 1)
            w = 2 if double else 1
            pool.tensor_tensor(ln_rs[:, 0:w, :], ln_ve[:, 0:w, :], mhalf[:, 0:TPB * w].rearrange("p (w i) -> p w i", w=w),
                               ALU.pow).then_inc(S["ln_rstd"], 1)

        def ln_pe(pe, u, out):
            pe.wait_ge(S["ln_xn"], u + 1)
            for i in range(TPB):
                ins = pe.transpose(out[:, i * P:(i + 1) * P], xn[:, i, :], ident[:, :])
            ins.then_inc(S["ln_turned"], 1)

        def mm3(pe, out, w, x, start=True, stop=True):
            pe.matmul(out, w[1], x[0], start=start, stop=False, skip_group_check=True)
            pe.matmul(out, w[0], x[1], start=False, stop=False, skip_group_check=True)
            return pe.matmul(out, w[0], x[0], start=False, stop=stop, skip_group_check=True)

        def front_pe(pe, ring, b):
            xb = ring.take((S["xT_hi"], b + 1), (S["xT_lo"], b + 1))
            ln_pe(pe, b, xb)
            pe.wait_ge(S["xT_hi"], b + 1)
            pe.wait_ge(S["xT_lo"], b + 1)
            if b == 0:
                pe.wait_ge(S["w_split"], 2)
            for j in range(9):
                when = (S["pj_act"], 7 * b + j + 1) if j < 7 else (S["pj_dve"], 2 * b + j - 6)
                out = ring.take(when)
                mm3(pe, out[:, :], [w[:, j, :] for w in win], [x[:, :] for x in xT]).then_inc(S["pj_filled"], 1)

        ring_start, n_fill = {}, 0
        for b in range(NB + 1):
            for stage, n in (("front", 10), ("post", 7)):
                at = (stage, b if stage == "front" else b - 1)
                if 0 <= at[1] < NB:
                    ring_start[at] = n_fill
                    n_fill += n

        def ring_bank(stage, b, n):
            return bank[(ring_start[stage, b] + n) % 3]

        turn_a, turn_b = bank[3], bank[4]
        arg = [bank[5], bank[6]]
        ys_bank = bank[7]

        def chunk_front_pe(pe, g):
            b, c = divmod(g, TPB)
            cc = slice(c * P, (c + 1) * P)
            pe.wait_ge(S["dec_done"], b + 1)
            if g >= 1:
                pe.wait_ge(S["tok_dve"], 4 * g - 1)
            pe.transpose(turn_a[:, 0:P], dt[:, cc], ident[:, :])
            pe.transpose(turn_a[:, P:2 * P], dtA[:, cc], ident[:, :])
            pe.transpose(turn_a[:, 2 * P:3 * P], bdec[:, cc], ident[:, :]).then_inc(S["turned"], 1)
            if g >= 1:
                pe.wait_ge(S["m_done"], g)
            pe.transpose(turn_b[:, 0:P], xs[:, 0, cc], ident[:, :])
            pe.transpose(turn_b[:, P:2 * P], xs[:, 1, cc], ident[:, :])
            pe.matmul(turn_b[:, 2 * P:3 * P], xs[0:NS0, 2, cc], xs[0:NS0, 3, cc], start=True, stop=True).then_inc(S["turned"], 1)
            if g >= 1:
                pe.wait_ge(S["e_done"], g)
            pe.wait_ge(S["tok_dve"], 4 * g + 2)
            for half in range(2):
                hs = range(4 * half, 4 * half + 4)
                out = arg[half][:, :]
                for n, part in enumerate(dA_tok):
                    pe.matmul(out.rearrange("p (h t) -> p h t", h=4), negtri_r[:, :],
                              part[:, g % 2, 4 * half:4 * half + 4].unsqueeze(2).broadcast_to([P, 4, P]),
                              start=(n == 0), stop=False, skip_group_check=True)
                pe.matmul(out.rearrange("p (h t) -> p h t", h=4), identb[:, :],
                          maskneg[:, :].unsqueeze(1).broadcast_to([P, 4, P]), start=False, stop=False, skip_group_check=True)
                for h in hs:
                    for n, part in enumerate(dA_tok):
                        ins = pe.matmul(out[:, (h % 4) * P:(h % 4 + 1) * P], part[:, g % 2, h:h + 1].broadcast_to([P, P]),
                                        tri_r[:, :], start=False, stop=(n == 1), skip_group_check=True)
            ins.then_inc(S["arg_filled"], 1)

        def chunk_back_pe(pe, g):
            b, c = divmod(g, TPB)
            cc = slice(c * P, (c + 1) * P)
            pe.wait_ge(S["m_done"], g + 1)
            if g >= 1:
                pe.wait_ge(S["y_done"], g)
            for half in range(2):
                for q in range(4):
                    h = 4 * half + q
                    pe.matmul(ys_bank[q * HD0:(q + 1) * HD0, half * P:(half + 1) * P], xdt[:, g % 2, h, :],
                              mdec[:, g % 2, h, :], start=(half == 0), stop=False, skip_group_check=True)
            pe.wait_ge(S["state_done"], g + 1)
            for half in range(2):
                ins = pe.matmul(ys_bank[:, half * P:(half + 1) * P], state[:, g % 2, half * P:(half + 1) * P],
                                cdec[:, cc], start=False, stop=True, skip_group_check=True)
            pe.matmul(ys_bank[:, 2 * P:4 * P], bd_tok[:, g % 2, :], xdt[:, g % 2, :, :].rearrange("p h d -> p (h d)"),
                      start=True, stop=True).then_inc(S["s_filled"], 1)

        def post_pe(pe, ring, b):
            pe.wait_ge(S["y_done"], TPB * (b + 1))
            for pair in range(2):
                out = ring.take((S["yn_done"], 2 * b + pair + 1))
                for i in range(2):
                    for half in range(2):
                        ins = pe.transpose(out[:, (2 * i + half) * P:(2 * i + half + 1) * P],
                                           y_fm[:, half, (2 * pair + i) * P:(2 * pair + i + 1) * P], ident[:, :])
                ins.then_inc(S["yt_filled"], 1)
            pe.wait_ge(S["yn_done"], 2 * b + 2)
            for half in range(2):
                out = ring.take((S["yg_done"], 2 * b + half + 1))
                for i in range(TPB):
                    ins = pe.transpose(out[:, i * P:(i + 1) * P], yn[:, i, half * P:(half + 1) * P], ident[:, :])
                ins.then_inc(S["yb_filled"], 1)
            pe.wait_ge(S["yg_split"], b + 1)
            if b == 0:
                pe.wait_ge(S["w_split"], 4)
            for m in range(2):
                out = ring.take((S["sg_done"], 2 * b + m + 1))
                for k in range(2):
                    ins = mm3(pe, out[:, :], [w[:, 2 * k + m, :] for w in wgo], [y[:, k, :] for y in ygs],
                              start=(k == 0), stop=(k == 1))
                ins.then_inc(S["gate_filled"], 1)
            pe.wait_ge(S["skip_split"], b + 1)
            pe.wait_ge(S["gy_split"], b + 1)
            out = ring.take((S["x_mixed"], b + 1))
            for i in range(TPB):
                tt = slice(i * P, (i + 1) * P)
                for k in range(4):
                    act = [x[:, b % 2, k, tt] for x in cat] if k < 2 else [x[:, k - 2, tt] for x in gy]
                    ins = mm3(pe, out[:, tt], act, [w[:, 4 + k, :] for w in wgo], start=(i == 0 and k == 0), stop=(k == 3))
            ins.then_inc(S["out_filled"], 1)

        def front_act(o, act, b):
            act.wait_ge(S["ln_turned"], b + 1)
            if b >= 1:
                act.wait_ge(S["pj_filled"], 9 * b)
            act.activation(xT[0][:, :], ring_bank("front", b, 0)[:, :], ACT.Copy).then_inc(S["xT_hi"], 1)

            def pj(j):
                act.wait_ge(S["pj_filled"], 9 * b + j + 1)
                return ring_bank("front", b, 1 + j)[:, :]

            act.wait_ge(S["conv_hist"], b + 1)
            for j in (XA, XB, BREP, CREP):
                act.activation(convin[:, j, CONV - 1:], pj(j), ACT.Copy).then_inc(S["pj_act"], 1)
            if b >= 1:
                act.wait_ge(S["dt_done"], b)
            act.activation(dtv[:, :], pj(DTREP), ACT.Identity, bias=C("dt_bias")).then_inc(S["pj_act"], 1)
            if b >= 1:
                act.wait_ge(S["skip_done"], 2 * b)
            for n, j in enumerate((Z0A, Z0B)):
                act.activation(sz[:, n, :], pj(j), ACT.Silu).then_inc(S["pj_act"], 1)
            if b >= 1:
                act.wait_ge(S["y_done"], TPB * b)
            for j in range(4):
                act.wait_ge(S["conv_done"], 4 * b + j + 1)
                act.activation(xs[:, j, :], cacc[:, j, :], ACT.Silu, bias=C("conv0_b", j)).then_inc(S["xs_ready"], 1)
            act.wait_ge(S["pj_act"], 7 * b + 5)
            o.did(act.activation(dta[:, :], dtv[:, :], ACT.Abs))
            o.wait()
            o.did(act.activation(dte[:, :], dta[:, :], ACT.Exp, scale=-1.0))
            o.wait()
            act.activation(dta[:, :], dte[:, :], ACT.Ln, bias=one[:, 0:1]).then_inc(S["dt_lnd"], 1)
            act.wait_ge(S["cs_done"], b + 1)
            act.activation(ecs[:, :], cs[:, :], ACT.Exp).then_inc(S["ecs_done"], 1)
            for c in range(TPB):
                cc = slice(c * P, (c + 1) * P)
                ins = act.activation(eb[:, cc], cs[:, cc], ACT.Exp, scale=-1.0, bias=cs[:, (c + 1) * P - 1:(c + 1) * P])
            ins.then_inc(S["eb_done"], 1)

        def chunk_act(act, g):
            act.wait_ge(S["arg_filled"], g + 1)
            if g >= 2:
                act.wait_ge(S["m_done"], g - 1)
            act.activation(edec[:, g % 2, 0:4, :], arg[0][:, :].rearrange("p (h t) -> p h t", h=4), ACT.Exp)
            act.activation(edec[:, g % 2, 4:8, :], arg[1][:, :].rearrange("p (h t) -> p h t", h=4), ACT.Exp).then_inc(S["e_done"], 1)

        def post_act(act, b):
            if b >= 1:
                act.wait_ge(S["gy_split"], b)
            for half in range(2):
                act.wait_ge(S["yb_filled"], 2 * b + half + 1)
                act.activation(yg[:, half, :], ring_bank("post", b, 2 + half)[:, :], ACT.Identity,
                               scale=C("gamma", half), bias=C("beta", half)).then_inc(S["yg_done"], 1)
            for m in range(2):
                act.wait_ge(S["gate_filled"], 2 * b + m + 1)
                act.activation(sg[:, m, :], ring_bank("post", b, 4 + m)[:, :], ACT.Sigmoid,
                               bias=C("b_gate", m)).then_inc(S["sg_done"], 1)

        def lo_part(dve, out, value, hi):
            return dve.tensor_tensor(out, value, hi.bitcast(F32), ALU.subtract)

        def front_dve(o, dve, b):
            src = x_tok[:, b * TPB:(b + 1) * TPB, :]
            ln_stats_dve(o, dve, b, src)
            ln_apply_dve(dve, b, src, xn, 0)
            dve.wait_ge(S["xT_hi"], b + 1)
            lo_part(dve, xT[1][:, :], ring_bank("front", b, 0)[:, :], xT[0][:, :]).then_inc(S["xT_lo"], 1)
            if b == 0:
                dve.memset(convin[:, :, 0:CONV - 1], 0.0).then_inc(S["conv_hist"], 1)
            else:
                dve.tensor_copy(convin[:, :, 0:CONV - 1], convin[:, :, BLK:BLK + CONV - 1]).then_inc(S["conv_hist"], 1)
                dve.wait_ge(S["xs_ready"], 4 * b)
            dve.wait_ge(S["conv_hist"], b + 1)
            last = {}
            for j in range(4):
                dve.wait_ge(S["pj_act"], 7 * b + j + 1)
                last[j] = o.did(dve.tensor_scalar(cacc[:, j, :], convin[:, j, 0:BLK], C("conv0_w", CONV * j), None, ALU.mult))
            for k in range(1, CONV):
                for j in range(4):
                    o.wait(last[j])
                    ins = dve.scalar_tensor_tensor(cacc[:, j, :], convin[:, j, k:k + BLK], C("conv0_w", CONV * j + k),
                                                   cacc[:, j, :], ALU.mult, ALU.add)
                    if k < CONV - 1:
                        last[j] = o.did(ins)
                    else:
                        ins.then_inc(S["conv_done"], 1)
            if b >= 2:
                dve.wait_ge(S["out_filled"], b - 1)
            for n in range(2):
                dve.wait_ge(S["pj_filled"], 9 * b + X0A + n + 1)
                dve.wait_ge(S["pj_act"], 7 * b + 6 + n)
                dve.tensor_tensor(skip[:, n, :], ring_bank("front", b, 1 + X0A + n)[:, :], sz[:, n, :], ALU.mult).then_inc(S["pj_dve"], 1)
            for n in range(2):
                dve.wait_ge(S["pj_dve"], 2 * b + n + 1)
                dve.tensor_copy(cat[0][:, b % 2, n, :], skip[:, n, :]).then_inc(S["skip_done"], 1)
            dve.wait_ge(S["skip_done"], 2 * b + 2)
            lo_part(dve, cat[1][:, b % 2, :, :], skip[:, :, :], cat[0][:, b % 2, :, :]).then_inc(S["skip_split"], 1)
            dve.wait_ge(S["dt_lnd"], b + 1)
            o.did(dve.scalar_tensor_tensor(dt[:, :], dtv[:, :], 0.0, dta[:, :], ALU.max, ALU.add))
            o.wait()
            dve.tensor_scalar(dtA[:, :], dt[:, :], a_neg[:, 0:1], None, ALU.mult).then_inc(S["dt_done"], 1)
            dve.wait_ge(S["dt_done"], b + 1)
            for c in range(TPB):
                cc = slice(c * P, (c + 1) * P)
                ins = dve.tensor_tensor_scan(cs[:, cc], one[:, 0:1].broadcast_to([P, P]), dtA[:, cc], 0.0, ALU.mult, ALU.add)
            ins.then_inc(S["cs_done"], 1)
            dve.wait_ge(S["xs_ready"], 4 * b + 4)
            dve.wait_ge(S["ecs_done"], b + 1)
            o.did(dve.tensor_tensor(cdec[:, :], xs[:, 3, :], ecs[:, :], ALU.mult))
            dve.wait_ge(S["eb_done"], b + 1)
            dve.tensor_tensor(bdec[:, :], xs[:, 2, :], eb[:, :], ALU.mult).then_inc(S["dec_done"], 1)

        def chunk_front_dve(dve, g):
            s = g % 2
            dve.wait_ge(S["turned"], 2 * g + 1)
            if g >= 2:
                dve.wait_ge(S["s_filled"], g - 1)
            dve.tensor_copy(dt_tok[:, s, :], turn_a[:, 0:P:NS0]).then_inc(S["tok_dve"], 1)
            dve.tensor_copy(dA_tok[0][:, s, :], turn_a[:, P:2 * P:NS0]).then_inc(S["dA_hi"], 1)
            dve.wait_ge(S["dA_hi"], g + 1)
            lo_part(dve, dA_tok[1][:, s, :], turn_a[:, P:2 * P:NS0], dA_tok[0][:, s, :]).then_inc(S["tok_dve"], 1)
            dve.tensor_copy(bd_tok[:, s, :], turn_a[:, 2 * P:3 * P]).then_inc(S["tok_dve"], 1)
            dve.wait_ge(S["turned"], 2 * g + 2)
            dve.tensor_tensor(xdt[:, s, :, :], turn_b[:, 0:2 * P].rearrange("p (h d) -> p h d", h=H0),
                              dt_tok[:, s, :].unsqueeze(2).broadcast_to([P, H0, HD0]), ALU.mult).then_inc(S["tok_dve"], 1)

        def chunk_mid_dve(dve, g):
            s = g % 2
            dve.wait_ge(S["e_done"], g + 1)
            dve.tensor_tensor(mdec[:, s, :, :], edec[:, s, :, :], turn_b[:, 2 * P:3 * P].unsqueeze(1).broadcast_to([P, H0, P]),
                              ALU.mult).then_inc(S["m_done"], 1)

        def chunk_back_dve(o, dve, g):
            b, c = divmod(g, TPB)
            cc = slice(c * P, (c + 1) * P)
            if b >= 1 and c == 0:
                dve.wait_ge(S["yt_filled"], 2 * b)
            dve.wait_ge(S["s_filled"], g + 1)
            for half in range(2):
                ins = dve.scalar_tensor_tensor(y_fm[:, half, cc], xs[:, half, cc], C("d0", half),
                                               ys_bank[:, half * P:(half + 1) * P], ALU.mult, ALU.add)
            dve.tensor_tensor(stmp[:, :], ys_bank[:, 2 * P:4 * P], headmask[:, :, :].rearrange("p h d -> p (h d)"),
                              ALU.mult).then_inc(S["y_done"], 1)
            dve.wait_ge(S["y_done"], g + 1)
            dve.scalar_tensor_tensor(state[:, (g + 1) % 2, :], state[:, g % 2, :], ecs[:, (c + 1) * P - 1:(c + 1) * P],
                                     stmp[:, :], ALU.mult, ALU.add).then_inc(S["state_done"], 1)

        def post_dve(o, dve, b):
            for i in range(TPB):
                dve.wait_ge(S["yt_filled"], 2 * b + i // 2 + 1)
                src = ring_bank("post", b, i // 2)[:, (i % 2) * DI:(i % 2 + 1) * DI]
                o.did(dve.bn_stats(yst[:, i, :], src))
            o.wait()
            for i in range(TPB):
                o.did(dve.bn_aggr(ymv[:, i, :], yst[:, i, :]))
            o.wait()
            dve.tensor_scalar(ln_ve[:, 0, :], ymv[:, :, 1], EPS, None, ALU.add).then_inc(S["y_var"], 1)
            dve.wait_ge(S["y_rstd"], b + 1)
            if b >= 1:
                dve.wait_ge(S["yb_filled"], 2 * b)
            for i in range(TPB):
                src = ring_bank("post", b, i // 2)[:, (i % 2) * DI:(i % 2 + 1) * DI]
                ins = dve.tensor_scalar(yn[:, i, :], src, ymv[:, i, 0:1], ln_rs[:, 0, i:i + 1], ALU.subtract, ALU.mult)
                if i % 2:
                    ins.then_inc(S["yn_done"], 1)
            dve.wait_ge(S["yg_done"], 2 * b + 2)
            o.did(dve.tensor_copy(ygs[0][:, :, :], yg[:, :, :]))
            o.wait()
            lo_part(dve, ygs[1][:, :, :], yg[:, :, :], ygs[0][:, :, :]).then_inc(S["yg_split"], 1)
            dve.wait_ge(S["sg_done"], 2 * b + 2)
            o.did(dve.tensor_tensor(y2[:, :, :], sg[:, :, :], yg[:, :, :], ALU.mult))
            o.wait()
            if b >= 1:
                dve.wait_ge(S["out_filled"], b)
            o.did(dve.tensor_copy(gy[0][:, :, :], y2[:, :, :]))
            o.wait()
            lo_part(dve, gy[1][:, :, :], y2[:, :, :], gy[0][:, :, :]).then_inc(S["gy_split"], 1)
            dve.wait_ge(S["out_filled"], b + 1)
            xb = x_tok[:, b * TPB:(b + 1) * TPB, :]
            dve.tensor_tensor(xb, ring_bank("post", b, 6)[:, :].rearrange("p (i d) -> p i d", i=TPB), xb, ALU.add).then_inc(S["x_mixed"], 1)

        SCALE = HDA ** -0.5
        part_dram = nc.dram_tensor("qk_part_rows", (2, 3, P, T), BF16, kind="Internal").ap()
        Q_ROWS, K_ROWS = (0, 0, 1, 1, 0, 2), (0, 1, 0, 1, 2, 0)
        M_ROW = len(Q_ROWS) * HDA
        m_loaded = [sem(f"m_loaded{n}") for n in range(4)]
        ITEMS = [(b, grp) for b in range(NB) for grp in range(4)]

        def units(k):
            b, grp = ITEMS[k]
            return [(b, 4 * grp + hh, i, c) for hh in range(4) for i in range(TPB) for c in range(b + 1)]

        unit_base = [0]
        for k in range(16):
            unit_base.append(unit_base[-1] + len(units(k)))

        def unit_share(k, step):
            steps = 2 * (ITEMS[k][0] + 1)
            if k + 2 >= len(ITEMS):
                return []
            n = len(units(k + 2))
            return list(range(n * step // steps, n * (step + 1) // steps))

        def qkv_pe(pe, b):
            u = NB + b
            if b >= 1:
                pe.wait_ge(S["nx_ready"], b)
            ln_pe(pe, u, bank[0])
            pe.wait_ge(S["nx_split"], 2 * b + 2)
            if b == 0:
                pe.wait_ge(S["qkv_split"], 2)
            for j in range(2):
                if b >= 1:
                    pe.wait_ge(S["qk_evac"], 2 * b - 1 + j)
                mm3(pe, bank[1 + j][:, :], [w[:, j, :] for w in wqkv], [x[:, :] for x in nxs]).then_inc(S["qk_filled"], 1)
            if b >= 1:
                pe.wait_ge(S["v_done"], b)
            for i in range(TPB):
                tt = slice(i * P, (i + 1) * P)
                ins = mm3(pe, bank[3][:, tt], [x[:, tt] for x in nxs], [w[:, 2, :] for w in wqkv], start=(i == 0))
            ins.then_inc(S["v_filled"], 1)

        def qkv_act(act, b):
            act.wait_ge(S["ln_turned"], NB + b + 1)
            if b >= 1:
                act.wait_ge(S["nx_split"], 2 * b)
            act.activation(nx[:, :], bank[0][:, :], ACT.Identity, scale=C("ln1_w"), bias=C("ln1_b")).then_inc(S["nx_ready"], 1)
            for j, bias in enumerate(("bq", "bk")):
                act.wait_ge(S["qk_filled"], 2 * b + j + 1)
                if b >= 1:
                    act.wait_ge(S["parts_done"], 8 * b)
                act.activation(qk_f[:, j, :], bank[1 + j][:, :], ACT.Identity, bias=C(bias)).then_inc(S["qk_evac"], 1)

        def qkv_dve(o, dve, b):
            u = NB + b
            src = x_tok[:, b * TPB:(b + 1) * TPB, :]
            dst = inner[:, b * TPB:(b + 1) * TPB, :]
            ln_stats_dve(o, dve, u, src, double=True)
            for i in range(TPB):
                ins = dve.tensor_scalar(dst[:, i, :], src[:, i, :], ln_mv[:, i, 0:1], ln_rs[:, 0, i:i + 1],
                                        ALU.subtract, ALU.mult)
            ins.then_inc(S["inner_ready"], 1)
            ln_apply_dve(dve, u, src, xn, 1)
            dve.wait_ge(S["nx_ready"], b + 1)
            if b >= 1:
                dve.wait_ge(S["v_filled"], b)
            dve.tensor_copy(nxs[0][:, :], nx[:, :]).then_inc(S["nx_split"], 1)
            dve.wait_ge(S["nx_split"], 2 * b + 1)
            lo_part(dve, nxs[1][:, :], nx[:, :], nxs[0][:, :]).then_inc(S["nx_split"], 1)
            if b >= 1:
                dve.wait_ge(S["parts_saved"], 16 * 2 * b)
            for j in range(2):
                dve.wait_ge(S["qk_evac"], 2 * b + j + 1)
                dve.tensor_copy(qk_parts[:, j, 0, :], qk_f[:, j, :]).then_inc(S["parts_done"], 1)
            for j in range(2):
                dve.wait_ge(S["parts_done"], 8 * b + j + 1)
                dve.tensor_tensor(qk_r[:, j, :], qk_f[:, j, :], qk_parts[:, j, 0, :], ALU.subtract).then_inc(S["parts_done"], 1)
            for j in range(2):
                dve.wait_ge(S["parts_done"], 8 * b + j + 3)
                dve.tensor_copy(qk_parts[:, j, 1, :], qk_r[:, j, :]).then_inc(S["parts_done"], 1)
            for j in range(2):
                dve.wait_ge(S["parts_done"], 8 * b + j + 5)
                dve.tensor_tensor(qk_parts[:, j, 2, :], qk_r[:, j, :], qk_parts[:, j, 1, :], ALU.subtract).then_inc(S["parts_done"], 1)
            dve.wait_ge(S["v_filled"], b + 1)
            v_out = v9[:, b * TPB * VW:(b + 1) * TPB * VW].rearrange("p (i h e) -> p i h e", i=TPB, e=HDA + 1)[:, :, :, 0:HDA]
            dve.tensor_tensor(v_out, bank[3][:, :].rearrange("p (i h e) -> p i h e", i=TPB, e=HDA),
                              bv[:, :].rearrange("p (h e) -> p h e", e=HDA).unsqueeze(1).broadcast_to([P, TPB, HA, HDA]),
                              ALU.add).then_inc(S["v_done"], 1)

        def qkv_sp(sp, b):
            tt = slice(b * BLK, (b + 1) * BLK)
            for j in range(2):
                sp.wait_ge(S["parts_done"], 8 * b + j + 7)
                sp.dma_start(part_dram[j][:, :, tt].rearrange("n p t -> p n t"), qk_parts[:, j, :, :]).then_inc(S["parts_saved"], 16)
            sp.wait_ge(S["parts_saved"], 32 * (b + 1))
            if b == 0:
                sp.wait_ge(S["qk_zero"], 1)
                sp.wait_ge(S["kz_ready"], 1)
            for j, (rows, dst) in enumerate(((Q_ROWS, qa), (K_ROWS, kz))):
                for par in range(2):
                    for g, n in enumerate(rows):
                        r0 = 64 * par + g * HDA
                        out = dst[r0:r0 + HDA, :, tt] if j == 0 else dst[r0:r0 + HDA, par::2, tt]
                        src = part_dram[j, n].rearrange("(pair par e) t -> par e pair t", par=2, e=HDA)[par][:, :, tt]
                        sp.dma_start(out, src).then_inc(S["parts_loaded"], 16)

        ring_ab = [bank[4], bank[5]]
        fill_at, fills = {}, []

        def plan(name):
            fill_at[name] = len(fills)
            fills.append(name)

        def plan_item_maxima(k, lo, hi):
            for n in range(lo, hi):
                plan(("mx", k, n))

        for k in range(2):
            plan_item_maxima(k, 0, len(units(k)))
            plan(("mrow", k))
        for k in range(16):
            for step in range(2 * (ITEMS[k][0] + 1)):
                for n in unit_share(k, step):
                    plan(("mx", k + 2, n))
            if k + 2 < 16:
                plan(("mrow", k + 2))
            plan(("den", k))
            if k % 4 == 3:
                plan(("att", k // 4))

        def fill_bank(*name):
            return ring_ab[fill_at[name] % 2]

        def emptied(name):
            kind = name[0]
            if kind == "mx":
                return (S["mx_read"], unit_base[name[1]] + name[2] + 1)
            if kind == "mrow":
                return (S["mrow_done"], 2 * name[1] + 2)
            return (S["rden_done"], name[1] + 1) if kind == "den" else (S["att_done"], name[1] + 1)

        def take(pe, *name):
            n = fill_at[name]
            if n >= 2:
                pe.wait_ge(*emptied(fills[n - 2]))
            return ring_ab[n % 2]

        def mx_pe(pe, k, n):
            b, h, i, c = units(k)[n]
            out = take(pe, "mx", k, n)
            q0 = b * BLK + i * P
            w = BLK if c < b else (i + 1) * P
            last = c == b
            ins = pe.matmul(out[:, 0:w], qa[:, h // 2, q0:q0 + P], kz[:, h, c * BLK:c * BLK + w], start=True, stop=not last,
                            skip_group_check=True)
            if last:
                ins = pe.matmul(out[:, w - P:w], maskneg[:, :], identb[:, :], start=False, stop=True, skip_group_check=True)
            ins.then_inc(S["mx_filled"], 1)

        def mx_dve(dve, k, n):
            b, h, i, c = units(k)[n]
            w = BLK if c < b else (i + 1) * P
            dve.wait_ge(S["mx_filled"], unit_base[k] + n + 1)
            if n == 0 and k >= 1:
                dve.wait_ge(S["mneg_done"], 2 * k)
            dve.tensor_reduce(mx[:, 4 * i + h % 4, c:c + 1], fill_bank("mx", k, n)[:, 0:w], AX.X, ALU.max).then_inc(S["mx_read"], 1)

        def mneg_dve(o, dve, k):
            b = ITEMS[k][0]
            dve.wait_ge(S["mx_read"], unit_base[k + 1])
            if k >= 2:
                dve.wait_ge(S["mrow_filled"], k - 1)
            dve.tensor_reduce(mneg[:, k % 2, :], mx[:, :, 0:b + 1], AX.X, ALU.max).then_inc(S["mneg_done"], 1)
            dve.wait_ge(S["mneg_done"], 2 * k + 1)
            dve.tensor_scalar(mneg[:, k % 2, :], mneg[:, k % 2, :], -1.0, None, ALU.mult).then_inc(S["mneg_done"], 1)

        def mrow_pe(pe, k):
            out = take(pe, "mrow", k)
            pe.wait_ge(S["mneg_done"], 2 * k + 2)
            for i in range(TPB):
                ins = pe.transpose(out[0:4, i * P:(i + 1) * P], mneg[:, k % 2, 4 * i:4 * i + 4], ident[:, :])
            ins.then_inc(S["mrow_filled"], 1)

        def mrow_dve(dve, k):
            dve.wait_ge(S["mrow_filled"], k + 1)
            if k >= 2:
                dve.wait_ge(m_loaded[(k - 2) % 4], 8 * 16 * ((k - 2) // 4 + 1))
            src = fill_bank("mrow", k)[0:4, :]
            dve.tensor_copy(mrow[:, k % 2, 0, :], src).then_inc(S["mrow_done"], 1)
            dve.wait_ge(S["mrow_done"], 2 * k + 1)
            dve.tensor_tensor(mrow[:, k % 2, 1, :], src, mrow[:, k % 2, 0, :], ALU.subtract).then_inc(S["mrow_done"], 1)

        def mrow_sp(sp, k):
            b, grp = ITEMS[k]
            sp.wait_ge(S["mrow_done"], 2 * k + 2)
            for hh in range(4):
                h = 4 * grp + hh
                for n in range(2):
                    r = 64 * (h % 2) + M_ROW + n
                    sp.dma_start(qa[r:r + 1, h // 2, b * BLK:(b + 1) * BLK], mrow[hh:hh + 1, k % 2, n, :]).then_inc(m_loaded[k % 4], 16)

        step_base = [0]
        for b, _ in ITEMS:
            step_base.append(step_base[-1] + 2 * (b + 1))

        def q_lo(b, kt):
            r = max(0, kt - TPB * b)
            return r * P, r // 2 * 2 * P

        def scores_pe(pe, k, kp, hh):
            b, grp = ITEMS[k]
            h = 4 * grp + hh
            n = 4 * (step_base[k] + kp) + hh
            if n >= 2:
                pe.wait_ge(S["p_done"], n - 1)
            for j in range(2):
                kt = 2 * kp + j
                own, lo = q_lo(b, kt)
                out = bank[2 * (n % 2) + j]
                diag = kt >= TPB * b
                ins = pe.matmul(out[:, lo:], kz[:, h, kt * P:(kt + 1) * P], qa[:, h // 2, b * BLK + lo:(b + 1) * BLK],
                                start=True, stop=not diag, skip_group_check=True)
                if diag:
                    ins = pe.matmul(out[:, own:own + P], identb[:, :], maskneg[:, :], start=False, stop=True, skip_group_check=True)
            ins.then_inc(S["s_scores"], 1)

        def probs_act(act, k, kp, hh):
            b, grp = ITEMS[k]
            n = 4 * (step_base[k] + kp) + hh
            st = step_base[k] + kp
            act.wait_ge(S["s_scores"], n + 1)
            if st >= 2 and hh == 0:
                act.wait_ge(S["pv_done"], st - 1)
            _, lo = q_lo(b, 2 * kp)
            act.activation(probs[:, st % 2, hh, :, lo:], s_pair[n % 2][:, :, lo:], ACT.Exp, scale=SCALE).then_inc(S["p_done"], 1)

        def values_pe(pe, k, kp):
            b, grp = ITEMS[k]
            st = step_base[k] + kp
            pe.wait_ge(S["p_done"], 4 * st + 4)
            if kp == 0 and k >= 2:
                pe.wait_ge(S["o_copied"], k - 1)
            out = bank[6 + k % 2]
            for j in range(2):
                kt = 2 * kp + j
                own, _ = q_lo(b, kt)
                for hh in range(4):
                    at = kt * VW + (4 * grp + hh) * (HDA + 1)
                    ins = pe.matmul(out[32 * hh:32 * hh + 32, own:], v9[:, at:at + 32], probs[:, st % 2, hh, j, own:],
                                    start=(kt == 0), stop=(kt == TPB * (b + 1) - 1), skip_group_check=True)
            ins.then_inc(S["pv_done"], 1)

        def attention_pe(pe):
            for k in range(2):
                for n in range(len(units(k))):
                    mx_pe(pe, k, n)
                mrow_pe(pe, k)
            for k, (b, grp) in enumerate(ITEMS):
                steps = 2 * (b + 1)
                pe.wait_ge(m_loaded[k % 4], 8 * 16 * (k // 4 + 1))
                for step in range(steps):
                    for hh in range(4):
                        scores_pe(pe, k, step, hh)
                        share = unit_share(k, step)
                        for n in share[len(share) * hh // 4:len(share) * (hh + 1) // 4]:
                            mx_pe(pe, k + 2, n)
                    if step:
                        values_pe(pe, k, step - 1)
                values_pe(pe, k, steps - 1)
                if k + 2 < 16:
                    mrow_pe(pe, k + 2)
                out = take(pe, "den", k)
                pe.wait_ge(S["o_copied"], k + 1)
                pe.matmul(out[:, :], den_sel[:, :], o_sb[:, :], start=True, stop=True).then_inc(S["den_filled"], 1)
                if grp == 3:
                    out = take(pe, "att", b)
                    pe.wait_ge(S["on_done"], 4 * b + 4)
                    for i in range(TPB):
                        tt = slice(i * P, (i + 1) * P)
                        for g in range(4):
                            ins = pe.matmul(out[:, tt], o_n[:, g, tt], wo[:, g, :], start=(g == 0), stop=(g == 3))
                    ins.then_inc(S["att_filled"], 1)

        def attention_act(act):
            for k, (b, grp) in enumerate(ITEMS):
                for kp in range(2 * (b + 1)):
                    for hh in range(4):
                        probs_act(act, k, kp, hh)
                act.wait_ge(S["pv_done"], step_base[k + 1])
                if k >= 1:
                    act.wait_ge(S["on_done"], k)
                act.activation(o_sb[:, :], bank[6 + k % 2][:, :], ACT.Copy).then_inc(S["o_copied"], 1)

        def attention_dve(o, dve):
            for k in range(2):
                for n in range(len(units(k))):
                    mx_dve(dve, k, n)
                mneg_dve(o, dve, k)
                mrow_dve(dve, k)
            for k, (b, grp) in enumerate(ITEMS):
                if k + 2 < 16:
                    for n in range(len(units(k + 2))):
                        mx_dve(dve, k + 2, n)
                    mneg_dve(o, dve, k + 2)
                    mrow_dve(dve, k + 2)
                dve.wait_ge(S["den_filled"], k + 1)
                dve.reciprocal(rden[:, :], fill_bank("den", k)[:, :]).then_inc(S["rden_done"], 1)
                dve.wait_ge(S["rden_done"], k + 1)
                if grp == 0 and b >= 1:
                    dve.wait_ge(S["att_filled"], b)
                dve.tensor_tensor(o_n[:, grp, :], o_sb[:, :], rden[:, :], ALU.mult).then_inc(S["on_done"], 1)
                if grp == 3:
                    dve.wait_ge(S["att_filled"], b + 1)
                    ib = inner[:, b * TPB:(b + 1) * TPB, :]
                    dve.tensor_tensor(ib, fill_bank("att", b)[:, :].rearrange("p (i d) -> p i d", i=TPB), ib,
                                      ALU.add).then_inc(S["att_done"], 1)

        def attention_sp(sp):
            for k in range(16):
                mrow_sp(sp, k)

        UNITS = [(e, b) for e in range(NE) for b in range(NB)]

        def moe_emptied(kind, n, m):
            if kind == "gate":
                return S["gbc_done"], n + 1
            return (S["gelu_done"], FC * n + m + 1) if kind == "hid" else (S["moe_added"], n + 1)

        moe_fill = Fillings(bank[4:8], [(kind, n, m) for n in range(len(UNITS)) for kind, m in
                                        [("gate", 0)] + [("hid", m) for m in range(FC)]] + [("turn", b, 0) for b in range(NB)],
                            moe_emptied)

        def route_pe(pe, b):
            if b >= 1:
                pe.wait_ge(S["nx2_ready"], b)
            ln_pe(pe, 2 * NB + b, bank[4])
            pe.wait_ge(S["nx2_ready"], b + 1)
            if b >= 1:
                pe.wait_ge(S["lg_done"], b)
            for i in range(TPB):
                ins = pe.matmul(bank[5][:, i * NE:(i + 1) * NE], nx2f[:, i * P:(i + 1) * P], gw[:, :], start=True, stop=True)
            ins.then_inc(S["lg_filled"], 1)
            pe.wait_ge(S["gates_done"], b + 1)
            if b >= 1:
                pe.wait_ge(S["gT_done"], 2 * b)
            for i in range(TPB):
                ins = pe.transpose(bank[6][:, i * P:(i + 1) * P], gates[:, i, :], ident[:, :])
            ins.then_inc(S["gT_filled"], 1)

        def route_act(act, b):
            act.wait_ge(S["ln_turned"], 2 * NB + b + 1)
            if b >= 1:
                act.wait_ge(S["nx2_split"], 2 * b)
                act.wait_ge(S["lg_filled"], b)
            act.activation(nx2f[:, :], bank[4][:, :], ACT.Identity, scale=C("ln2_w"), bias=C("ln2_b")).then_inc(S["nx2_ready"], 1)
            act.wait_ge(S["lgm_done"], b + 1)
            act.activation(ex8[:, :, :], lg[:, :, :], ACT.Exp).then_inc(S["ex8_done"], 1)
            act.wait_ge(S["gT_filled"], b + 1)
            tt = slice(b * BLK, (b + 1) * BLK)
            act.activation(gT[0][:, tt], bank[6][:, :], ACT.Copy).then_inc(S["gT_done"], 1)

        def route_dve(o, dve, b):
            src = inner[:, b * TPB:(b + 1) * TPB, :]
            u = 2 * NB + b
            ln_stats_dve(o, dve, u, src)
            ln_apply_dve(dve, u, src, xn, 0)
            tt = slice(b * BLK, (b + 1) * BLK)
            dve.wait_ge(S["nx2_ready"], b + 1)
            dve.tensor_copy(nx2[0][:, tt], nx2f[:, :]).then_inc(S["nx2_split"], 1)
            dve.wait_ge(S["nx2_split"], 2 * b + 1)
            lo_part(dve, nx2[1][:, tt], nx2f[:, :], nx2[0][:, tt]).then_inc(S["nx2_split"], 1)
            dve.wait_ge(S["lg_filled"], b + 1)
            if b >= 1:
                dve.wait_ge(S["ex8_done"], b)
            dve.tensor_copy(lg[:, :, :], bank[5][:, 0:TPB * NE].rearrange("p (i e) -> p i e", i=TPB)).then_inc(S["lg_done"], 1)
            dve.wait_ge(S["lg_done"], b + 1)
            shape = [P, TPB, NE, NE]
            other, own = lg[:, :, :].unsqueeze(2).broadcast_to(shape), lg[:, :, :].unsqueeze(3).broadcast_to(shape)
            o.did(dve.tensor_tensor(above[:, :, :, :], other, own, ALU.is_gt))
            o.did(dve.tensor_tensor(equal[:, :, :, :], other, own, ALU.is_equal))
            n_max = o.did(dve.tensor_reduce(lgm[:, :, 0], lg[:, :, :], AX.X, ALU.max))
            o.wait(n_max - 1)
            o.did(dve.tensor_tensor(equal[:, :, :, :], equal[:, :, :, :], lower8[:, :, :].unsqueeze(1).broadcast_to(shape), ALU.mult))
            o.wait(n_max)
            dve.tensor_tensor(lg[:, :, :], lg[:, :, :], lgm[:, :, :].broadcast_to([P, TPB, NE]), ALU.subtract).then_inc(S["lgm_done"], 1)
            o.wait()
            o.did(dve.tensor_tensor(above[:, :, :, :], above[:, :, :, :], equal[:, :, :, :], ALU.add))
            o.wait()
            o.did(dve.tensor_reduce(rank[:, :, :], above[:, :, :, :], AX.X, ALU.add))
            o.wait()
            dve.wait_ge(S["ex8_done"], b + 1)
            o.did(dve.scalar_tensor_tensor(rank[:, :, :], rank[:, :, :], 1.5, ex8[:, :, :], ALU.is_lt, ALU.mult))
            o.wait()
            o.did(dve.tensor_reduce(lgm[:, :, 0], rank[:, :, :], AX.X, ALU.add))
            o.wait()
            o.did(dve.reciprocal(lgm[:, :, 0], lgm[:, :, 0]))
            o.wait()
            if b >= 1:
                dve.wait_ge(S["gT_filled"], b)
            dve.tensor_tensor(gates[:, :, 0:NE], rank[:, :, :], lgm[:, :, :].broadcast_to([P, TPB, NE]),
                              ALU.mult).then_inc(S["gates_done"], 1)
            dve.wait_ge(S["gT_done"], 2 * b + 1)
            lo_part(dve, gT[1][:, tt], bank[6][:, :], gT[0][:, tt]).then_inc(S["gT_done"], 1)

        def experts_up_pe(pe, n):
            e, b = UNITS[n]
            tt = slice(b * BLK, (b + 1) * BLK)
            if b == 0:
                pe.wait_ge(S["ew_split"], 2 * (e + 1))
            out = moe_fill.take(pe, "gate", n, 0)
            pe.matmul(out[:, :], sel8[:, e, :], gT[1][:, tt], start=True, stop=False)
            pe.matmul(out[:, :], sel8[:, e, :], gT[0][:, tt], start=False, stop=True).then_inc(S["gbc_filled"], 1)
            for m in range(FC):
                out = moe_fill.take(pe, "hid", n, m)
                mm3(pe, out[:, :], [w[:, e % 2, m, :] for w in ew], [x[:, tt] for x in nx2]).then_inc(S["hid_filled"], 1)

        def experts_down_pe(pe, n):
            e, b = UNITS[n]
            tt = slice(b * BLK, (b + 1) * BLK)
            if e == 0:
                mm3(pe, bank[b][:, :], [w[:, :] for w in b2], [x[:, tt] for x in gT], start=True, stop=False)
            pe.wait_ge(S["hid_split"], n + 1)
            for m in range(FC):
                ins = mm3(pe, bank[b][:, :], [w[:, e % 2, FC + m, :] for w in ew], [h[:, n % 2, m, :] for h in hids],
                          start=False, stop=(e == NE - 1 and m == FC - 1))
            ins.then_inc(S["down_done"], 1)

        def experts_act(act, n):
            e, b = UNITS[n]
            act.wait_ge(S["gbc_filled"], n + 1)
            if n >= 2:
                act.wait_ge(S["hid_split"], n - 1)
            act.activation(gate_bc[:, n % 2, :], moe_fill.bank("gate", n, 0)[:, :], ACT.Copy).then_inc(S["gbc_done"], 1)
            for m in range(FC):
                act.wait_ge(S["hid_filled"], FC * n + m + 1)
                act.activation(hid[:, n % 2, m, :], moe_fill.bank("hid", n, m)[:, :], ACT.Gelu,
                               bias=C("fc1_b", FC * e + m)).then_inc(S["gelu_done"], 1)

        def experts_hi_act(act, n):
            act.wait_ge(S["hid_gated"], n + 1)
            if n >= 2:
                act.wait_ge(S["down_done"], n - 1)
            act.activation(hids[0][:, n % 2, :, :], hid[:, n % 2, :, :], ACT.Copy).then_inc(S["hid_hi"], 1)

        def experts_dve(dve, n):
            dve.wait_ge(S["gbc_done"], n + 1)
            dve.wait_ge(S["gelu_done"], FC * n + FC)
            dve.tensor_tensor(hid[:, n % 2, :, :], hid[:, n % 2, :, :],
                              gate_bc[:, n % 2, :].unsqueeze(1).broadcast_to([P, FC, BLK]), ALU.mult).then_inc(S["hid_gated"], 1)

        def experts_lo_dve(dve, n):
            dve.wait_ge(S["hid_hi"], n + 1)
            if n >= 2:
                dve.wait_ge(S["down_done"], n - 1)
            lo_part(dve, hids[1][:, n % 2, :, :], hid[:, n % 2, :, :], hids[0][:, n % 2, :, :]).then_inc(S["hid_split"], 1)

        def split_weights_act(act, e):
            act.wait_ge(ew_in[e % 2], 16 * (e // 2 + 1))
            if e >= 2:
                act.wait_ge(S["down_done"], NB * (e - 1))
            act.activation(ew[0][:, e % 2, :, :], ew_raw[:, e % 2, :, :], ACT.Copy).then_inc(S["ew_split_hi"], 1)

        def split_weights_pool(pool, e):
            pool.wait_ge(S["ew_split_hi"], e + 1)
            lo_part(pool, ew[1][:, e % 2, :, :], ew_raw[:, e % 2, :, :], ew[0][:, e % 2, :, :]).then_inc(S["ew_split"], 2)

        ew_in = [sem("ew_in0"), sem("ew_in1")]

        def experts_sp(sp):
            for e in range(NE):
                if e >= 2:
                    sp.wait_ge(S["ew_split"], 2 * (e - 1))
                sp.dma_start(ew_raw[:, e % 2, :, :], a["experts"][e].rearrange("p (j m) -> p j m", m=P)).then_inc(ew_in[e % 2], 16)

        def moe_pe(pe):
            pe.wait_ge(S["att_done"], NB)
            pe.wait_ge(S["moe_consts"], 1)
            for b in range(NB):
                route_pe(pe, b)
            pe.wait_ge(S["nx2_split"], 2 * NB)
            pe.wait_ge(S["gT_done"], 2 * NB)
            n = len(UNITS)
            for k in range(n + 2):
                if k < n:
                    experts_up_pe(pe, k)
                if k >= 2:
                    experts_down_pe(pe, k - 2)
            for b in range(NB):
                out = moe_fill.take(pe, "turn", b, 0)
                pe.wait_ge(S["moe_copied"], b + 1)
                for i in range(TPB):
                    ins = pe.transpose(out[:, i * P:(i + 1) * P], moe_sb[:, b % 2, i * P:(i + 1) * P], ident[:, :])
                ins.then_inc(S["moe_turned"], 1)

        def moe_act(act):
            act.wait_ge(S["att_done"], NB)
            for b in range(NB):
                route_act(act, b)
            n = len(UNITS)
            for k in range(n + 1):
                if k < n:
                    if k % NB == 0:
                        if k == 0:
                            split_weights_act(act, 0)
                            split_weights_act(act, 1)
                    experts_act(act, k)
                if k >= 1:
                    experts_hi_act(act, k - 1)
                if k % NB == 3 and 2 <= k // NB + 1 < NE:
                    split_weights_act(act, k // NB + 1)
            for b in range(NB):
                act.wait_ge(S["down_done"], len(UNITS) - NB + b + 1)
                if b >= 2:
                    act.wait_ge(S["moe_turned"], b - 1)
                act.activation(moe_sb[:, b % 2, :], bank[b][:, :], ACT.Copy).then_inc(S["moe_copied"], 1)

        def moe_dve(o, dve):
            dve.wait_ge(S["moe_pool_consts"], 1)
            o.did(dve.memset(gates[:, :, :], 0.0))
            o.did(dve.tensor_copy(sel8[:, :, :], ident[:, 0:NE].unsqueeze(2).broadcast_to([P, NE, P])))
            dve.wait_ge(S["in_moe"], 32)
            o.did(dve.tensor_copy(b2[0][:, :], b2_raw[:, :]))
            o.wait()
            lo_part(dve, b2[1][:, :], b2_raw[:, :], b2[0][:, :]).then_inc(S["moe_consts"], 1)
            for b in range(NB):
                route_dve(o, dve, b)
            n = len(UNITS)
            for k in range(n + 1):
                if k < n:
                    experts_dve(dve, k)
                if k >= 1:
                    experts_lo_dve(dve, k - 1)
            for b in range(NB):
                dve.wait_ge(S["moe_turned"], b + 1)
                xb = x_tok[:, b * TPB:(b + 1) * TPB, :]
                dve.tensor_tensor(xb, moe_fill.bank("turn", b, 0)[:, :].rearrange("p (i d) -> p i d", i=TPB), xb,
                                  ALU.add).then_inc(S["moe_added"], 1)

        def moe_pool(o, pool):
            pool.wait_ge(S["att_done"], NB)
            o.did(pool.memset(lower8[:, :, :], 1.0))
            o.did(pool.memset(b2_raw[:, :], 0.0))
            o.wait()
            pool.affine_select(out=lower8[:, :, :], in_=lower8[:, :, :], compare_op=ALU.is_gt, fill=0.0, base=0,
                               pattern=[[1, NE], [-1, NE]], channel_multiplier=0).then_inc(S["moe_pool_consts"], 1)
            for b in range(NB):
                ln_pool(pool, 2 * NB + b)
                xb, ib = (t[:, b * TPB:(b + 1) * TPB, :] for t in (x_tok, inner))
                pool.tensor_tensor(xb, xb, ib, ALU.add)
            for e in range(NE):
                split_weights_pool(pool, e)
            pool.wait_ge(S["sw_split"], 1)
            lo_part(pool, sw[1][:, :, :], sw_raw[:, :, :], sw[0][:, :, :]).then_inc(S["sw_split"], 1)
            scan_pool(o, pool)

        W_IN, W_U, W_DB, W_DT, W_OUT = 0, 4, 8, 12, 14
        LN_C = 3 * NB

        def scan_names(b):
            return [("x", b, 0)] + [("in", b, j) for j in range(4)] + [("u", b, m) for m in range(2)] + \
                   [("db", b, m) for m in range(2)] + [("dt", b, m) for m in range(2)]

        def scan_emptied(kind, b, j):
            return {"x": (S["xT_lo"], NB + b + 1), "in": (S["c_in_read"], 4 * b + j + 1), "u": (S["c_u_read"], 2 * b + j + 1),
                    "db": (S["c_db_read"], 2 * b + j + 1), "dt": (S["c_dt_read"], 2 * b + j + 1),
                    "bbc": (S["bbc_done"], NS1 * b + j + 1), "out": (S["c_mixed"], b + 1)}[kind]

        names = scan_names(0)
        for b in range(NB):
            names += [("bbc", b, n) for n in range(NS1)]
            if b + 1 < NB:
                names += scan_names(b + 1)
            names += [("out", b, 0)]
        scan_fill = Fillings(bank[2:8], names, scan_emptied)

        def sweights(j):
            return [w[:, j, :] for w in sw]

        def scan_front_pe(pe, b):
            out = scan_fill.take(pe, "x", b, 0)
            ln_pe(pe, LN_C + b, out)
            pe.wait_ge(S["xT_lo"], NB + b + 1)
            for j in range(4):
                out = scan_fill.take(pe, "in", b, j)
                mm3(pe, out[:, :], sweights(W_IN + j), [x[:, :] for x in xT]).then_inc(S["c_in_filled"], 1)
            pe.wait_ge(S["xc_split"], b + 1)
            for name, w0, done in (("u", W_U, S["c_u_filled"]), ("db", W_DB, S["c_db_filled"])):
                for m in range(2):
                    out = scan_fill.take(pe, name, b, m)
                    for k in range(2):
                        ins = mm3(pe, out[:, :], sweights(w0 + 2 * k + m), [x[:, k, :] for x in xcs], start=(k == 0), stop=(k == 1))
                    ins.then_inc(done, 1)
            pe.wait_ge(S["dB_split"], b + 1)
            for m in range(2):
                out = scan_fill.take(pe, "dt", b, m)
                mm3(pe, out[:, :], sweights(W_DT + m), [x[:, 0, :] for x in dBs]).then_inc(S["c_dt_filled"], 1)

        def scan_front_act(o, act, b):
            act.wait_ge(S["ln_turned"], LN_C + b + 1)
            if b >= 1:
                act.wait_ge(S["c_in_filled"], 4 * b)
            act.activation(xT[0][:, :], scan_fill.bank("x", b, 0)[:, :], ACT.Copy).then_inc(S["xT_hi"], 1)
            act.wait_ge(S["conv_hist"], NB + b + 1)
            for j in range(2):
                act.wait_ge(S["c_in_filled"], 4 * b + j + 1)
                act.activation(cin1[:, j, CONV - 1:], scan_fill.bank("in", b, j)[:, :], ACT.Identity,
                               bias=C("in1_b", j)).then_inc(S["c_in_read"], 1)
            if b >= 1:
                act.wait_ge(S["y1_split"], b)
            for j in range(2):
                act.wait_ge(S["c_in_filled"], 4 * b + j + 3)
                act.activation(sz1[:, j, :], scan_fill.bank("in", b, 2 + j)[:, :], ACT.Silu,
                               bias=C("in1_b", 2 + j)).then_inc(S["c_in_read"], 1)
            for j in range(2):
                act.wait_ge(S["conv_done"], 4 * NB + 2 * b + j + 1)
                if b >= 1:
                    act.wait_ge(S["xc_split"], b)
                act.activation(xc[:, j, :], cacc1[:, j, :], ACT.Silu, bias=C("conv1_b", j)).then_inc(S["xc_ready"], 1)
            for m in range(2):
                act.wait_ge(S["c_u_filled"], 2 * b + m + 1)
                act.activation(u1[:, m, :], scan_fill.bank("u", b, m)[:, :], ACT.Identity,
                               bias=C("xu_b", m)).then_inc(S["c_u_read"], 1)
            if b >= 1:
                act.wait_ge(S["dB_split"], b)
            for m, bias in enumerate(("xd_b", "xB_b")):
                act.wait_ge(S["c_db_filled"], 2 * b + m + 1)
                act.activation(dB[:, m, :], scan_fill.bank("db", b, m)[:, :], ACT.Identity,
                               bias=C(bias)).then_inc(S["c_db_read"], 1)
            for m in range(2):
                act.wait_ge(S["c_dt_filled"], 2 * b + m + 1)
                act.activation(dv1[:, m, :], scan_fill.bank("dt", b, m)[:, :], ACT.Identity,
                               bias=C("dt1_b", m)).then_inc(S["c_dt_read"], 1)
            act.wait_ge(S["c_dt_read"], 2 * b + 2)
            o.did(act.activation(da1[:, :, :], dv1[:, :, :], ACT.Abs))
            o.wait()
            o.did(act.activation(da1[:, :, :], da1[:, :, :], ACT.Exp, scale=-1.0))
            o.wait()
            act.activation(da1[:, :, :], da1[:, :, :], ACT.Ln, bias=one[:, 0:1]).then_inc(S["dt_lnd"], 1)

        def scan_front_dve(o, dve, b):
            src = x_tok[:, b * TPB:(b + 1) * TPB, :]
            ln_stats_dve(o, dve, LN_C + b, src)
            ln_apply_dve(dve, LN_C + b, src, xn, 0)
            dve.wait_ge(S["xT_hi"], NB + b + 1)
            lo_part(dve, xT[1][:, :], scan_fill.bank("x", b, 0)[:, :], xT[0][:, :]).then_inc(S["xT_lo"], 1)
            if b == 0:
                dve.memset(cin1[:, :, 0:CONV - 1], 0.0).then_inc(S["conv_hist"], 1)
            else:
                dve.tensor_copy(cin1[:, :, 0:CONV - 1], cin1[:, :, BLK:BLK + CONV - 1]).then_inc(S["conv_hist"], 1)
                dve.wait_ge(S["xc_ready"], 2 * b)
            dve.wait_ge(S["conv_hist"], NB + b + 1)
            last = {}
            for k in range(CONV):
                for j in range(2):
                    w = C("conv1_w", CONV * j + k)
                    if k == 0:
                        dve.wait_ge(S["c_in_read"], 4 * b + j + 1)
                        last[j] = o.did(dve.tensor_scalar(cacc1[:, j, :], cin1[:, j, 0:BLK], w, None, ALU.mult))
                        continue
                    o.wait(last[j])
                    ins = dve.scalar_tensor_tensor(cacc1[:, j, :], cin1[:, j, k:k + BLK], w, cacc1[:, j, :], ALU.mult, ALU.add)
                    if k < CONV - 1:
                        last[j] = o.did(ins)
                    else:
                        ins.then_inc(S["conv_done"], 1)
            dve.wait_ge(S["xc_ready"], 2 * b + 2)
            if b >= 1:
                dve.wait_ge(S["c_db_filled"], 2 * b)
            o.did(dve.tensor_copy(xcs[0][:, :, :], xc[:, :, :]))
            o.wait()
            lo_part(dve, xcs[1][:, :, :], xc[:, :, :], xcs[0][:, :, :]).then_inc(S["xc_split"], 1)
            dve.wait_ge(S["c_db_read"], 2 * b + 2)
            if b >= 1:
                dve.wait_ge(S["bbc_filled"], NS1 * b)
            o.did(dve.tensor_copy(dBs[0][:, :, :], dB[:, :, :]))
            o.wait()
            lo_part(dve, dBs[1][:, :, :], dB[:, :, :], dBs[0][:, :, :]).then_inc(S["dB_split"], 1)
            dve.wait_ge(S["dt_lnd"], NB + b + 1)
            o.did(dve.scalar_tensor_tensor(delta[:, :, :], dv1[:, :, :], 0.0, da1[:, :, :], ALU.max, ALU.add))
            o.wait()
            if b >= 1:
                dve.wait_ge(S["drive_done"], NS1 * b)
            dve.tensor_tensor(du[:, :, :], delta[:, :, :], u1[:, :, :], ALU.mult).then_inc(S["delta_ready"], 1)

        def state_b_pe(pe, b, n):
            out = scan_fill.take(pe, "bbc", b, n)
            pe.matmul(out[:, :], sel16[:, n, :], dBs[1][:, 1, :], start=True, stop=False)
            pe.matmul(out[:, :], sel16[:, n, :], dBs[0][:, 1, :], start=False, stop=True).then_inc(S["bbc_filled"], 1)

        def state_sum_pe(pe, b, n):
            pe.wait_ge(S["scanned"], NS1 * b + n + 1)
            if n == 0 and b >= 1:
                pe.wait_ge(S["y1_read"], b)
            for j in range(2):
                ins = pe.matmul(bank[j][:, :], ident[:, :], hst[:, (NS1 * b + n) % 2, j, :], start=(n == 0), stop=(n == NS1 - 1))
            ins.then_inc(S["summed"], 1)

        def state_act(act, b, n):
            k = NS1 * b + n
            act.wait_ge(S["bbc_filled"], k + 1)
            if k >= 2:
                act.wait_ge(S["drive_done"], k - 1)
                act.wait_ge(S["scanned"], k - 1)
            act.activation(b_bc[:, k % 2, :], scan_fill.bank("bbc", b, n)[:, :], ACT.Copy).then_inc(S["bbc_done"], 1)
            if n == 0:
                act.wait_ge(S["delta_ready"], b + 1)
            act.activation(decay[:, k % 2, :, :], delta[:, :, :], ACT.Exp, scale=-float(n + 1)).then_inc(S["decay_done"], 1)

        def state_pool(pool, b, n):
            k = NS1 * b + n
            pool.wait_ge(S["bbc_done"], k + 1)
            if n == 0:
                pool.wait_ge(S["delta_ready"], b + 1)
            if k >= 2:
                pool.wait_ge(S["scanned"], k - 1)
            pool.tensor_tensor(drive[:, k % 2, :, :], du[:, :, :], b_bc[:, k % 2, :].unsqueeze(1).broadcast_to([P, 2, BLK]),
                               ALU.mult).then_inc(S["drive_done"], 1)

        def state_dve(o, dve, b, n):
            k = NS1 * b + n
            dve.wait_ge(S["decay_done"], k + 1)
            dve.wait_ge(S["drive_done"], k + 1)
            if k >= 2:
                dve.wait_ge(S["summed"], k - 1)
                dve.wait_ge(S["hlast_done"], k - 1)
            for j in range(2):
                init = 0.0 if b == 0 else hlast[:, n, j:j + 1]
                ins = dve.tensor_tensor_scan(hst[:, k % 2, j, :], decay[:, k % 2, j, :], drive[:, k % 2, j, :], init,
                                             ALU.mult, ALU.add)
            ins.then_inc(S["scanned"], 1)

        def state_last_dve(dve, b, n):
            k = NS1 * b + n
            dve.wait_ge(S["scanned"], k + 1)
            dve.tensor_copy(hlast[:, n, :], hst[:, k % 2, :, BLK - 1]).then_inc(S["hlast_done"], 1)

        def scan_y_dve(o, dve, b):
            dve.wait_ge(S["summed"], NS1 * (b + 1))
            for j in range(2):
                ins = dve.scalar_tensor_tensor(u1[:, j, :], u1[:, j, :], C("d1", j), bank[j][:, :], ALU.mult, ALU.add)
            ins.then_inc(S["y1_read"], 1)
            dve.wait_ge(S["y1_read"], b + 1)
            o.did(dve.tensor_tensor(u1[:, :, :], u1[:, :, :], sz1[:, :, :], ALU.mult))
            o.wait()
            if b >= 1:
                dve.wait_ge(S["c_out_filled"], b)
            o.did(dve.tensor_copy(y1s[0][:, :, :], u1[:, :, :]))
            o.wait()
            lo_part(dve, y1s[1][:, :, :], u1[:, :, :], y1s[0][:, :, :]).then_inc(S["y1_split"], 1)

        def scan_post_pe(pe, b):
            pe.wait_ge(S["y1_split"], b + 1)
            out = scan_fill.take(pe, "out", b, 0)
            for i in range(TPB):
                tt = slice(i * P, (i + 1) * P)
                for k in range(2):
                    ins = mm3(pe, out[:, tt], [y[:, k, tt] for y in y1s], sweights(W_OUT + k), start=(i == 0 and k == 0), stop=(k == 1))
            ins.then_inc(S["c_out_filled"], 1)

        def scan_post_dve(dve, b):
            dve.wait_ge(S["c_out_filled"], b + 1)
            xb = x_tok[:, b * TPB:(b + 1) * TPB, :]
            dve.tensor_tensor(xb, scan_fill.bank("out", b, 0)[:, :].rearrange("p (i d) -> p i d", i=TPB), xb,
                              ALU.add).then_inc(S["c_mixed"], 1)

        def scan_pe(pe):
            pe.wait_ge(S["sw_split"], 2)
            pe.wait_ge(S["moe_added"], NB)
            pe.wait_ge(S["sel16_done"], 1)
            scan_front_pe(pe, 0)
            for b in range(NB):
                for n in range(NS1 + 2):
                    if n < NS1:
                        state_b_pe(pe, b, n)
                    if n >= 2:
                        state_sum_pe(pe, b, n - 2)
                if b + 1 < NB:
                    scan_front_pe(pe, b + 1)
                scan_post_pe(pe, b)

        def scan_act(o, act):
            act.wait_ge(S["moe_added"], NB)
            scan_front_act(o, act, 0)
            for b in range(NB):
                for n in range(NS1):
                    state_act(act, b, n)
                for c in range(3 * b, min(3 * b + 3, 11)):
                    fweights_act(act, c)
                if b + 1 < NB:
                    scan_front_act(o, act, b + 1)

        def scan_dve(o, dve):
            dve.wait_ge(S["moe_added"], NB)
            dve.tensor_copy(sel16[:, :, :], ident[:, 0:NS1].unsqueeze(2).broadcast_to([P, NS1, P])).then_inc(S["sel16_done"], 1)
            scan_front_dve(o, dve, 0)
            for b in range(NB):
                for n in range(NS1 + 1):
                    if n < NS1:
                        state_dve(o, dve, b, n)
                    if n >= 1:
                        state_last_dve(dve, b, n - 1)
                scan_y_dve(o, dve, b)
                if b + 1 < NB:
                    scan_front_dve(o, dve, b + 1)
                scan_post_dve(dve, b)

        def scan_pool(o, pool):
            ln_pool(pool, LN_C)
            pool.wait_ge(S["in_out1_b"], 16)
            for b in range(NB):
                for n in range(NS1):
                    state_pool(pool, b, n)
                if b + 1 < NB:
                    ln_pool(pool, LN_C + b + 1)
                for c in range(3 * b, min(3 * b + 3, 11)):
                    fweights_pool(pool, c)
                pool.wait_ge(S["c_mixed"], b + 1)
                xb = x_tok[:, b * TPB:(b + 1) * TPB, :]
                pool.tensor_tensor(xb, xb, out1_b[:, :].unsqueeze(1).broadcast_to([P, TPB, D]), ALU.add).then_inc(S["x1_done"], 1)
            for b in range(NB):
                ln_pool(pool, LN_D + b)

        W_1, W_2, W_H1, W_H2, W_3 = 0, HC, 2 * HC, 2 * HC + HC * HC, 2 * HC + 2 * HC * HC
        LN_D = 4 * NB

        def net_names(b):
            return [("x", b, 0)] + [(w, b, m) for m in range(HC) for w in ("w1", "w2")] + \
                   [(w, b, m) for w in ("h1", "h2") for m in range(HC)] + [("w3", b, 0), ("turn", b, 0)]

        def net_emptied(kind, b, m):
            return {"x": (S["xT_lo"], 2 * NB + b + 1), "w1": (S["f_a_done"], HC * b + m + 1), "w2": (S["f_prod"], HC * b + m + 1),
                    "h1": (S["f_g_hi"], 2 * HC * b + m + 1), "h2": (S["f_g_hi"], 2 * HC * b + HC + m + 1),
                    "w3": (S["f_o_done"], b + 1), "turn": (S["f_added"], b + 1)}[kind]

        net_fill = Fillings(bank, [x for b in range(NB) for x in net_names(b)], net_emptied)

        def fweights(j):
            return [w[:, j, :] for w in fw]

        def net_pe(pe):
            pe.wait_ge(S["c_mixed"], NB)
            pe.wait_ge(S["fw_split"], 2 * 11)
            for b in range(NB):
                ln_pe(pe, LN_D + b, net_fill.take(pe, "x", b, 0))
                pe.wait_ge(S["xT_lo"], 2 * NB + b + 1)
                for m in range(HC):
                    for name, w0 in (("w1", W_1), ("w2", W_2)):
                        mm3(pe, net_fill.take(pe, name, b, m)[:, :], fweights(w0 + m), [x[:, :] for x in xT]).then_inc(S["f_filled"], 1)
                for l, (name, w0) in enumerate((("h1", W_H1), ("h2", W_H2))):
                    for m in range(HC):
                        out = net_fill.take(pe, name, b, m)
                        for k in range(HC):
                            if m == 0:
                                pe.wait_ge(S["f_split"], 3 * HC * b + HC * l + k + 1)
                            ins = mm3(pe, out[:, :], fweights(w0 + HC * k + m), [h[:, l, k, :] for h in fhs],
                                      start=(k == 0), stop=(k == HC - 1))
                        ins.then_inc(S["f_filled"], 1)
                out = net_fill.take(pe, "w3", b, 0)
                for k in range(HC):
                    pe.wait_ge(S["f_split"], 3 * HC * b + 2 * HC + k + 1)
                    ins = mm3(pe, out[:, :], fweights(W_3 + k), [h[:, 2, k, :] for h in fhs], start=(k == 0), stop=(k == HC - 1))
                ins.then_inc(S["f_filled"], 1)
                out = net_fill.take(pe, "turn", b, 0)
                pe.wait_ge(S["f_o_done"], b + 1)
                for i in range(TPB):
                    ins = pe.transpose(out[:, i * P:(i + 1) * P], fo[:, b % 2, i * P:(i + 1) * P], ident[:, :])
                ins.then_inc(S["f_turned"], 1)

        FPB = 4 * HC + 1

        def net_act(act):
            act.wait_ge(S["c_mixed"], NB)
            for b in range(NB):
                act.wait_ge(S["ln_turned"], LN_D + b + 1)
                act.activation(xT[0][:, :], net_fill.bank("x", b, 0)[:, :], ACT.Copy).then_inc(S["xT_hi"], 1)
                for m in range(HC):
                    act.wait_ge(S["f_filled"], FPB * b + 2 * m + 1)
                    if HC * b + m >= 2:
                        act.wait_ge(S["f_prod"], HC * b + m - 1)
                    act.activation(fa[:, m % 2, :], net_fill.bank("w1", b, m)[:, :], ACT.Silu,
                                   scale=C("w1_s", m)).then_inc(S["f_a_done"], 1)
                for m in range(HC):
                    act.wait_ge(S["f_prod"], HC * b + m + 1)
                    act.activation(fhs[0][:, 0, m, :], fh[:, m, :], ACT.Copy).then_inc(S["f_hi"], 1)
                for l, scale in enumerate(("h1_s", "h2_s")):
                    for m in range(HC):
                        act.wait_ge(S["f_filled"], FPB * b + 2 * HC + HC * l + m + 1)
                        act.wait_ge(S["f_split"], 3 * HC * b + HC * l + m + 1)
                        src = net_fill.bank("h1" if l == 0 else "h2", b, m)[:, :]
                        act.activation(fh[:, m, :], src, ACT.Gelu, scale=C(scale, m))
                        act.activation(fhs[0][:, l + 1, m, :], src, ACT.Gelu, scale=C(scale, m)).then_inc(S["f_g_hi"], 1)
                act.wait_ge(S["f_filled"], FPB * (b + 1))
                if b >= 2:
                    act.wait_ge(S["f_turned"], b - 1)
                act.activation(fo[:, b % 2, :], net_fill.bank("w3", b, 0)[:, :], ACT.Identity, scale=C("w3_s")).then_inc(S["f_o_done"], 1)

        def net_dve(o, dve):
            for b in range(NB):
                src = x_tok[:, b * TPB:(b + 1) * TPB, :]
                dve.wait_ge(S["x1_done"], b + 1)
                ln_stats_dve(o, dve, LN_D + b, src)
                ln_apply_dve(dve, LN_D + b, src, xn, 0)
                dve.wait_ge(S["xT_hi"], 2 * NB + b + 1)
                lo_part(dve, xT[1][:, :], net_fill.bank("x", b, 0)[:, :], xT[0][:, :]).then_inc(S["xT_lo"], 1)
                for m in range(HC):
                    dve.wait_ge(S["f_filled"], FPB * b + 2 * m + 2)
                    dve.wait_ge(S["f_a_done"], HC * b + m + 1)
                    if b >= 1:
                        dve.wait_ge(S["f_split"], 3 * HC * b)
                    dve.scalar_tensor_tensor(fh[:, m, :], net_fill.bank("w2", b, m)[:, :], C("w2_s", m), fa[:, m % 2, :],
                                             ALU.mult, ALU.mult).then_inc(S["f_prod"], 1)
                for l in range(3):
                    for m in range(HC):
                        if l == 0:
                            dve.wait_ge(S["f_hi"], HC * b + m + 1)
                        else:
                            dve.wait_ge(S["f_g_hi"], 2 * HC * b + HC * (l - 1) + m + 1)
                        lo_part(dve, fhs[1][:, l, m, :], fh[:, m, :], fhs[0][:, l, m, :]).then_inc(S["f_split"], 1)
                dve.wait_ge(S["f_turned"], b + 1)
                dve.tensor_tensor(src, net_fill.bank("turn", b, 0)[:, :].rearrange("p (i d) -> p i d", i=TPB), src,
                                  ALU.add).then_inc(S["f_added"], 1)

        def fweights_sp(sp):
            for c in range(11):
                if c >= 2:
                    sp.wait_ge(S["fw_split"], 2 * (c - 1))
                sp.dma_start(fw_raw[:, c % 2, :, :], a["net"][:, c * 4 * P:(c + 1) * 4 * P].rearrange("p (j m) -> p j m", m=P)
                             ).then_inc(fw_in[c % 2], 16)

        fw_in = [sem("fw_in0"), sem("fw_in1")]

        def fweights_act(act, c):
            act.wait_ge(fw_in[c % 2], 16 * (c // 2 + 1))
            act.activation(fw[0][:, 4 * c:4 * c + 4, :], fw_raw[:, c % 2, :, :], ACT.Copy).then_inc(S["fw_hi"], 1)

        def fweights_pool(pool, c):
            pool.wait_ge(S["fw_hi"], c + 1)
            lo_part(pool, fw[1][:, 4 * c:4 * c + 4, :], fw_raw[:, c % 2, :, :], fw[0][:, 4 * c:4 * c + 4, :]).then_inc(S["fw_split"], 2)

        block = ctx.enter_context(nc.Block())

        @block.sync
        def _(sp):
            sp.dma_start(x_tok[:, :, :], a["x"].rearrange("b (i p) d -> p (b i) d", p=P)).then_inc(S["in_x"], 16)
            sp.dma_start(cols[:, :], a["cols"]).then_inc(S["in_cols"], 16)
            sp.dma_start(w_raw[:, :], a["win"]).then_inc(S["in_win"], 16)
            sp.dma_start(wg_raw[:, :, :], a["wgo"].rearrange("p (j m) -> p j m", m=P)).then_inc(S["in_wg"], 16)
            sp.dma_start(wqkv_raw[:, :, :], a["wqkv"].rearrange("p (j m) -> p j m", m=P)).then_inc(S["in_qkv"], 16)
            sp.dma_start(wo[:, :, :], a["wo"].rearrange("p (g d) -> p g d", g=4)).then_inc(S["in_wo"], 16)
            sp.dma_start(bv[:, :], a["bv"].partition_broadcast(P)).then_inc(S["in_wo"], 16)
            sp.dma_start(bo[:, :], a["bo"].partition_broadcast(P)).then_inc(S["in_wo"], 16)
            sp.dma_start(den_sel[:, :], a["den_sel"]).then_inc(S["in_wo"], 16)
            sp.wait_ge(S["x_mixed"], NB)
            for b in range(NB):
                qkv_sp(sp, b)
            attention_sp(sp)
            sp.wait_ge(S["moe_pool_consts"], 1)
            sp.dma_start(b2_raw[0:NE, :], a["fc2_b"]).then_inc(S["in_moe"], 16)
            sp.dma_start(gw[:, :], a["gate_w"]).then_inc(S["in_moe"], 16)
            experts_sp(sp)
            sp.dma_start(sw_raw[:, :, :], a["scan"].rearrange("p (j m) -> p j m", m=P)).then_inc(S["in_sw"], 16)
            sp.dma_start(out1_b[:, :], a["out1_b"].partition_broadcast(P)).then_inc(S["in_out1_b"], 16)
            sp.wait_ge(S["moe_added"], NB)
            fweights_sp(sp)
            sp.wait_ge(S["f_added"], NB)
            sp.dma_start(a["out"].rearrange("b (i p) d -> p (b i) d", p=P), x_tok[:, :, :]).then_inc(S["stored"], 16)
            sp.wait_ge(S["stored"], 16)

        @block.gpsimd
        def _(pool):
            o = Order(pool, S["pool_order"])
            o.did(pool.memset(ident[:, :], 0.0))
            o.did(pool.memset(tri[:, :], 1.0))
            o.did(pool.memset(headmask[:, :, :], 1.0))
            o.did(pool.memset(maskneg[:, :], 0.0))
            o.did(pool.memset(mhalf[:, :], -0.5))
            o.did(pool.memset(one[:, :], 1.0))
            o.wait()
            o.did(pool.affine_select(out=ident[:, :], in_=ident[:, :], compare_op=ALU.not_equal, fill=1.0, base=0,
                                     pattern=[[-1, P]], channel_multiplier=1))
            o.did(pool.affine_select(out=tri[:, :], in_=tri[:, :], compare_op=ALU.is_ge, fill=0.0, base=0,
                                     pattern=[[1, P]], channel_multiplier=-1))
            o.did(pool.affine_select(out=maskneg[:, :], in_=maskneg[:, :], compare_op=ALU.is_ge, fill=NEG, base=0,
                                     pattern=[[1, P]], channel_multiplier=-1))
            o.did(pool.affine_select(out=headmask[:, :, :], in_=headmask[:, :, :], compare_op=ALU.is_ge, fill=0.0, base=0,
                                     pattern=[[-NS0, H0], [0, HD0]], channel_multiplier=1))
            o.wait()
            pool.affine_select(out=headmask[:, :, :], in_=headmask[:, :, :], compare_op=ALU.is_ge, fill=0.0, base=NS0 - 1,
                               pattern=[[NS0, H0], [0, HD0]], channel_multiplier=-1).then_inc(S["consts"], 1)
            pool.wait_ge(S["w_split"], 1)
            lo_part(pool, win[1][:, :, :], w_raw[:, :].rearrange("p (j m) -> p j m", m=P), win[0][:, :, :]).then_inc(S["w_split"], 1)
            ln_pool(pool, 0)
            pool.wait_ge(S["w_split"], 3)
            lo_part(pool, wgo[1][:, :, :], wg_raw[:, :, :], wgo[0][:, :, :]).then_inc(S["w_split"], 1)
            for b in range(NB):
                if b + 1 < NB:
                    ln_pool(pool, b + 1)
                pool.wait_ge(S["y_var"], b + 1)
                pool.tensor_tensor(ln_rs[:, 0, :], ln_ve[:, 0, :], mhalf[:, 0:TPB], ALU.pow).then_inc(S["y_rstd"], 1)
            pool.wait_ge(S["qkv_split"], 1)
            lo_part(pool, wqkv[1][:, :, :], wqkv_raw[:, :, :], wqkv[0][:, :, :]).then_inc(S["qkv_split"], 1)
            pool.wait_ge(S["x_mixed"], NB)
            ln_pool(pool, NB, double=True)
            o.did(pool.memset(kz[:, :, :].bitcast(mybir.dt.uint32), 0))
            o.wait()
            o.did(pool.memset(kz[32:64, 0::2, :], 1.0))
            o.wait()
            pool.memset(kz[96:128, 1::2, :], 1.0).then_inc(S["kz_ready"], 1)
            pool.wait_ge(S["kz_ready"], 1)
            pool.wait_ge(S["in_wo"], 64)
            for b in range(NB):
                if b:
                    ln_pool(pool, NB + b, double=True)
                pool.wait_ge(S["inner_ready"], b + 1)
                ib = inner[:, b * TPB:(b + 1) * TPB, :]
                pool.tensor_tensor(ib, ib, bo[:, :].unsqueeze(1).broadcast_to([P, TPB, D]), ALU.add).then_inc(S["bo_added"], 1)
            moe_pool(o, pool)

        @block.scalar
        def _(act):
            o = Order(act, S["act_order"])
            act.wait_ge(S["in_cols"], 16)
            act.activation(a_neg[:, :], C("a_log"), ACT.Exp).then_inc(S["a_ready"], 1)
            act.wait_ge(S["in_win"], 16)
            act.activation(win[0][:, :, :], w_raw[:, :].rearrange("p (j m) -> p j m", m=P), ACT.Copy).then_inc(S["w_split"], 1)
            front_act(o, act, 0)
            act.wait_ge(S["in_wg"], 16)
            act.wait_ge(S["w_split"], 2)
            act.activation(wgo[0][:, :, :], wg_raw[:, :, :], ACT.Copy).then_inc(S["w_split"], 1)
            for b in range(NB):
                for c in range(TPB):
                    chunk_act(act, TPB * b + c)
                if b + 1 < NB:
                    front_act(o, act, b + 1)
                post_act(act, b)
            act.wait_ge(S["in_qkv"], 16)
            act.activation(wqkv[0][:, :, :], wqkv_raw[:, :, :], ACT.Copy).then_inc(S["qkv_split"], 1)
            act.wait_ge(S["x_mixed"], NB)
            for b in range(NB):
                qkv_act(act, b)
            attention_act(act)
            moe_act(act)
            act.wait_ge(S["in_sw"], 16)
            act.activation(sw[0][:, :, :], sw_raw[:, :, :], ACT.Copy).then_inc(S["sw_split"], 1)
            scan_act(o, act)
            net_act(act)

        @block.vector
        def _(dve):
            o = Order(dve, S["dve_order"])
            dve.memset(state[:, 0, :], 0.0).then_inc(S["state_done"], 1)
            dve.wait_ge(S["consts"], 1)
            o.did(dve.tensor_copy(tri_r[:, :], tri[:, :]))
            o.did(dve.tensor_scalar(negtri_r[:, :], tri[:, :], -1.0, None, ALU.mult))
            o.did(dve.tensor_copy(identb[:, :], ident[:, :]))
            dve.wait_ge(S["a_ready"], 1)
            dve.tensor_scalar(a_neg[:, :], a_neg[:, :], -1.0, None, ALU.mult).then_inc(S["consts_r"], 1)
            dve.wait_ge(S["consts_r"], 1)
            dve.wait_ge(S["in_x"], 16)
            front_dve(o, dve, 0)
            for b in range(NB):
                for c in range(TPB + 1):
                    g = TPB * b + c
                    if c < TPB:
                        chunk_front_dve(dve, g)
                    if c >= 1:
                        chunk_back_dve(o, dve, g - 1)
                    if c < TPB:
                        chunk_mid_dve(dve, g)
                if b + 1 < NB:
                    front_dve(o, dve, b + 1)
                post_dve(o, dve, b)
            dve.wait_ge(S["x_mixed"], NB)
            o.did(dve.memset(v9[:, :], 1.0))
            dve.memset(qa[:, :, :].bitcast(mybir.dt.uint32), 0).then_inc(S["qk_zero"], 1)
            o.wait()
            dve.wait_ge(S["in_wo"], 64)
            for b in range(NB):
                qkv_dve(o, dve, b)
            dve.wait_ge(S["bo_added"], NB)
            attention_dve(o, dve)
            moe_dve(o, dve)
            scan_dve(o, dve)
            net_dve(o, dve)

        @block.tensor
        def _(pe):
            ring = Ring(pe, bank[0:3])
            pe.wait_ge(S["consts"], 1)
            pe.wait_ge(S["consts_r"], 1)
            front_pe(pe, ring, 0)
            for b in range(NB):
                for c in range(TPB + 1):
                    if c < TPB:
                        chunk_front_pe(pe, TPB * b + c)
                    if c >= 1:
                        chunk_back_pe(pe, TPB * b + c - 1)
                if b + 1 < NB:
                    front_pe(pe, ring, b + 1)
                post_pe(pe, ring, b)
            pe.wait_ge(S["x_mixed"], NB)
            pe.wait_ge(S["in_wo"], 64)
            for b in range(NB):
                qkv_pe(pe, b)
            pe.wait_ge(S["qk_evac"], 2 * NB)
            pe.wait_ge(S["v_done"], NB)
            pe.wait_ge(S["parts_loaded"], 24 * 16 * NB)
            attention_pe(pe)
            moe_pe(pe)
            scan_pe(pe)
            net_pe(pe)


def host_layout(x):
    import numpy as np

    win = x["L0_attn_W_in"]
    rows = [win[3 * DI:3 * DI + P], win[3 * DI + P:3 * DI + 2 * P],
            np.tile(win[4 * DI:4 * DI + NS0], (H0, 1)), np.tile(win[4 * DI + NS0:4 * DI + 2 * NS0], (H0, 1)),
            np.repeat(win[4 * DI + 2 * NS0:], NS0, axis=0),
            win[0:P], win[P:2 * P], win[DI:DI + P], win[DI + P:2 * DI]]
    out = {"x": x["L0_attn_u"], "win": np.concatenate(rows, 0).T}

    def kxm(w, k, m):
        return w.reshape(k, P, m, P).transpose(1, 0, 2, 3).reshape(P, k * m * P)

    out["wgo"] = np.concatenate([kxm(x["L0_attn_W_gate"].T, 2, 2), kxm(x["L0_attn_W_out"].T, 4, 1)], 1)

    wqkv = x["L0_ffn_Wqkv"]
    out["wqkv"] = wqkv
    wo = x["L0_ffn_Wo"].reshape(4, 4, HDA, D)
    pad_wo = np.zeros((4, 4, 32, D), np.float32)
    pad_wo[:, :, 0:HDA] = wo
    out["wo"] = pad_wo.reshape(4, P, D).transpose(1, 0, 2).reshape(P, 4 * D)
    out["bv"], out["bo"] = x["L0_ffn_bqkv"][2 * P:], x["L0_ffn_bo"]
    out["experts"] = np.concatenate(
        [x["L0_ffn_fc1_w"].transpose(0, 2, 1), np.stack([kxm(w.T, FC, 1) for w in x["L0_ffn_fc2_w"]])], 2)
    out["fc2_b"], out["gate_w"] = x["L0_ffn_fc2_b"], x["L0_ffn_gate_W"]
    xw, dw = x["L1_attn_x_proj_w"], x["L1_attn_dt_proj_w"]
    xdb = np.zeros((DI, 2 * P), np.float32)
    xdb[:, 0:NS1], xdb[:, P:P + NS1] = xw[:, 0:NS1], xw[:, NS1:2 * NS1]
    dtw = np.zeros((P, DI), np.float32)
    dtw[0:NS1] = dw
    out["scan"] = np.concatenate([x["L1_attn_in_proj_w"], kxm(xw[:, 2 * NS1:], 2, 2), kxm(xdb, 2, 2), dtw,
                                  kxm(x["L1_attn_out_proj_w"], 2, 1)], 1)
    out["out1_b"] = x["L1_attn_out_proj_b"]
    out["net"] = np.concatenate([x["L1_ffn_w1_w"].T, x["L1_ffn_w2_w"].T, kxm(x["L1_ffn_h1_w"].T, HC, HC),
                                 kxm(x["L1_ffn_h2_w"].T, HC, HC), kxm(x["L1_ffn_w3_w"].T, HC, 1)], 1)
    sel = np.zeros((P, P), np.float32)
    for m in range(P):
        sel[m // 32 * 32 + HDA, m] = 1
    out["den_sel"] = sel

    def vec(v, n):
        return np.asarray(v).reshape(n, P).T

    cw = x["L0_attn_conv_w"][:, 0, :]
    cb = x["L0_attn_conv_b"]
    conv = [cw[0:P], cw[P:DI], np.tile(cw[DI:DI + NS0], (H0, 1)), np.tile(cw[DI + NS0:], (H0, 1))]
    convb = [cb[0:P], cb[P:DI], np.tile(cb[DI:DI + NS0], H0), np.tile(cb[DI + NS0:], H0)]
    c1 = x["L1_attn_conv_w"][:, 0, :]
    xpb = x["L1_attn_x_proj_b"]
    pad = np.zeros(P - NS1, np.float32)
    put = {
        "conv0_w": np.concatenate(conv, 1), "conv0_b": np.stack(convb, 1),
        "dt_bias": np.repeat(x["L0_attn_dt_bias"], NS0)[:, None], "a_log": np.repeat(x["L0_attn_A_log"], NS0)[:, None],
        "d0": vec(np.repeat(x["L0_attn_D_param"], HD0), 2), "gamma": vec(x["L0_attn_ln_gamma"], 2),
        "beta": vec(x["L0_attn_ln_beta"], 2), "b_gate": vec(x["L0_attn_b_gate"], 2),
        "ln1_w": vec(x["L0_ffn_ln1_w"], 1), "ln1_b": vec(x["L0_ffn_ln1_b"], 1),
        "ln2_w": vec(x["L0_ffn_ln2_w"], 1), "ln2_b": vec(x["L0_ffn_ln2_b"], 1),
        "bq": vec(x["L0_ffn_bqkv"][0:P], 1), "bk": vec(x["L0_ffn_bqkv"][P:2 * P], 1),
        "fc1_b": vec(x["L0_ffn_fc1_b"], NE * FC), "in1_b": vec(x["L1_attn_in_proj_b"], 4),
        "conv1_w": np.concatenate([c1[0:P], c1[P:]], 1), "conv1_b": vec(x["L1_attn_conv_b"], 2),
        "xu_b": vec(xpb[2 * NS1:], 2), "xd_b": vec(np.concatenate([xpb[0:NS1], pad]), 1),
        "xB_b": vec(np.concatenate([xpb[NS1:2 * NS1], pad]), 1), "dt1_b": vec(x["L1_attn_dt_proj_b"], 2),
        "d1": vec(x["L1_attn_D"], 2), "w1_s": vec(x["L1_ffn_w1_s"], HC), "w2_s": vec(x["L1_ffn_w2_s"], HC),
        "h1_s": vec(x["L1_ffn_h1_s"], HC), "h2_s": vec(x["L1_ffn_h2_s"], HC), "w3_s": vec(x["L1_ffn_w3_s"], 1),
        "out1_b": vec(x["L1_attn_out_proj_b"], 1),
    }
    out["cols"] = np.concatenate([put[n] for n, _ in _COLS], 1)
    return {k: np.ascontiguousarray(v) for k, v in out.items()}


def kernel(**inputs):
    import numpy as np
    import concourse.bacc as bacc
    from concourse.bass_utils import run_bass_kernel_spmd

    arrays = host_layout({name: np.asarray(v) for name, v in inputs.items()})
    nc = bacc.Bacc("TRN2", target_bir_lowering=False, num_devices=1)
    tensors = {name: nc.dram_tensor(name + "_dram", v.shape, mybir.dt.from_np(v.dtype), kind="ExternalInput").ap()
               for name, v in arrays.items()}
    tensors["out"] = nc.dram_tensor("out_dram", (1, T, D), F32, kind="ExternalOutput").ap()
    build(nc, tensors)
    r = run_bass_kernel_spmd(nc, [{name + "_dram": v for name, v in arrays.items()}], core_ids=[0])
    return r.results[0]["out_dram"]
```

```python
from contextlib import ExitStack

import concourse.bass as bass
from concourse import mybir

F32 = mybir.dt.float32
F32R = mybir.dt.float32r
BF16 = mybir.dt.bfloat16
ALU = mybir.AluOpType
ACT = mybir.ActivationFunctionType
AX = mybir.AxisListType

P = 128
T = 2048
D = 128
BLK = 512
NB = T // BLK
TPB = BLK // P
NT = T // P
EPS = 1e-5
NEG = -1e30

H0, HD0, NS0, CONV = 8, 32, 16, 4
DI = 256
HA, HDA = 16, 8
NE, FF = 8, 512
FC = FF // P
NS1 = 16
HBUF = 4
HID = 512
HC = HID // P

XA, XB, BREP, CREP, DTREP, Z0A, Z0B, X0A, X0B = range(9)

_COLS = [
    ("conv0_w", 4 * CONV), ("conv0_b", 4), ("dt_bias", 1), ("a_log", 1), ("d0", 2), ("gamma", 2), ("beta", 2),
    ("b_gate", 2), ("ln1_w", 1), ("ln1_b", 1), ("ln2_w", 1), ("ln2_b", 1), ("bq", 1), ("bk", 1),
    ("fc1_b", NE * FC), ("in1_b", 4), ("conv1_w", 2 * CONV), ("conv1_b", 2), ("xu_b", 2), ("xdB_b", 1),
    ("dt1_b", 2), ("d1", 2), ("w1_s", HC), ("w2_s", HC), ("h1_s", HC), ("h2_s", HC), ("w3_s", 1),
    ("out1_b", 1),
]
COL = {}
_n = 0
for _name, _w in _COLS:
    COL[_name] = _n
    _n += _w
NCOL = _n


class Order:

    def __init__(self, eng, sem):
        self.eng, self.sem, self.n = eng, sem, 0

    def did(self, ins):
        ins.then_inc(self.sem, 1)
        self.n += 1
        return self.n

    def wait(self, n=None):
        self.eng.wait_ge(self.sem, self.n if n is None else n)


class Fillings:

    def __init__(self, banks, names, emptied):
        self.banks, self.names, self.emptied = banks, names, emptied
        self.at = {name: n for n, name in enumerate(names)}

    def bank(self, *name):
        return self.banks[self.at[name] % len(self.banks)]

    def take(self, pe, *name):
        n = self.at[name]
        if n >= len(self.banks):
            pe.wait_ge(*self.emptied(*self.names[n - len(self.banks)]))
        return self.bank(*name)


def build(nc, a):
    ctx = ExitStack()
    sems = {}

    def sem(name):
        if name not in sems:
            sems[name] = ctx.enter_context(nc.semaphore(name))
        return sems[name]

    free = [0]

    def sb(name, shape, dt, at=None):
        size = 4 if dt in (F32, F32R) else 2
        for s in shape[1:]:
            size *= s
        size = (size + 31) // 32 * 32
        if at is None:
            at = free[0]
            free[0] += size
        t = nc.alloc_sbuf_tensor_at(name, shape, dt, offset=at + BASE)
        t_end[name] = at + size
        return t

    t_end = {}
    BASE = (nc.sbuf_base + 31) // 32 * 32
    with ctx:
        x_tok = sb("x_tok", [P, NT, D], F32)
        cols = sb("cols", [P, NCOL], F32)
        ident = sb("ident", [P, P], F32)
        identb = sb("identb", [P, P], BF16)
        tri = sb("tri", [P, P], F32)
        tri_r = sb("tri_r", [P, P], F32R)
        negtri_r = sb("negtri_r", [P, P], F32R)
        maskneg = sb("maskneg", [P, P], BF16)
        headmask = sb("headmask", [P, H0, HD0], F32)
        mhalf = sb("mhalf", [P, 8], F32)
        one = sb("one", [P, 1], F32)
        a_neg = sb("a_neg", [P, 1], F32)
        ln_st = sb("ln_st", [P, TPB, 6], F32)
        ln_mv = sb("ln_mv", [P, TPB, 2], F32)
        ln_ve = sb("ln_ve", [P, 2, TPB], F32)
        ln_rs = sb("ln_rs", [P, 2, TPB], F32)
        xn = sb("xn", [P, TPB, D], F32)
        xT = [sb("xT_hi", [D, BLK], F32R), sb("xT_lo", [D, BLK], F32R)]
        SHARED = free[0]

        w_raw = sb("w_raw", [P, 9 * P], F32)
        win = [sb("win_hi", [P, 9, P], F32R), sb("win_lo", [P, 9, P], F32R)]
        wg_raw = sb("wg_raw", [P, 8, P], F32)
        wgo = [sb("wgo_hi", [P, 8, P], F32R), sb("wgo_lo", [P, 8, P], F32R)]
        convin = sb("convin", [P, 4, CONV - 1 + BLK], F32)
        cacc = sb("cacc", [P, 4, BLK], F32)
        xs_even = sb("xs_even", [P, 4, BLK], F32)
        dtv = sb("dtv", [P, BLK], F32)
        dta = sb("dta", [P, BLK], F32)
        dte = sb("dte", [P, BLK], F32)
        cs = sb("cs", [P, BLK], F32)
        eb = sb("eb", [P, BLK], F32)
        sz = sb("sz", [P, 2, BLK], F32)
        skip = sb("skip", [P, 2, BLK], F32)
        cat = [sb("cat_hi", [P, 2, 2, BLK], F32R), sb("cat_lo", [P, 2, 2, BLK], F32R)]
        gy = [sb("gy_hi", [P, 2, BLK], F32R), sb("gy_lo", [P, 2, BLK], F32R)]
        dt_tok = sb("dt_tok", [P, 2, H0], F32)
        dA_tok = [sb("dA_hi", [P, 2, H0], F32R), sb("dA_lo", [P, 2, H0], F32R)]
        bd_tok = sb("bd_tok", [P, 2, P], F32)
        xdt = sb("xdt", [P, 2, H0, HD0], F32)
        edec = sb("edec", [P, 2, H0, P], F32)
        mdec = sb("mdec", [P, 2, H0, P], F32)
        state = sb("state", [P, 2, DI], F32)
        stmp = sb("stmp", [P, DI], F32)
        y_fm_even = sb("y_fm_even", [P, 2, BLK], F32)
        dt, dtA, ecs, cdec, bdec = ([sb(f"{n}_even", [P, BLK], F32)] for n in ("dt", "dtA", "ecs", "cdec", "bdec"))
        yn = sb("yn", [P, TPB, DI], F32)
        yst = sb("yst", [P, TPB, 6], F32)
        ymv = sb("ymv", [P, TPB, 2], F32)
        yg = sb("yg", [P, 2, BLK], F32)
        ygs = [sb("yg_hi", [P, 2, BLK], F32R), sb("yg_lo", [P, 2, BLK], F32R)]
        sg = sb("sg", [P, 2, BLK], F32)
        y2 = sb("y2", [P, 2, BLK], F32)

        A_END = free[0]

        wqkv_raw = sb("wqkv_raw", [P, 3, P], F32)
        wqkv = [sb("wqkv_hi", [P, 3, P], F32R), sb("wqkv_lo", [P, 3, P], F32R)]
        wo = sb("wo", [P, D], F32)
        bv = sb("bv", [P, D], F32)
        bo = sb("bo", [P, D], F32)
        W_END = free[0]

        xs = [xs_even, sb("xs_odd", [P, 4, BLK], F32)]
        y_fm = [y_fm_even, sb("y_fm_odd", [P, 2, BLK], F32)]
        for bufs, n in ((dt, "dt"), (dtA, "dtA"), (ecs, "ecs"), (cdec, "cdec"), (bdec, "bdec")):
            bufs.append(sb(f"{n}_odd", [P, BLK], F32))
        assert BASE + free[0] <= nc.sbuf_usable_end

        free[0] = SHARED
        inner = sb("inner", [P, NT, D], F32)
        I_END = free[0]
        kz = sb("kz", [P, HA, T], BF16)
        qa = sb("qa", [P, HA // 2, T], BF16)
        VW = HA * (HDA + 1)
        v9 = sb("v9", [P, NT * VW + 32], F32)
        probs = sb("probs", [P, 2, 4, 2, BLK], F32)
        assert free[0] <= A_END, (free[0], A_END)
        free[0] = W_END
        nx = sb("nx", [P, BLK], F32)
        nxs = [sb("nx_hi", [P, BLK], F32R), sb("nx_lo", [P, BLK], F32R)]
        QK_AT = free[0]
        qk_f = sb("qk_f", [P, 2, BLK], F32)
        qk_r = sb("qk_r", [P, 2, BLK], F32)
        qk_parts = sb("qk_parts", [P, 2, 3, BLK], BF16)
        mx = sb("mx", [P, 16, 4], F32)
        mneg = sb("mneg", [P, 2, 16], F32)
        mrow = sb("mrow", [4, 2, 2, BLK], BF16)
        o_sb = sb("o_sb", [P, BLK], F32)
        rden = sb("rden", [P, 2, TPB, 4, 1], F32)
        o_tok = sb("o_tok", [P, TPB, D], F32)
        o_fm = sb("o_fm", [P, BLK], F32)
        END = free[0]
        assert BASE + END <= nc.sbuf_usable_end, (END, nc.sbuf_usable_end)

        free[0] = I_END
        nx2 = [sb("nx2_hi", [P, T], F32R), sb("nx2_lo", [P, T], F32R)]
        gT = [sb("gT_hi", [P, T], F32R), sb("gT_lo", [P, T], F32R)]
        nx2f = sb("nx2f", [P, BLK], F32)
        ew_raw = sb("ew_raw", [P, 2, 8, P], F32)
        ew = [sb("ew_hi", [P, 2, 8, P], F32R), sb("ew_lo", [P, 2, 8, P], F32R)]
        hid = sb("hid", [P, 3, FC, BLK], F32)
        hids = [sb("hid_hi", [P, 2, FC, BLK], F32R), sb("hid_lo", [P, 2, FC, BLK], F32R)]
        gate_bc = sb("gate_bc", [P, 3, BLK], F32)
        moe_sb = sb("moe_sb", [P, 2, BLK], F32)
        sel8 = sb("sel8", [P, NE, P], F32R)
        b2_raw = sb("b2_raw", [P, D], F32)
        b2 = [sb("b2_hi", [P, D], F32R), sb("b2_lo", [P, D], F32R)]
        gw = sb("gw", [P, NE], F32)
        lower8 = sb("lower8", [P, NE, NE], F32)
        lg = sb("lg", [P, TPB, NE], F32)
        above = sb("above", [P, TPB, NE, NE], F32)
        equal = sb("equal", [P, TPB, NE, NE], F32)
        rank = sb("rank", [P, TPB, NE], F32)
        lgm = sb("lgm", [P, TPB, 1], F32)
        ex8 = sb("ex8", [P, TPB, NE], F32)
        gates = sb("gates", [P, TPB, P], F32)
        assert free[0] <= A_END, (free[0], A_END)

        free[0] = W_END
        sw_raw = sb("sw_raw", [P, 14, P], F32)
        sw = [sb("sw_hi", [P, 14, P], F32R), sb("sw_lo", [P, 14, P], F32R)]
        out1_b = sb("out1_b", [P, D], F32)
        sz1 = [sb("sz1_even", [P, 2, BLK], F32)]
        assert BASE + free[0] <= nc.sbuf_usable_end

        free[0] = SHARED
        N_FFN = 2 * HC + 2 * HC * HC + HC
        fw_raw = sb("fw_raw", [P, 2, 4, P], F32)
        fw = [sb("fw_hi", [P, N_FFN, P], F32R), sb("fw_lo", [P, N_FFN, P], F32R)]
        SCAN_AT = free[0]
        cin1 = sb("cin1", [P, 2, CONV - 1 + BLK], F32)
        sz1.append(sb("sz1_odd", [P, 2, BLK], F32))
        u1 = sb("u1", [P, 2, 2, BLK], F32)
        CACC_AT = free[0]
        cacc1 = sb("cacc1", [P, 2, BLK], F32)
        XC_AT = free[0]
        xc = sb("xc", [P, 2, BLK], F32)
        xcs = [sb("xc_hi", [P, 2, BLK], F32R), sb("xc_lo", [P, 2, BLK], F32R)]
        dB = sb("dB", [P, BLK], F32, at=CACC_AT)
        dBs = [sb("dB_hi", [P, 2, BLK], F32R), sb("dB_lo", [P, 2, BLK], F32R)]
        dv1 = sb("dv1", [P, 2, BLK], F32, at=XC_AT)
        da1 = sb("da1", [P, 2, BLK], F32, at=CACC_AT)
        delta = sb("delta", [P, 2, 2, BLK], F32)
        du = sb("du", [P, 2, 2, BLK], F32)
        b_bc = sb("b_bc", [P, 2, BLK], F32)
        decay = sb("decay", [P, 2, 2, BLK], F32)
        drive = sb("drive", [P, 2, 2, BLK], F32)
        hst = sb("hst", [P, HBUF, 2, BLK], F32)
        hlast = sb("hlast", [P, NS1, 2], F32)
        sel16 = sb("sel16", [P, NS1, P], F32R)
        y1s = [sb("y1_hi", [P, 2, BLK], F32R), sb("y1_lo", [P, 2, BLK], F32R)]
        assert free[0] <= W_END, (free[0], W_END)
        free[0] = SCAN_AT
        fa = sb("fa", [P, 2, BLK], F32)
        fh = sb("fh", [P, HC, BLK], F32)
        fhs = [sb("fh_hi", [P, 3, HC, BLK], F32R), sb("fh_lo", [P, 3, HC, BLK], F32R)]
        fo = sb("fo", [P, 2, BLK], F32)
        assert free[0] <= W_END, (free[0], W_END)
        psum = ctx.enter_context(nc.psum_tensor("psum", [P, 8, BLK], F32))
        bank = [psum[:, i, :] for i in range(8)]
        s_pair = [psum[:, 0:2, :], psum[:, 2:4, :]]

        S = {n: sem(n) for n in """
            ln_var ln_rstd ln_turned ln_xn pj_act pj_dve xT_lo yn_done yg_done sg_done end_act x_mixed xT_hi
            w_split pj_filled dec_done tok_dve turned m_done xs_ready e_done arg_filled y_done state_done
            s_filled yt_filled yb_filled yg_split gate_filled skip_split gy_split out_filled conv_hist dt_done
            dt_lnd cs_done ecs_done eb_done conv_done skip_done y2_done y_var y_rstd dA_hi nx_ready nx_split
            qkv_split qk_evac qk_filled v_done v_filled parts_done inner_ready parts_saved v_ones qk_cleared
            bo_added mx_read mrow_done on_done back_copied att_done mx_filled mneg_done mrow_filled p_done
            s_scores pv_done o_copied tok_filled back_filled att_filled rden_done gbc_done nx2_split lg_done
            gT_done gelu_done moe_added nx2_ready lg_filled gates_done gT_filled lgm_done ex8_done ew_split
            gbc_filled hid_filled hid_split down_done hid_gated hid_hi ew_split_hi moe_consts moe_copied
            moe_turned moe_pool_consts in_moe sw_split c_in_read c_u_read c_db_read c_dt_read bbc_done c_mixed
            c_in_filled xc_split c_db_filled c_u_filled dB_split c_dt_filled y1_split xc_ready bbc_filled
            decay_done drive_done delta_ready scanned y1_read summed hlast_done c_out_filled sel16_done x1_done
            in_sw f_a_done f_prod f_g_hi f_o_done f_added fw_split f_filled f_split f_turned f_hi fw_hi in_x
            in_win in_wg in_wo stored pool_order consts act_order a_ready dve_order consts_r
            """.split()}

        def C(name, j=0, w=1):
            return cols[:, COL[name] + j:COL[name] + j + w]

        def ln_stats_dve(o, dve, u, src, double=False, wait=True):
            for i in range(TPB):
                o.did(dve.bn_stats(ln_st[:, i, :], src[:, i, :]))
            o.wait()
            for i in range(TPB):
                o.did(dve.bn_aggr(ln_mv[:, i, :], ln_st[:, i, :]))
            o.wait()
            if double:
                o.did(dve.tensor_scalar(ln_ve[:, 1, :], ln_mv[:, :, 1], 1.0 + EPS, EPS * EPS, ALU.mult, ALU.add))
            dve.tensor_scalar(ln_ve[:, 0, :], ln_mv[:, :, 1], EPS, None, ALU.add).then_inc(S["ln_var"], 1)
            if wait:
                dve.wait_ge(S["ln_rstd"], u + 1)

        def ln_apply_dve(dve, u, src, dst, which):
            if u >= 1:
                dve.wait_ge(S["ln_turned"], u)
            for i in range(TPB):
                ins = dve.tensor_scalar(dst[:, i, :], src[:, i, :], ln_mv[:, i, 0:1], ln_rs[:, which, i:i + 1],
                                        ALU.subtract, ALU.mult)
            ins.then_inc(S["ln_xn"], 1)

        def ln_pool(pool, u, double=False):
            pool.wait_ge(S["ln_var"], u + 1)
            w = 2 if double else 1
            pool.tensor_tensor(ln_rs[:, 0:w, :], ln_ve[:, 0:w, :], mhalf[:, 0:TPB * w].rearrange("p (w i) -> p w i", w=w),
                               ALU.pow).then_inc(S["ln_rstd"], 1)

        def ln_pe(pe, u, out):
            pe.wait_ge(S["ln_xn"], u + 1)
            for i in range(TPB):
                ins = pe.transpose(out[:, i * P:(i + 1) * P], xn[:, i, :], ident[:, :])
            ins.then_inc(S["ln_turned"], 1)

        def mm3(pe, out, w, x, start=True, stop=True):
            pe.matmul(out, w[1], x[0], start=start, stop=False, skip_group_check=True)
            pe.matmul(out, w[0], x[1], start=False, stop=False, skip_group_check=True)
            return pe.matmul(out, w[0], x[0], start=False, stop=stop, skip_group_check=True)

        G = NB * TPB

        def mixer_parts(g):
            b, c = divmod(g, TPB)
            parts = [("end", b - 2, 4), ("front", b, 4)] if c == 0 else [("end", b - 2, 5)] if c == 1 else []
            parts += [("front", b + 1, c), ("end", b - 1, c)]
            return [(what, at, n) for what, at, n in parts if 0 <= at < NB and not (what == "front" and at == 0)]

        G_END = G + TPB + 2

        def mixer_fills(what, b, n):
            return {("front", 0): [("x", b, 0)], ("front", 1): [("pj", b, j) for j in range(4)],
                    ("front", 2): [("pj", b, j) for j in range(4, 9)],
                    ("end", 0): [("yt", b, 0), ("yt", b, 1)], ("end", 1): [("yb", b, 0), ("yb", b, 1)],
                    ("end", 3): [("gate", b, 0), ("gate", b, 1)], ("end", 4): [("out", b, 0)],
                    ("end", 5): [("mix", b, 0)]}.get((what, n), [])

        def mixer_emptied(kind, b, j):
            if kind == "pj":
                return (S["pj_act"], 7 * b + j + 1) if j < 7 else (S["pj_dve"], 2 * b + j - 6)
            return {"x": (S["xT_lo"], b + 1), "yt": (S["yn_done"], 2 * b + j + 1), "yb": (S["yg_done"], 2 * b + j + 1),
                    "gate": (S["sg_done"], 2 * b + j + 1), "out": (S["end_act"], 3 * b + 3),
                    "mix": (S["x_mixed"], b + 1)}[kind]

        ring = Fillings(bank[0:3], [name for n in range(5) for name in mixer_fills("front", 0, n)] +
                        [name for g in range(G_END) for part in mixer_parts(g) for name in mixer_fills(*part)], mixer_emptied)

        def front_pe(pe, b, part):
            if part == 0:
                ln_pe(pe, b, ring.take(pe, "x", b, 0))
            if part in (1, 2):
                pe.wait_ge(S["xT_hi"], b + 1)
                pe.wait_ge(S["xT_lo"], b + 1)
                if b == 0:
                    pe.wait_ge(S["w_split"], 2)
                for j in range(4) if part == 1 else range(4, 9):
                    out = ring.take(pe, "pj", b, j)
                    mm3(pe, out[:, :], [w[:, j, :] for w in win], [x[:, :] for x in xT]).then_inc(S["pj_filled"], 1)

        turn_a, turn_b = bank[3], bank[4]
        arg = [bank[5], bank[6]]
        ys_bank = bank[7]

        def chunk_front_pe(pe, g):
            b, c = divmod(g, TPB)
            cc = slice(c * P, (c + 1) * P)
            pe.wait_ge(S["dec_done"], b + 1)
            if g >= 1:
                pe.wait_ge(S["tok_dve"], 4 * g - 1)
            pe.transpose(turn_a[:, 0:P], dt[b % 2][:, cc], ident[:, :])
            pe.transpose(turn_a[:, P:2 * P], dtA[b % 2][:, cc], ident[:, :])
            pe.transpose(turn_a[:, 2 * P:3 * P], bdec[b % 2][:, cc], ident[:, :]).then_inc(S["turned"], 1)
            if g >= 1:
                pe.wait_ge(S["m_done"], g)
            pe.wait_ge(S["xs_ready"], 4 * b + 4)
            pe.transpose(turn_b[:, 0:P], xs[b % 2][:, 0, cc], ident[:, :])
            pe.transpose(turn_b[:, P:2 * P], xs[b % 2][:, 1, cc], ident[:, :])
            pe.matmul(turn_b[:, 2 * P:3 * P], xs[b % 2][0:NS0, 2, cc], xs[b % 2][0:NS0, 3, cc], start=True, stop=True).then_inc(S["turned"], 1)
            if g >= 1:
                pe.wait_ge(S["e_done"], g)
            pe.wait_ge(S["tok_dve"], 4 * g + 2)
            for half in range(2):
                hs = range(4 * half, 4 * half + 4)
                out = arg[half][:, :]
                for n, part in enumerate(dA_tok):
                    pe.matmul(out.rearrange("p (h t) -> p h t", h=4), negtri_r[:, :],
                              part[:, g % 2, 4 * half:4 * half + 4].unsqueeze(2).broadcast_to([P, 4, P]),
                              start=(n == 0), stop=False, skip_group_check=True)
                pe.matmul(out.rearrange("p (h t) -> p h t", h=4), identb[:, :],
                          maskneg[:, :].unsqueeze(1).broadcast_to([P, 4, P]), start=False, stop=False, skip_group_check=True)
                for h in hs:
                    for n, part in enumerate(dA_tok):
                        ins = pe.matmul(out[:, (h % 4) * P:(h % 4 + 1) * P], part[:, g % 2, h:h + 1].broadcast_to([P, P]),
                                        tri_r[:, :], start=False, stop=(n == 1), skip_group_check=True)
            ins.then_inc(S["arg_filled"], 1)

        def chunk_back_pe(pe, g):
            b, c = divmod(g, TPB)
            cc = slice(c * P, (c + 1) * P)
            pe.wait_ge(S["m_done"], g + 1)
            if g >= 1:
                pe.wait_ge(S["y_done"], g)
            for half in range(2):
                for q in range(4):
                    h = 4 * half + q
                    pe.matmul(ys_bank[q * HD0:(q + 1) * HD0, half * P:(half + 1) * P], xdt[:, g % 2, h, :],
                              mdec[:, g % 2, h, :], start=(half == 0), stop=False, skip_group_check=True)
            pe.wait_ge(S["state_done"], g + 1)
            for half in range(2):
                ins = pe.matmul(ys_bank[:, half * P:(half + 1) * P], state[:, g % 2, half * P:(half + 1) * P],
                                cdec[b % 2][:, cc], start=False, stop=True, skip_group_check=True)
            pe.matmul(ys_bank[:, 2 * P:4 * P], bd_tok[:, g % 2, :], xdt[:, g % 2, :, :].rearrange("p h d -> p (h d)"),
                      start=True, stop=True).then_inc(S["s_filled"], 1)

        def end_pe(pe, b, part):
            if part == 0:
                pe.wait_ge(S["y_done"], TPB * (b + 1))
                for pair in range(2):
                    out = ring.take(pe, "yt", b, pair)
                    for i in range(2):
                        for half in range(2):
                            ins = pe.transpose(out[:, (2 * i + half) * P:(2 * i + half + 1) * P],
                                               y_fm[b % 2][:, half, (2 * pair + i) * P:(2 * pair + i + 1) * P], ident[:, :])
                    ins.then_inc(S["yt_filled"], 1)
            elif part == 1:
                pe.wait_ge(S["yn_done"], 2 * b + 2)
                for half in range(2):
                    out = ring.take(pe, "yb", b, half)
                    for i in range(TPB):
                        ins = pe.transpose(out[:, i * P:(i + 1) * P], yn[:, i, half * P:(half + 1) * P], ident[:, :])
                    ins.then_inc(S["yb_filled"], 1)
            elif part == 3:
                pe.wait_ge(S["yg_split"], b + 1)
                if b == 0:
                    pe.wait_ge(S["w_split"], 4)
                for m in range(2):
                    out = ring.take(pe, "gate", b, m)
                    for k in range(2):
                        ins = mm3(pe, out[:, :], [w[:, 2 * k + m, :] for w in wgo], [y[:, k, :] for y in ygs],
                                  start=(k == 0), stop=(k == 1))
                    ins.then_inc(S["gate_filled"], 1)
            elif part == 4:
                pe.wait_ge(S["skip_split"], b + 1)
                pe.wait_ge(S["gy_split"], b + 1)
                out = ring.take(pe, "out", b, 0)
                for k in range(4):
                    act = [x[:, b % 2, k, :] for x in cat] if k < 2 else [x[:, k - 2, :] for x in gy]
                    ins = mm3(pe, out[:, :], [w[:, 4 + k, :] for w in wgo], act, start=(k == 0), stop=(k == 3))
                ins.then_inc(S["out_filled"], 1)
            elif part == 5:
                out = ring.take(pe, "mix", b, 0)
                pe.wait_ge(S["end_act"], 3 * b + 3)
                for i in range(TPB):
                    ins = pe.transpose(out[:, i * P:(i + 1) * P], dte[:, i * P:(i + 1) * P], ident[:, :])
                ins.then_inc(S["out_filled"], 1)

        CONV_ORDER = (2, 3, 0, 1)

        def front_act(o, act, b, part):
            def pj(j):
                act.wait_ge(S["pj_filled"], 9 * b + j + 1)
                return ring.bank("pj", b, j)[:, :]

            if part == 0:
                act.wait_ge(S["ln_turned"], b + 1)
                if b >= 1:
                    act.wait_ge(S["pj_filled"], 9 * b)
                act.activation(xT[0][:, :], ring.bank("x", b, 0)[:, :], ACT.Copy).then_inc(S["xT_hi"], 1)
            elif part == 1:
                act.wait_ge(S["conv_hist"], b + 1)
                for j in (XA, XB, BREP, CREP):
                    act.activation(convin[:, j, CONV - 1:], pj(j), ACT.Copy).then_inc(S["pj_act"], 1)
            elif part == 2:
                if b >= 1:
                    act.wait_ge(S["dt_done"], b)
                act.activation(dtv[:, :], pj(DTREP), ACT.Identity, bias=C("dt_bias")).then_inc(S["pj_act"], 1)
                if b >= 1:
                    act.wait_ge(S["pj_dve"], 2 * b)
                for n, j in enumerate((Z0A, Z0B)):
                    act.activation(sz[:, n, :], pj(j), ACT.Silu).then_inc(S["pj_act"], 1)
                act.wait_ge(S["pj_act"], 7 * b + 5)
                o.did(act.activation(dta[:, :], dtv[:, :], ACT.Abs))
                o.wait()
                if b >= 3:
                    act.wait_ge(S["out_filled"], 2 * (b - 3) + 2)
                o.did(act.activation(dte[:, :], dta[:, :], ACT.Exp, scale=-1.0))
                o.wait()
                act.activation(dta[:, :], dte[:, :], ACT.Ln, bias=one[:, 0:1]).then_inc(S["dt_lnd"], 1)
            elif part == 3:
                if b >= 2:
                    act.wait_ge(S["state_done"], TPB * (b - 1) + 1)
                act.wait_ge(S["cs_done"], b + 1)
                if b >= 1:
                    act.wait_ge(S["dec_done"], b)
                act.activation(ecs[b % 2][:, :], cs[:, :], ACT.Exp).then_inc(S["ecs_done"], 1)
                for c in range(TPB):
                    cc = slice(c * P, (c + 1) * P)
                    ins = act.activation(eb[:, cc], cs[:, cc], ACT.Exp, scale=-1.0, bias=cs[:, (c + 1) * P - 1:(c + 1) * P])
                ins.then_inc(S["eb_done"], 1)
                for n, j in enumerate(CONV_ORDER):
                    act.wait_ge(S["conv_done"], 4 * b + n + 1)
                    act.activation(xs[b % 2][:, j, :], cacc[:, j, :], ACT.Silu, bias=C("conv0_b", j)).then_inc(S["xs_ready"], 1)
            elif part == 4:
                if b >= 2:
                    act.wait_ge(S["out_filled"], 2 * (b - 2) + 1)
                act.wait_ge(S["pj_dve"], 2 * b + 2)
                act.activation(cat[0][:, b % 2, :, :], skip[:, :, :], ACT.Copy).then_inc(S["skip_done"], 1)

        def chunk_act(act, g):
            act.wait_ge(S["arg_filled"], g + 1)
            if g >= 2:
                act.wait_ge(S["m_done"], g - 1)
            act.activation(edec[:, g % 2, 0:4, :], arg[0][:, :].rearrange("p (h t) -> p h t", h=4), ACT.Exp)
            act.activation(edec[:, g % 2, 4:8, :], arg[1][:, :].rearrange("p (h t) -> p h t", h=4), ACT.Exp).then_inc(S["e_done"], 1)

        def end_act(act, b, part):
            if part == 1:
                if b >= 1:
                    act.wait_ge(S["gy_split"], b)
                for half in range(2):
                    act.wait_ge(S["yb_filled"], 2 * b + half + 1)
                    act.activation(yg[:, half, :], ring.bank("yb", b, half)[:, :], ACT.Identity,
                                   scale=C("gamma", half), bias=C("beta", half)).then_inc(S["yg_done"], 1)
                act.wait_ge(S["yg_done"], 2 * b + 2)
                act.activation(ygs[0][:, :, :], yg[:, :, :], ACT.Copy).then_inc(S["end_act"], 1)
            elif part == 3:
                for m in range(2):
                    act.wait_ge(S["gate_filled"], 2 * b + m + 1)
                    act.activation(sg[:, m, :], ring.bank("gate", b, m)[:, :], ACT.Sigmoid,
                                   bias=C("b_gate", m)).then_inc(S["sg_done"], 1)
                act.wait_ge(S["y2_done"], b + 1)
                if b >= 1:
                    act.wait_ge(S["out_filled"], 2 * (b - 1) + 1)
                act.activation(gy[0][:, :, :], y2[:, :, :], ACT.Copy).then_inc(S["end_act"], 1)
            elif part == 4:
                act.wait_ge(S["dt_lnd"], min(b + 3, NB))
                act.wait_ge(S["out_filled"], 2 * b + 1)
                act.activation(dte[:, :], ring.bank("out", b, 0)[:, :], ACT.Copy).then_inc(S["end_act"], 1)

        def lo_part(dve, out, value, hi):
            return dve.tensor_tensor(out, value, hi.bitcast(F32), ALU.subtract)

        conv0_at = {}

        def conv0_dve(o, dve, b, taps):
            for k in taps:
                for j in CONV_ORDER:
                    w = C("conv0_w", CONV * j + k)
                    if k == 0:
                        dve.wait_ge(S["pj_act"], 7 * b + j + 1)
                        conv0_at[j] = o.did(dve.tensor_scalar(cacc[:, j, :], convin[:, j, 0:BLK], w, None, ALU.mult))
                        continue
                    o.wait(conv0_at[j])
                    ins = dve.scalar_tensor_tensor(cacc[:, j, :], convin[:, j, k:k + BLK], w, cacc[:, j, :], ALU.mult, ALU.add)
                    if k < CONV - 1:
                        conv0_at[j] = o.did(ins)
                    else:
                        ins.then_inc(S["conv_done"], 1)

        def front_early_dve(o, dve, b, part):
            if part == 0:
                src = x_tok[:, b * TPB:(b + 1) * TPB, :]
                ln_stats_dve(o, dve, b, src)
                ln_apply_dve(dve, b, src, xn, 0)
            elif part == 2:
                dve.wait_ge(S["conv_hist"], b + 1)
                if b >= 1:
                    dve.wait_ge(S["xs_ready"], 4 * b)
                conv0_dve(o, dve, b, (0, 1))
            elif part == 3:
                dve.wait_ge(S["dt_lnd"], b + 1)
                o.did(dve.scalar_tensor_tensor(dt[b % 2][:, :], dtv[:, :], 0.0, dta[:, :], ALU.max, ALU.add))
                o.wait()
                dve.tensor_scalar(dtA[b % 2][:, :], dt[b % 2][:, :], a_neg[:, 0:1], None, ALU.mult).then_inc(S["dt_done"], 1)
                dve.wait_ge(S["dt_done"], b + 1)
                for c in range(TPB):
                    cc = slice(c * P, (c + 1) * P)
                    ins = dve.tensor_tensor_scan(cs[:, cc], one[:, 0:1].broadcast_to([P, P]), dtA[b % 2][:, cc], 0.0,
                                                 ALU.mult, ALU.add)
                ins.then_inc(S["cs_done"], 1)
                conv0_dve(o, dve, b, (2, 3))

        def front_late_dve(o, dve, b, part):
            if part == 0:
                dve.wait_ge(S["xT_hi"], b + 1)
                lo_part(dve, xT[1][:, :], ring.bank("x", b, 0)[:, :], xT[0][:, :]).then_inc(S["xT_lo"], 1)
                if b == 0:
                    dve.memset(convin[:, :, 0:CONV - 1], 0.0).then_inc(S["conv_hist"], 1)
                else:
                    dve.tensor_copy(convin[:, :, 0:CONV - 1], convin[:, :, BLK:BLK + CONV - 1]).then_inc(S["conv_hist"], 1)
            elif part == 2:
                if b >= 1:
                    dve.wait_ge(S["skip_split"], b)
                for n in range(2):
                    dve.wait_ge(S["pj_filled"], 9 * b + X0A + n + 1)
                    dve.wait_ge(S["pj_act"], 7 * b + 6 + n)
                    dve.tensor_tensor(skip[:, n, :], ring.bank("pj", b, X0A + n)[:, :], sz[:, n, :], ALU.mult).then_inc(S["pj_dve"], 1)

        def front_pool(o, pool, b, part):
            if part == 0:
                ln_pool(pool, b)
            elif part == 3:
                if b >= 2:
                    pool.wait_ge(S["state_done"], TPB * (b - 1) + 1)
                pool.wait_ge(S["xs_ready"], 4 * b + 2)
                pool.wait_ge(S["eb_done"], b + 1)
                o.did(pool.tensor_tensor(bdec[b % 2][:, :], xs[b % 2][:, 2, :], eb[:, :], ALU.mult))
                pool.tensor_tensor(cdec[b % 2][:, :], xs[b % 2][:, 3, :], ecs[b % 2][:, :], ALU.mult).then_inc(S["dec_done"], 1)
            elif part == 4:
                pool.wait_ge(S["skip_done"], b + 1)
                lo_part(pool, cat[1][:, b % 2, :, :], skip[:, :, :], cat[0][:, b % 2, :, :]).then_inc(S["skip_split"], 1)

        def end_pool(o, pool, b, part):
            if part == 1:
                pool.wait_ge(S["y_var"], b + 1)
                pool.tensor_tensor(ln_rs[:, 0, :], ln_ve[:, 0, :], mhalf[:, 0:TPB], ALU.pow).then_inc(S["y_rstd"], 1)
            elif part == 2:
                pool.wait_ge(S["end_act"], 3 * b + 1)
                lo_part(pool, ygs[1][:, :, :], yg[:, :, :], ygs[0][:, :, :]).then_inc(S["yg_split"], 1)
            elif part == 3:
                pool.wait_ge(S["sg_done"], 2 * b + 2)
                pool.tensor_tensor(y2[:, :, :], sg[:, :, :], yg[:, :, :], ALU.mult).then_inc(S["y2_done"], 1)
            elif part == 4:
                pool.wait_ge(S["end_act"], 3 * b + 2)
                lo_part(pool, gy[1][:, :, :], y2[:, :, :], gy[0][:, :, :]).then_inc(S["gy_split"], 1)

        def chunk_front_dve(dve, g):
            s = g % 2
            dve.wait_ge(S["turned"], 2 * g + 1)
            if g >= 2:
                dve.wait_ge(S["s_filled"], g - 1)
            dve.tensor_copy(dt_tok[:, s, :], turn_a[:, 0:P:NS0]).then_inc(S["tok_dve"], 1)
            dve.tensor_copy(dA_tok[0][:, s, :], turn_a[:, P:2 * P:NS0]).then_inc(S["dA_hi"], 1)
            dve.wait_ge(S["dA_hi"], g + 1)
            lo_part(dve, dA_tok[1][:, s, :], turn_a[:, P:2 * P:NS0], dA_tok[0][:, s, :]).then_inc(S["tok_dve"], 1)
            dve.tensor_copy(bd_tok[:, s, :], turn_a[:, 2 * P:3 * P]).then_inc(S["tok_dve"], 1)
            dve.wait_ge(S["turned"], 2 * g + 2)
            dve.tensor_tensor(xdt[:, s, :, :], turn_b[:, 0:2 * P].rearrange("p (h d) -> p h d", h=H0),
                              dt_tok[:, s, :].unsqueeze(2).broadcast_to([P, H0, HD0]), ALU.mult).then_inc(S["tok_dve"], 1)

        def chunk_mid_dve(dve, g):
            s = g % 2
            dve.wait_ge(S["e_done"], g + 1)
            dve.tensor_tensor(mdec[:, s, :, :], edec[:, s, :, :], turn_b[:, 2 * P:3 * P].unsqueeze(1).broadcast_to([P, H0, P]),
                              ALU.mult).then_inc(S["m_done"], 1)

        def chunk_back_dve(o, dve, g):
            b, c = divmod(g, TPB)
            cc = slice(c * P, (c + 1) * P)
            if b >= 2 and c == 0:
                dve.wait_ge(S["yt_filled"], 2 * b - 2)
            dve.wait_ge(S["s_filled"], g + 1)
            for half in range(2):
                ins = dve.scalar_tensor_tensor(y_fm[b % 2][:, half, cc], xs[b % 2][:, half, cc], C("d0", half),
                                               ys_bank[:, half * P:(half + 1) * P], ALU.mult, ALU.add)
            dve.tensor_tensor(stmp[:, :], ys_bank[:, 2 * P:4 * P], headmask[:, :, :].rearrange("p h d -> p (h d)"),
                              ALU.mult).then_inc(S["y_done"], 1)
            dve.wait_ge(S["y_done"], g + 1)
            dve.scalar_tensor_tensor(state[:, (g + 1) % 2, :], state[:, g % 2, :], ecs[b % 2][:, (c + 1) * P - 1:(c + 1) * P],
                                     stmp[:, :], ALU.mult, ALU.add).then_inc(S["state_done"], 1)

        def end_early_dve(o, dve, b, part):
            if part != 1:
                return
            for i in range(TPB):
                dve.wait_ge(S["yt_filled"], 2 * b + i // 2 + 1)
                src = ring.bank("yt", b, i // 2)[:, (i % 2) * DI:(i % 2 + 1) * DI]
                o.did(dve.bn_stats(yst[:, i, :], src))
            o.wait()
            for i in range(TPB):
                o.did(dve.bn_aggr(ymv[:, i, :], yst[:, i, :]))
            o.wait()
            dve.tensor_scalar(ln_ve[:, 0, :], ymv[:, :, 1], EPS, None, ALU.add).then_inc(S["y_var"], 1)
            dve.wait_ge(S["y_rstd"], b + 1)
            if b >= 1:
                dve.wait_ge(S["yb_filled"], 2 * b)
            for i in range(TPB):
                src = ring.bank("yt", b, i // 2)[:, (i % 2) * DI:(i % 2 + 1) * DI]
                ins = dve.tensor_scalar(yn[:, i, :], src, ymv[:, i, 0:1], ln_rs[:, 0, i:i + 1], ALU.subtract, ALU.mult)
                if i % 2:
                    ins.then_inc(S["yn_done"], 1)

        def end_late_dve(o, dve, b, part):
            if part == 5:
                dve.wait_ge(S["out_filled"], 2 * b + 2)
                xb = x_tok[:, b * TPB:(b + 1) * TPB, :]
                dve.tensor_tensor(xb, ring.bank("mix", b, 0)[:, :].rearrange("p (i d) -> p i d", i=TPB), xb,
                                  ALU.add).then_inc(S["x_mixed"], 1)

        SCALE = HDA ** -0.5
        part_dram = nc.dram_tensor("qk_part_rows", (2, 3, P, T), BF16, kind="Internal").ap()
        Q_ROWS, K_ROWS = (0, 0, 1, 1, 0, 2), (0, 1, 0, 1, 2, 0)
        M_ROW = len(Q_ROWS) * HDA
        m_loaded = [sem(f"m_loaded{n}") for n in range(4)]
        ITEMS = [(b, grp) for b in range(NB) for grp in range(4)]

        def units(k):
            b, grp = ITEMS[k]
            return [(b, 4 * grp + hh, i, c) for hh in range(4) for i in range(TPB) for c in range(b + 1)]

        unit_base = [0]
        for k in range(16):
            unit_base.append(unit_base[-1] + len(units(k)))

        def unit_share(k, step):
            steps = 2 * (ITEMS[k][0] + 1)
            if k + 2 >= len(ITEMS):
                return []
            n = len(units(k + 2))
            return list(range(n * step // steps, n * (step + 1) // steps))

        parts_loaded = [sem("parts_loaded_even"), sem("parts_loaded_odd")]

        def qkv_pe(pe, b):
            u = NB + b
            if b >= 1:
                pe.wait_ge(S["nx_ready"], b)
            ln_pe(pe, u, bank[0])
            pe.wait_ge(S["nx_split"], 2 * b + 2)
            if b == 0:
                pe.wait_ge(S["qkv_split"], 2)
            for j in range(2):
                if b >= 1:
                    pe.wait_ge(S["qk_evac"], 2 * b - 1 + j)
                mm3(pe, bank[1 + j][:, :], [w[:, j, :] for w in wqkv], [x[:, :] for x in nxs]).then_inc(S["qk_filled"], 1)
            if b >= 1:
                pe.wait_ge(S["v_done"], b)
            for i in range(TPB):
                tt = slice(i * P, (i + 1) * P)
                ins = mm3(pe, bank[3][:, tt], [x[:, tt] for x in nxs], [w[:, 2, :] for w in wqkv], start=(i == 0))
            ins.then_inc(S["v_filled"], 1)

        def qkv_act(act, b):
            act.wait_ge(S["ln_turned"], NB + b + 1)
            if b >= 1:
                act.wait_ge(S["nx_split"], 2 * b)
            act.activation(nx[:, :], bank[0][:, :], ACT.Identity, scale=C("ln1_w"), bias=C("ln1_b")).then_inc(S["nx_ready"], 1)
            for j, bias in enumerate(("bq", "bk")):
                act.wait_ge(S["qk_filled"], 2 * b + j + 1)
                if b >= 1:
                    act.wait_ge(S["parts_done"], 8 * b)
                act.activation(qk_f[:, j, :], bank[1 + j][:, :], ACT.Identity, bias=C(bias)).then_inc(S["qk_evac"], 1)

        def qkv_dve(o, dve, b):
            u = NB + b
            src = x_tok[:, b * TPB:(b + 1) * TPB, :]
            dst = inner[:, b * TPB:(b + 1) * TPB, :]
            ln_stats_dve(o, dve, u, src, double=True)
            for i in range(TPB):
                ins = dve.tensor_scalar(dst[:, i, :], src[:, i, :], ln_mv[:, i, 0:1], ln_rs[:, 0, i:i + 1],
                                        ALU.subtract, ALU.mult)
            ins.then_inc(S["inner_ready"], 1)
            ln_apply_dve(dve, u, src, xn, 1)
            dve.wait_ge(S["nx_ready"], b + 1)
            if b >= 1:
                dve.wait_ge(S["v_filled"], b)
            dve.tensor_copy(nxs[0][:, :], nx[:, :]).then_inc(S["nx_split"], 1)
            dve.wait_ge(S["nx_split"], 2 * b + 1)
            lo_part(dve, nxs[1][:, :], nx[:, :], nxs[0][:, :]).then_inc(S["nx_split"], 1)
            if b >= 1:
                dve.wait_ge(S["parts_saved"], 16 * 2 * b)
            for j in range(2):
                dve.wait_ge(S["qk_evac"], 2 * b + j + 1)
                dve.tensor_copy(qk_parts[:, j, 0, :], qk_f[:, j, :]).then_inc(S["parts_done"], 1)
            for j in range(2):
                dve.wait_ge(S["parts_done"], 8 * b + j + 1)
                dve.tensor_tensor(qk_r[:, j, :], qk_f[:, j, :], qk_parts[:, j, 0, :], ALU.subtract).then_inc(S["parts_done"], 1)
            for j in range(2):
                dve.wait_ge(S["parts_done"], 8 * b + j + 3)
                dve.tensor_copy(qk_parts[:, j, 1, :], qk_r[:, j, :]).then_inc(S["parts_done"], 1)
            for j in range(2):
                dve.wait_ge(S["parts_done"], 8 * b + j + 5)
                dve.tensor_tensor(qk_parts[:, j, 2, :], qk_r[:, j, :], qk_parts[:, j, 1, :], ALU.subtract).then_inc(S["parts_done"], 1)
            dve.wait_ge(S["v_filled"], b + 1)
            dve.wait_ge(S["v_ones"], 1)
            v_out = v9[:, b * TPB * VW:(b + 1) * TPB * VW].rearrange("p (i h e) -> p i h e", i=TPB, e=HDA + 1)[:, :, :, 0:HDA]
            dve.tensor_tensor(v_out, bank[3][:, :].rearrange("p (i h e) -> p i h e", i=TPB, e=HDA),
                              bv[:, :].rearrange("p (h e) -> p h e", e=HDA).unsqueeze(1).broadcast_to([P, TPB, HA, HDA]),
                              ALU.add).then_inc(S["v_done"], 1)

        def qkv_sp(sp, b):
            tt = slice(b * BLK, (b + 1) * BLK)
            for j in range(2):
                sp.wait_ge(S["parts_done"], 8 * b + j + 7)
                sp.dma_start(part_dram[j][:, :, tt].rearrange("n p t -> p n t"), qk_parts[:, j, :, :]).then_inc(S["parts_saved"], 16)
            sp.wait_ge(S["parts_saved"], 32 * (b + 1))
            if b == 0:
                sp.wait_ge(S["qk_cleared"], 2)
                sp.wait_ge(S["bo_added"], 1)
            if b >= 2:
                sp.wait_ge(parts_loaded[b % 2], 24 * 16 * (b // 2))
            for j, (rows, dst) in enumerate(((Q_ROWS, qa), (K_ROWS, kz))):
                for par in range(2):
                    for g, n in enumerate(rows):
                        r0 = 64 * par + g * HDA
                        out = dst[r0:r0 + HDA, :, tt] if j == 0 else dst[r0:r0 + HDA, par::2, tt]
                        src = part_dram[j, n].rearrange("(pair par e) t -> par e pair t", par=2, e=HDA)[par][:, :, tt]
                        sp.dma_start(out, src).then_inc(parts_loaded[b % 2], 16)

        ring_m = [bank[4], bank[5], bank[6]]
        fill_at, fills = {}, []

        def plan(name):
            fill_at[name] = len(fills)
            fills.append(name)

        def plan_item_maxima(k, lo, hi):
            for n in range(lo, hi):
                plan(("mx", k, n))

        def plan_tail(k):
            plan(("tok", k))
            if k % 4 == 3:
                plan(("back", k // 4))
                plan(("att", k // 4))

        for k in range(2):
            plan_item_maxima(k, 0, len(units(k)))
            plan(("mrow", k))
        for k in range(16):
            for step in range(2 * (ITEMS[k][0] + 1)):
                for n in unit_share(k, step):
                    plan(("mx", k + 2, n))
                if step == 0 and 2 <= k + 1 < 16:
                    plan(("mrow", k + 1))
                if step == 1 and k >= 1:
                    plan_tail(k - 1)
        plan_tail(15)

        def fill_bank(*name):
            return ring_m[fill_at[name] % 3]

        def emptied(name):
            kind = name[0]
            if kind == "mx":
                return (S["mx_read"], unit_base[name[1]] + name[2] + 1)
            if kind == "mrow":
                return (S["mrow_done"], 2 * name[1] + 2)
            return {"tok": (S["on_done"], name[1] + 1), "back": (S["back_copied"], name[1] + 1),
                    "att": (S["att_done"], name[1] + 1)}[kind]

        def take(pe, *name):
            n = fill_at[name]
            if n >= 3:
                pe.wait_ge(*emptied(fills[n - 3]))
            return ring_m[n % 3]

        def mx_pe(pe, k, n):
            b, h, i, c = units(k)[n]
            if n == 0 and k % 4 == 0:
                pe.wait_ge(parts_loaded[b % 2], 24 * 16 * (b // 2 + 1))
            out = take(pe, "mx", k, n)
            q0 = b * BLK + i * P
            w = BLK if c < b else (i + 1) * P
            last = c == b
            ins = pe.matmul(out[:, 0:w], qa[:, h // 2, q0:q0 + P], kz[:, h, c * BLK:c * BLK + w], start=True, stop=not last,
                            skip_group_check=True)
            if last:
                ins = pe.matmul(out[:, w - P:w], maskneg[:, :], identb[:, :], start=False, stop=True, skip_group_check=True)
            ins.then_inc(S["mx_filled"], 1)

        def mx_dve(dve, k, n):
            b, h, i, c = units(k)[n]
            w = BLK if c < b else (i + 1) * P
            dve.wait_ge(S["mx_filled"], unit_base[k] + n + 1)
            if n == 0 and k >= 1:
                dve.wait_ge(S["mneg_done"], 2 * k)
            dve.tensor_reduce(mx[:, 4 * i + h % 4, c:c + 1], fill_bank("mx", k, n)[:, 0:w], AX.X, ALU.max).then_inc(S["mx_read"], 1)

        def mneg_dve(o, dve, k):
            b = ITEMS[k][0]
            dve.wait_ge(S["mx_read"], unit_base[k + 1])
            if k >= 2:
                dve.wait_ge(S["mrow_filled"], k - 1)
            dve.tensor_reduce(mneg[:, k % 2, :], mx[:, :, 0:b + 1], AX.X, ALU.max).then_inc(S["mneg_done"], 1)
            dve.wait_ge(S["mneg_done"], 2 * k + 1)
            dve.tensor_scalar(mneg[:, k % 2, :], mneg[:, k % 2, :], -1.0, None, ALU.mult).then_inc(S["mneg_done"], 1)

        def mrow_pe(pe, k):
            out = take(pe, "mrow", k)
            pe.wait_ge(S["mneg_done"], 2 * k + 2)
            for i in range(TPB):
                ins = pe.transpose(out[0:4, i * P:(i + 1) * P], mneg[:, k % 2, 4 * i:4 * i + 4], ident[:, :])
            ins.then_inc(S["mrow_filled"], 1)

        def mrow_dve(dve, k):
            dve.wait_ge(S["mrow_filled"], k + 1)
            if k >= 2:
                dve.wait_ge(m_loaded[(k - 2) % 4], 8 * 16 * ((k - 2) // 4 + 1))
            src = fill_bank("mrow", k)[0:4, :]
            dve.tensor_copy(mrow[:, k % 2, 0, :], src).then_inc(S["mrow_done"], 1)
            dve.wait_ge(S["mrow_done"], 2 * k + 1)
            dve.tensor_tensor(mrow[:, k % 2, 1, :], src, mrow[:, k % 2, 0, :], ALU.subtract).then_inc(S["mrow_done"], 1)

        def mrow_sp(sp, k):
            b, grp = ITEMS[k]
            sp.wait_ge(S["mrow_done"], 2 * k + 2)
            for hh in range(4):
                h = 4 * grp + hh
                for n in range(2):
                    r = 64 * (h % 2) + M_ROW + n
                    sp.dma_start(qa[r:r + 1, h // 2, b * BLK:(b + 1) * BLK], mrow[hh:hh + 1, k % 2, n, :]).then_inc(m_loaded[k % 4], 16)

        step_base = [0]
        for b, _ in ITEMS:
            step_base.append(step_base[-1] + 2 * (b + 1))

        def q_lo(b, kt):
            r = max(0, kt - TPB * b)
            return r * P, r // 2 * 2 * P

        def scores_pe(pe, k, kp, hh):
            b, grp = ITEMS[k]
            h = 4 * grp + hh
            n = 4 * (step_base[k] + kp) + hh
            if n >= 2:
                pe.wait_ge(S["p_done"], n - 1)
            for j in range(2):
                kt = 2 * kp + j
                own, lo = q_lo(b, kt)
                out = bank[2 * (n % 2) + j]
                diag = kt >= TPB * b
                ins = pe.matmul(out[:, lo:], kz[:, h, kt * P:(kt + 1) * P], qa[:, h // 2, b * BLK + lo:(b + 1) * BLK],
                                start=True, stop=not diag, skip_group_check=True)
                if diag:
                    ins = pe.matmul(out[:, own:own + P], identb[:, :], maskneg[:, :], start=False, stop=True, skip_group_check=True)
            ins.then_inc(S["s_scores"], 1)

        def probs_act(act, k, kp, hh):
            b, grp = ITEMS[k]
            n = 4 * (step_base[k] + kp) + hh
            st = step_base[k] + kp
            act.wait_ge(S["s_scores"], n + 1)
            if st >= 2 and hh == 0:
                act.wait_ge(S["pv_done"], st - 1)
            _, lo = q_lo(b, 2 * kp)
            act.activation(probs[:, st % 2, hh, :, lo:], s_pair[n % 2][:, :, lo:], ACT.Exp, scale=SCALE).then_inc(S["p_done"], 1)

        def values_pe(pe, k, kp, j):
            b, grp = ITEMS[k]
            st = step_base[k] + kp
            pe.wait_ge(S["p_done"], 4 * st + 4)
            if kp == 0 and j == 0 and k >= 1:
                pe.wait_ge(S["o_copied"], k)
            out = bank[7]
            kt = 2 * kp + j
            own, _ = q_lo(b, kt)
            for hh in range(4):
                at = kt * VW + (4 * grp + hh) * (HDA + 1)
                ins = pe.matmul(out[32 * hh:32 * hh + 32, own:], v9[:, at:at + 32], probs[:, st % 2, hh, j, own:],
                                start=(kt == 0), stop=(kt == TPB * (b + 1) - 1), skip_group_check=True)
            if j == 1:
                ins.then_inc(S["pv_done"], 1)

        def tail_pe(pe, k):
            b, grp = ITEMS[k]
            out = take(pe, "tok", k)
            pe.wait_ge(S["o_copied"], k + 1)
            for i in range(TPB):
                ins = pe.transpose(out[:, i * P:(i + 1) * P], o_sb[:, i * P:(i + 1) * P], ident[:, :])
            ins.then_inc(S["tok_filled"], 1)
            if grp == 3:
                out = take(pe, "back", b)
                pe.wait_ge(S["on_done"], 4 * b + 4)
                for i in range(TPB):
                    ins = pe.transpose(out[:, i * P:(i + 1) * P], o_tok[:, i, :], ident[:, :])
                ins.then_inc(S["back_filled"], 1)
                out = take(pe, "att", b)
                pe.wait_ge(S["back_copied"], b + 1)
                for i in range(TPB):
                    tt = slice(i * P, (i + 1) * P)
                    ins = pe.matmul(out[:, tt], o_fm[:, tt], wo[:, :], start=True, stop=True)
                ins.then_inc(S["att_filled"], 1)

        def first_maxima_pe(pe, k):
            for n in range(len(units(k))):
                mx_pe(pe, k, n)
            mrow_pe(pe, k)

        def attention_pe(pe):
            for k, (b, grp) in enumerate(ITEMS):
                steps = 2 * (b + 1)
                pe.wait_ge(m_loaded[k % 4], 8 * 16 * (k // 4 + 1))
                for step in range(steps):
                    for hh in range(4):
                        scores_pe(pe, k, step, hh)
                        share = unit_share(k, step)
                        for n in share[len(share) * hh // 4:len(share) * (hh + 1) // 4]:
                            mx_pe(pe, k + 2, n)
                        if step and hh % 2:
                            values_pe(pe, k, step - 1, hh // 2)
                        elif k >= 1 and hh % 2:
                            values_pe(pe, k - 1, 2 * ITEMS[k - 1][0] + 1, hh // 2)
                    if step == 0 and 2 <= k + 1 < 16:
                        mrow_pe(pe, k + 1)
                    if step == 1 and k >= 1:
                        tail_pe(pe, k - 1)
            for j in range(2):
                values_pe(pe, 15, 2 * NB - 1, j)
            tail_pe(pe, 15)

        def o_copy_act(act, k):
            act.wait_ge(S["pv_done"], step_base[k + 1])
            if k >= 1:
                act.wait_ge(S["tok_filled"], k)
            act.activation(o_sb[:, :], bank[7][:, :], ACT.Copy).then_inc(S["o_copied"], 1)

        def attention_act(act):
            for k, (b, grp) in enumerate(ITEMS):
                for kp in range(2 * (b + 1)):
                    for hh in range(4):
                        probs_act(act, k, kp, hh)
                    if kp == 0 and k >= 1:
                        o_copy_act(act, k - 1)
            o_copy_act(act, 15)

        def tail_dve(o, dve, k):
            b, grp = ITEMS[k]
            dve.wait_ge(S["tok_filled"], k + 1)
            if grp == 0 and b >= 1:
                dve.wait_ge(S["back_filled"], b)
            tok = fill_bank("tok", k)[:, :].rearrange("p (i h e) -> p i h e", i=TPB, h=4)
            if k >= 2:
                dve.wait_ge(S["on_done"], k - 1)
            dve.reciprocal(rden[:, k % 2, :, :, :], tok[:, :, :, HDA:HDA + 1]).then_inc(S["rden_done"], 1)
            dve.wait_ge(S["rden_done"], k + 1)
            dst = o_tok[:, :, 4 * grp * HDA:4 * (grp + 1) * HDA].rearrange("p i (h e) -> p i h e", h=4)
            dve.tensor_tensor(dst, tok[:, :, :, 0:HDA], rden[:, k % 2, :, :, :].broadcast_to([P, TPB, 4, HDA]),
                              ALU.mult).then_inc(S["on_done"], 1)
            if grp == 3:
                dve.wait_ge(S["back_filled"], b + 1)
                dve.tensor_copy(o_fm[:, :], fill_bank("back", b)[:, :]).then_inc(S["back_copied"], 1)
                dve.wait_ge(S["att_filled"], b + 1)
                ib = inner[:, b * TPB:(b + 1) * TPB, :]
                dve.tensor_tensor(ib, fill_bank("att", b)[:, :].rearrange("p (i d) -> p i d", i=TPB), ib,
                                  ALU.add).then_inc(S["att_done"], 1)

        def first_maxima_dve(o, dve, k):
            for n in range(len(units(k))):
                mx_dve(dve, k, n)
            mneg_dve(o, dve, k)
            mrow_dve(dve, k)

        def attention_dve(o, dve):
            for k in range(16):
                for step in range(2 * (ITEMS[k][0] + 1)):
                    for n in unit_share(k, step):
                        mx_dve(dve, k + 2, n)
                    if step == 0 and 2 <= k + 1 < 16:
                        mrow_dve(dve, k + 1)
                    if step == 1 and k >= 1:
                        tail_dve(o, dve, k - 1)
                if k + 2 < 16:
                    mneg_dve(o, dve, k + 2)
            route_norm_dve(o, dve, 0)
            tail_dve(o, dve, 15)

        def attention_sp(sp):
            for k in range(2, 16):
                mrow_sp(sp, k)

        UNITS = [(e, b) for e in range(NE) for b in range(NB)]

        def moe_emptied(kind, n, m):
            if kind == "gate":
                return S["gbc_done"], n + 1
            if kind.startswith("route"):
                return {"route_x": (S["nx2_split"], 2 * n + 2), "route_lg": (S["lg_done"], n + 1),
                        "route_gT": (S["gT_done"], 2 * n + 2)}[kind]
            return (S["gelu_done"], FC * n + m + 1) if kind == "hid" else (S["moe_added"], n + 1)

        def route_fills(b):
            return [(kind, b, 0) for kind in ("route_x", "route_lg", "route_gT")]

        moe_fill = Fillings(bank[4:8], [name for n in range(len(UNITS)) for name in (route_fills(n) if n < NB else []) +
                                        [("gate", n, 0)] + [("hid", n, m) for m in range(FC)]] +
                            [("turn", b, 0) for b in range(NB)], moe_emptied)

        def route_pe(pe, b):
            if b >= 1:
                pe.wait_ge(S["nx2_ready"], b)
            ln_pe(pe, 2 * NB + b, moe_fill.take(pe, "route_x", b, 0))
            if b == 0:
                pe.wait_ge(S["moe_consts"], 1)
            pe.wait_ge(S["nx2_ready"], b + 1)
            if b >= 1:
                pe.wait_ge(S["lg_done"], b)
            out = moe_fill.take(pe, "route_lg", b, 0)
            for i in range(TPB):
                ins = pe.matmul(out[:, i * NE:(i + 1) * NE], nx2f[:, i * P:(i + 1) * P], gw[:, :], start=True, stop=True)
            ins.then_inc(S["lg_filled"], 1)
            pe.wait_ge(S["gates_done"], b + 1)
            if b >= 1:
                pe.wait_ge(S["gT_done"], 2 * b)
            out = moe_fill.take(pe, "route_gT", b, 0)
            for i in range(TPB):
                ins = pe.transpose(out[:, i * P:(i + 1) * P], gates[:, i, :], ident[:, :])
            ins.then_inc(S["gT_filled"], 1)

        def route_act(act, b):
            act.wait_ge(S["ln_turned"], 2 * NB + b + 1)
            if b >= 1:
                act.wait_ge(S["nx2_split"], 2 * b)
                act.wait_ge(S["lg_filled"], b)
            act.activation(nx2f[:, :], moe_fill.bank("route_x", b, 0)[:, :], ACT.Identity, scale=C("ln2_w"), bias=C("ln2_b")).then_inc(S["nx2_ready"], 1)
            act.wait_ge(S["lgm_done"], b + 1)
            act.activation(ex8[:, :, :], lg[:, :, :], ACT.Exp).then_inc(S["ex8_done"], 1)
            act.wait_ge(S["gT_filled"], b + 1)
            tt = slice(b * BLK, (b + 1) * BLK)
            act.activation(gT[0][:, tt], moe_fill.bank("route_gT", b, 0)[:, :], ACT.Copy).then_inc(S["gT_done"], 1)

        def route_norm_dve(o, dve, b):
            src = inner[:, b * TPB:(b + 1) * TPB, :]
            u = 2 * NB + b
            dve.wait_ge(S["att_done"], b + 1)
            ln_stats_dve(o, dve, u, src)
            ln_apply_dve(dve, u, src, xn, 0)

        def route_dve(o, dve, b):
            if b >= 1:
                route_norm_dve(o, dve, b)
            tt = slice(b * BLK, (b + 1) * BLK)
            dve.wait_ge(S["nx2_ready"], b + 1)
            dve.tensor_copy(nx2[0][:, tt], nx2f[:, :]).then_inc(S["nx2_split"], 1)
            dve.wait_ge(S["nx2_split"], 2 * b + 1)
            lo_part(dve, nx2[1][:, tt], nx2f[:, :], nx2[0][:, tt]).then_inc(S["nx2_split"], 1)
            dve.wait_ge(S["lg_filled"], b + 1)
            if b >= 1:
                dve.wait_ge(S["ex8_done"], b)
            dve.tensor_copy(lg[:, :, :], moe_fill.bank("route_lg", b, 0)[:, 0:TPB * NE].rearrange("p (i e) -> p i e", i=TPB)).then_inc(S["lg_done"], 1)
            dve.wait_ge(S["lg_done"], b + 1)
            shape = [P, TPB, NE, NE]
            other, own = lg[:, :, :].unsqueeze(2).broadcast_to(shape), lg[:, :, :].unsqueeze(3).broadcast_to(shape)
            o.did(dve.tensor_tensor(above[:, :, :, :], other, own, ALU.is_gt))
            o.did(dve.tensor_tensor(equal[:, :, :, :], other, own, ALU.is_equal))
            n_max = o.did(dve.tensor_reduce(lgm[:, :, 0], lg[:, :, :], AX.X, ALU.max))
            o.wait(n_max - 1)
            o.did(dve.tensor_tensor(equal[:, :, :, :], equal[:, :, :, :], lower8[:, :, :].unsqueeze(1).broadcast_to(shape), ALU.mult))
            o.wait(n_max)
            dve.tensor_tensor(lg[:, :, :], lg[:, :, :], lgm[:, :, :].broadcast_to([P, TPB, NE]), ALU.subtract).then_inc(S["lgm_done"], 1)
            o.wait()
            o.did(dve.tensor_tensor(above[:, :, :, :], above[:, :, :, :], equal[:, :, :, :], ALU.add))
            o.wait()
            o.did(dve.tensor_reduce(rank[:, :, :], above[:, :, :, :], AX.X, ALU.add))
            o.wait()
            dve.wait_ge(S["ex8_done"], b + 1)
            o.did(dve.scalar_tensor_tensor(rank[:, :, :], rank[:, :, :], 1.5, ex8[:, :, :], ALU.is_lt, ALU.mult))
            o.wait()
            o.did(dve.tensor_reduce(lgm[:, :, 0], rank[:, :, :], AX.X, ALU.add))
            o.wait()
            o.did(dve.reciprocal(lgm[:, :, 0], lgm[:, :, 0]))
            o.wait()
            if b >= 1:
                dve.wait_ge(S["gT_filled"], b)
            dve.tensor_tensor(gates[:, :, 0:NE], rank[:, :, :], lgm[:, :, :].broadcast_to([P, TPB, NE]),
                              ALU.mult).then_inc(S["gates_done"], 1)
            dve.wait_ge(S["gT_done"], 2 * b + 1)
            lo_part(dve, gT[1][:, tt], moe_fill.bank("route_gT", b, 0)[:, :], gT[0][:, tt]).then_inc(S["gT_done"], 1)

        def experts_up_pe(pe, n):
            e, b = UNITS[n]
            tt = slice(b * BLK, (b + 1) * BLK)
            if b == 0:
                pe.wait_ge(S["ew_split"], 2 * (e + 1))
            out = moe_fill.take(pe, "gate", n, 0)
            pe.matmul(out[:, :], sel8[:, e, :], gT[1][:, tt], start=True, stop=False)
            pe.matmul(out[:, :], sel8[:, e, :], gT[0][:, tt], start=False, stop=True).then_inc(S["gbc_filled"], 1)
            for m in range(FC):
                out = moe_fill.take(pe, "hid", n, m)
                mm3(pe, out[:, :], [w[:, e % 2, m, :] for w in ew], [x[:, tt] for x in nx2]).then_inc(S["hid_filled"], 1)

        def experts_down_pe(pe, n):
            e, b = UNITS[n]
            tt = slice(b * BLK, (b + 1) * BLK)
            if e == 0:
                mm3(pe, bank[b][:, :], [w[:, :] for w in b2], [x[:, tt] for x in gT], start=True, stop=False)
            pe.wait_ge(S["hid_split"], n + 1)
            for m in range(FC):
                ins = mm3(pe, bank[b][:, :], [w[:, e % 2, FC + m, :] for w in ew], [h[:, n % 2, m, :] for h in hids],
                          start=False, stop=(e == NE - 1 and m == FC - 1))
            ins.then_inc(S["down_done"], 1)

        def experts_act(act, n):
            e, b = UNITS[n]
            act.wait_ge(S["gbc_filled"], n + 1)
            if n >= 3:
                act.wait_ge(S["hid_split"], n - 2)
            act.activation(gate_bc[:, n % 3, :], moe_fill.bank("gate", n, 0)[:, :], ACT.Copy).then_inc(S["gbc_done"], 1)
            for m in range(FC):
                act.wait_ge(S["hid_filled"], FC * n + m + 1)
                act.activation(hid[:, n % 3, m, :], moe_fill.bank("hid", n, m)[:, :], ACT.Gelu,
                               bias=C("fc1_b", FC * e + m)).then_inc(S["gelu_done"], 1)

        def experts_hi_act(act, n):
            act.wait_ge(S["hid_gated"], n + 1)
            if n >= 2:
                act.wait_ge(S["down_done"], n - 1)
            act.activation(hids[0][:, n % 2, :, :], hid[:, n % 3, :, :], ACT.Copy).then_inc(S["hid_hi"], 1)

        def experts_dve(dve, n):
            dve.wait_ge(S["gbc_done"], n + 1)
            dve.wait_ge(S["gelu_done"], FC * n + FC)
            dve.tensor_tensor(hid[:, n % 3, :, :], hid[:, n % 3, :, :],
                              gate_bc[:, n % 3, :].unsqueeze(1).broadcast_to([P, FC, BLK]), ALU.mult).then_inc(S["hid_gated"], 1)

        def experts_lo_dve(dve, n):
            dve.wait_ge(S["hid_hi"], n + 1)
            if n >= 2:
                dve.wait_ge(S["down_done"], n - 1)
            lo_part(dve, hids[1][:, n % 2, :, :], hid[:, n % 3, :, :], hids[0][:, n % 2, :, :]).then_inc(S["hid_split"], 1)

        def split_weights_act(act, e):
            act.wait_ge(ew_in[e % 2], 16 * (e // 2 + 1))
            if e >= 2:
                act.wait_ge(S["down_done"], NB * (e - 1))
            act.activation(ew[0][:, e % 2, :, :], ew_raw[:, e % 2, :, :], ACT.Copy).then_inc(S["ew_split_hi"], 1)

        def split_weights_pool(pool, e):
            pool.wait_ge(S["ew_split_hi"], e + 1)
            lo_part(pool, ew[1][:, e % 2, :, :], ew_raw[:, e % 2, :, :], ew[0][:, e % 2, :, :]).then_inc(S["ew_split"], 2)

        ew_in = [sem("ew_in0"), sem("ew_in1")]

        def experts_sp(sp):
            for e in range(NE):
                if e >= 2:
                    sp.wait_ge(S["ew_split"], 2 * (e - 1))
                sp.dma_start(ew_raw[:, e % 2, :, :], a["experts"][e].rearrange("p (j m) -> p j m", m=P)).then_inc(ew_in[e % 2], 16)

        def experts_turn_pe(pe, b):
            out = moe_fill.take(pe, "turn", b, 0)
            pe.wait_ge(S["moe_copied"], b + 1)
            for i in range(TPB):
                ins = pe.transpose(out[:, i * P:(i + 1) * P], moe_sb[:, b % 2, i * P:(i + 1) * P], ident[:, :])
            ins.then_inc(S["moe_turned"], 1)

        def moe_pe(pe):
            pe.wait_ge(S["att_done"], NB)
            n = len(UNITS)
            for k in range(n + 2):
                if k < NB:
                    route_pe(pe, k)
                    pe.wait_ge(S["nx2_split"], 2 * k + 2)
                    pe.wait_ge(S["gT_done"], 2 * k + 2)
                if k < n:
                    experts_up_pe(pe, k)
                if k >= 2:
                    experts_down_pe(pe, k - 2)
                if k == n:
                    experts_turn_pe(pe, 0)
            for b in range(1, NB):
                experts_turn_pe(pe, b)

        def moe_act(act):
            act.wait_ge(S["att_done"], NB)
            route_act(act, 0)
            n = len(UNITS)
            for k in range(n + 1):
                if k < n:
                    if k % NB == 0:
                        if k == 0:
                            split_weights_act(act, 0)
                            split_weights_act(act, 1)
                    experts_act(act, k)
                if 1 <= k + 1 < NB:
                    route_act(act, k + 1)
                if k >= 1:
                    experts_hi_act(act, k - 1)
                if k % NB == 3 and 2 <= k // NB + 1 < NE:
                    split_weights_act(act, k // NB + 1)
                if k == n - NB + 1:
                    act.wait_ge(S["in_sw"], 32)
                    act.activation(sw[0][:, :, :], sw_raw[:, :, :], ACT.Copy).then_inc(S["sw_split"], 1)
            for b in range(NB):
                act.wait_ge(S["down_done"], len(UNITS) - NB + b + 1)
                if b >= 2:
                    act.wait_ge(S["moe_turned"], b - 1)
                act.activation(moe_sb[:, b % 2, :], bank[b][:, :], ACT.Copy).then_inc(S["moe_copied"], 1)

        def moe_dve(o, dve):
            dve.wait_ge(S["moe_pool_consts"], 1)
            o.did(dve.memset(gates[:, :, :], 0.0))
            o.did(dve.tensor_copy(sel8[:, :, :], ident[:, 0:NE].unsqueeze(2).broadcast_to([P, NE, P])))
            dve.wait_ge(S["in_moe"], 32)
            o.did(dve.tensor_copy(b2[0][:, :], b2_raw[:, :]))
            o.wait()
            lo_part(dve, b2[1][:, :], b2_raw[:, :], b2[0][:, :]).then_inc(S["moe_consts"], 1)
            route_dve(o, dve, 0)
            n = len(UNITS)
            for k in range(n + 1):
                if k + 1 < NB:
                    route_dve(o, dve, k + 1)
                if k < n:
                    experts_dve(dve, k)
                if k >= 1:
                    experts_lo_dve(dve, k - 1)
            for b in range(NB):
                dve.wait_ge(S["moe_turned"], b + 1)
                xb = x_tok[:, b * TPB:(b + 1) * TPB, :]
                dve.tensor_tensor(xb, moe_fill.bank("turn", b, 0)[:, :].rearrange("p (i d) -> p i d", i=TPB), xb,
                                  ALU.add).then_inc(S["moe_added"], 1)
                if b == 0:
                    dve.wait_ge(S["moe_added"], 1)
                    scan_front_dve(o, dve, 0, "stats")
                elif b == 1:
                    scan_front_dve(o, dve, 0, "apply")

        def moe_pool(o, pool):
            ln_pool(pool, 2 * NB)
            pool.wait_ge(S["att_done"], NB)
            o.did(pool.memset(lower8[:, :, :], 1.0))
            o.did(pool.memset(b2_raw[:, :], 0.0))
            o.wait()
            pool.affine_select(out=lower8[:, :, :], in_=lower8[:, :, :], compare_op=ALU.is_gt, fill=0.0, base=0,
                               pattern=[[1, NE], [-1, NE]], channel_multiplier=0).then_inc(S["moe_pool_consts"], 1)
            for b in range(NB):
                if b >= 1:
                    ln_pool(pool, 2 * NB + b)
                xb, ib = (t[:, b * TPB:(b + 1) * TPB, :] for t in (x_tok, inner))
                pool.tensor_tensor(xb, xb, ib, ALU.add)
                if b < 2:
                    split_weights_pool(pool, b)
            for e in range(2, NE):
                split_weights_pool(pool, e)
            pool.wait_ge(S["sw_split"], 1)
            lo_part(pool, sw[1][:, :, :], sw_raw[:, :, :], sw[0][:, :, :]).then_inc(S["sw_split"], 1)
            scan_pool(o, pool)

        W_IN, W_U, W_DB, W_DT, W_OUT = 0, 4, 8, 10, 12
        LN_C = 3 * NB

        FRONT_PE = [(0, "turn"), (2, "x"), (3, "z"), (8, "db"), (9, "u0"), (10, "u1"), (11, "dt")]
        FRONT_ACT = [(0, "hi"), (3, "x"), (6, "silu"), (8, "db"), (9, "u0"), (10, "u1"), (11, "dt"), (12, "softplus")]
        FRONT_DVE = [(-3, "stats"), (-1, "apply"), (1, "lo"), (4, "conv0"), (5, "conv1"), (7, "xc"), (9, "dB"), (13, "delta")]
        FRONT_POOL = [(-3, "ln")]
        EARLIEST = -3
        POST_Y, POST_PE, POST_DVE, POST_POOL = 3, 5, 6, 7
        FW_ACT, FW_POOL = {4: 0, 8: 1, 11: 2}, {5: 0, 9: 1, 12: 2}
        B_AHEAD, SUM_AFTER = 2, 3

        def front_parts(table, k):
            return [((k - at) // NS1 + 1, part) for at, part in table
                    if (k - at) % NS1 == 0 and 1 <= (k - at) // NS1 + 1 < NB]

        def part_names(part, b):
            return {"turn": [("x", b, 0)], "x": [("in", b, 0), ("in", b, 1)], "z": [("in", b, 2), ("in", b, 3)],
                    "u0": [("u", b, 0)], "u1": [("u", b, 1)], "db": [("db", b, 0)],
                    "dt": [("dt", b, 0), ("dt", b, 1)]}[part]

        def scan_emptied(kind, b, j):
            return {"x": (S["xT_lo"], NB + b + 1), "in": (S["c_in_read"], 4 * b + j + 1), "u": (S["c_u_read"], 2 * b + j + 1),
                    "db": (S["c_db_read"], b + 1), "dt": (S["c_dt_read"], 2 * b + j + 1),
                    "bbc": (S["bbc_done"], NS1 * b + j + 1), "out": (S["c_mixed"], b + 1)}[kind]

        names = [name for _, part in FRONT_PE for name in part_names(part, 0)]
        names += [("bbc", 0, n) for n in range(B_AHEAD)]
        for k in range(NB * NS1):
            b, n = divmod(k, NS1)
            if k + B_AHEAD < NB * NS1:
                names.append(("bbc", *divmod(k + B_AHEAD, NS1)))
            if n == POST_PE and b >= 1:
                names.append(("out", b - 1, 0))
            for nb, part in front_parts(FRONT_PE, k):
                names += part_names(part, nb)
        names.append(("out", NB - 1, 0))
        scan_fill = Fillings(bank[2:8], names, scan_emptied)

        def sweights(j):
            return [w[:, j, :] for w in sw]

        def scan_front_pe(pe, b, part):
            if part == "turn":
                ln_pe(pe, LN_C + b, scan_fill.take(pe, "x", b, 0))
            elif part in ("x", "z"):
                pe.wait_ge(S["xT_lo"], NB + b + 1)
                for j in (0, 1) if part == "x" else (2, 3):
                    out = scan_fill.take(pe, "in", b, j)
                    mm3(pe, out[:, :], sweights(W_IN + j), [x[:, :] for x in xT]).then_inc(S["c_in_filled"], 1)
            elif part in ("u0", "u1", "db"):
                pe.wait_ge(S["xc_split"], b + 1)
                m = 1 if part == "u1" else 0
                out = scan_fill.take(pe, part[0:1] if part != "db" else part, b, m)
                for k in range(2):
                    w = W_DB + k if part == "db" else W_U + 2 * k + m
                    ins = mm3(pe, out[:, :], sweights(w), [x[:, k, :] for x in xcs], start=(k == 0), stop=(k == 1))
                ins.then_inc(S["c_db_filled"] if part == "db" else S["c_u_filled"], 1)
            else:
                pe.wait_ge(S["dB_split"], b + 1)
                for m in range(2):
                    out = scan_fill.take(pe, "dt", b, m)
                    mm3(pe, out[:, :], sweights(W_DT + m), [x[:, b % 2, :] for x in dBs]).then_inc(S["c_dt_filled"], 1)

        def scan_front_act(o, act, b, part):
            if part == "hi":
                act.wait_ge(S["ln_turned"], LN_C + b + 1)
                if b >= 1:
                    act.wait_ge(S["c_in_filled"], 4 * b)
                act.activation(xT[0][:, :], scan_fill.bank("x", b, 0)[:, :], ACT.Copy).then_inc(S["xT_hi"], 1)
            elif part == "x":
                act.wait_ge(S["conv_hist"], NB + b + 1)
                for j in range(2):
                    act.wait_ge(S["c_in_filled"], 4 * b + j + 1)
                    act.activation(cin1[:, j, CONV - 1:], scan_fill.bank("in", b, j)[:, :], ACT.Identity,
                                   bias=C("in1_b", j)).then_inc(S["c_in_read"], 1)
            elif part == "silu":
                if b >= 2:
                    act.wait_ge(S["y1_split"], b - 1)
                for j in range(2):
                    act.wait_ge(S["c_in_filled"], 4 * b + j + 3)
                    act.activation(sz1[b % 2][:, j, :], scan_fill.bank("in", b, 2 + j)[:, :], ACT.Silu,
                                   bias=C("in1_b", 2 + j)).then_inc(S["c_in_read"], 1)
                for j in range(2):
                    act.wait_ge(S["conv_done"], 4 * NB + 2 * b + j + 1)
                    if b >= 1:
                        act.wait_ge(S["xc_split"], b)
                    act.activation(xc[:, j, :], cacc1[:, j, :], ACT.Silu, bias=C("conv1_b", j)).then_inc(S["xc_ready"], 1)
            elif part in ("u0", "u1"):
                m = int(part[1])
                act.wait_ge(S["c_u_filled"], 2 * b + m + 1)
                act.activation(u1[:, b % 2, m, :], scan_fill.bank("u", b, m)[:, :], ACT.Identity,
                               bias=C("xu_b", m)).then_inc(S["c_u_read"], 1)
            elif part == "db":
                if b >= 1:
                    act.wait_ge(S["dB_split"], b)
                act.wait_ge(S["c_db_filled"], b + 1)
                act.activation(dB[:, :], scan_fill.bank("db", b, 0)[:, :], ACT.Identity,
                               bias=C("xdB_b")).then_inc(S["c_db_read"], 1)
            elif part == "dt":
                for m in range(2):
                    act.wait_ge(S["c_dt_filled"], 2 * b + m + 1)
                    act.activation(dv1[:, m, :], scan_fill.bank("dt", b, m)[:, :], ACT.Identity,
                                   bias=C("dt1_b", m)).then_inc(S["c_dt_read"], 1)
            else:
                act.wait_ge(S["c_dt_read"], 2 * b + 2)
                o.did(act.activation(da1[:, :, :], dv1[:, :, :], ACT.Abs))
                o.wait()
                o.did(act.activation(da1[:, :, :], da1[:, :, :], ACT.Exp, scale=-1.0))
                o.wait()
                act.activation(da1[:, :, :], da1[:, :, :], ACT.Ln, bias=one[:, 0:1]).then_inc(S["dt_lnd"], 1)

        conv1_at = {}

        def scan_front_dve(o, dve, b, part):
            if part == "stats":
                ln_stats_dve(o, dve, LN_C + b, x_tok[:, b * TPB:(b + 1) * TPB, :], wait=False)
            elif part == "apply":
                dve.wait_ge(S["ln_rstd"], LN_C + b + 1)
                ln_apply_dve(dve, LN_C + b, x_tok[:, b * TPB:(b + 1) * TPB, :], xn, 0)
            elif part == "lo":
                dve.wait_ge(S["xT_hi"], NB + b + 1)
                lo_part(dve, xT[1][:, :], scan_fill.bank("x", b, 0)[:, :], xT[0][:, :]).then_inc(S["xT_lo"], 1)
                if b == 0:
                    dve.memset(cin1[:, :, 0:CONV - 1], 0.0).then_inc(S["conv_hist"], 1)
                else:
                    dve.tensor_copy(cin1[:, :, 0:CONV - 1], cin1[:, :, BLK:BLK + CONV - 1]).then_inc(S["conv_hist"], 1)
            elif part in ("conv0", "conv1"):
                if part == "conv0":
                    dve.wait_ge(S["conv_hist"], NB + b + 1)
                    if b >= 1:
                        dve.wait_ge(S["xc_ready"], 2 * b)
                for k in (0, 1) if part == "conv0" else (2, 3):
                    for j in range(2):
                        w = C("conv1_w", CONV * j + k)
                        if k == 0:
                            dve.wait_ge(S["c_in_read"], 4 * b + j + 1)
                            conv1_at[j] = o.did(dve.tensor_scalar(cacc1[:, j, :], cin1[:, j, 0:BLK], w, None, ALU.mult))
                            continue
                        o.wait(conv1_at[j])
                        ins = dve.scalar_tensor_tensor(cacc1[:, j, :], cin1[:, j, k:k + BLK], w, cacc1[:, j, :], ALU.mult, ALU.add)
                        if k < CONV - 1:
                            conv1_at[j] = o.did(ins)
                        else:
                            ins.then_inc(S["conv_done"], 1)
            elif part == "xc":
                dve.wait_ge(S["xc_ready"], 2 * b + 2)
                if b >= 1:
                    dve.wait_ge(S["c_u_filled"], 2 * b)
                o.did(dve.tensor_copy(xcs[0][:, :, :], xc[:, :, :]))
                o.wait()
                lo_part(dve, xcs[1][:, :, :], xc[:, :, :], xcs[0][:, :, :]).then_inc(S["xc_split"], 1)
            elif part == "dB":
                dve.wait_ge(S["c_db_read"], b + 1)
                if b >= 2:
                    dve.wait_ge(S["bbc_filled"], NS1 * (b - 1))
                o.did(dve.tensor_copy(dBs[0][:, b % 2, :], dB[:, :]))
                o.wait()
                lo_part(dve, dBs[1][:, b % 2, :], dB[:, :], dBs[0][:, b % 2, :]).then_inc(S["dB_split"], 1)
            else:
                dve.wait_ge(S["dt_lnd"], NB + b + 1)
                if b >= 2:
                    dve.wait_ge(S["decay_done"], NS1 * (b - 1))
                    dve.wait_ge(S["drive_done"], NS1 * (b - 1))
                o.did(dve.scalar_tensor_tensor(delta[:, b % 2, :, :], dv1[:, :, :], 0.0, da1[:, :, :], ALU.max, ALU.add))
                o.wait()
                dve.wait_ge(S["c_u_read"], 2 * b + 2)
                dve.tensor_tensor(du[:, b % 2, :, :], delta[:, b % 2, :, :], u1[:, b % 2, :, :], ALU.mult).then_inc(S["delta_ready"], 1)

        def state_b_pe(pe, b, n):
            out = scan_fill.take(pe, "bbc", b, n)
            pe.matmul(out[:, :], sel16[:, n, :], dBs[1][:, b % 2, :], start=True, stop=False)
            pe.matmul(out[:, :], sel16[:, n, :], dBs[0][:, b % 2, :], start=False, stop=True).then_inc(S["bbc_filled"], 1)

        def state_sum_pe(pe, b, n):
            pe.wait_ge(S["scanned"], NS1 * b + n + 1)
            if n == 0 and b >= 1:
                pe.wait_ge(S["y1_read"], b)
            for j in range(2):
                ins = pe.matmul(bank[j][:, :], ident[:, :], hst[:, (NS1 * b + n) % HBUF, j, :], start=(n == 0), stop=(n == NS1 - 1))
            ins.then_inc(S["summed"], 1)

        def state_act(act, b, n):
            k = NS1 * b + n
            act.wait_ge(S["bbc_filled"], k + 1)
            if k >= 2:
                act.wait_ge(S["drive_done"], k - 1)
            act.activation(b_bc[:, k % 2, :], scan_fill.bank("bbc", b, n)[:, :], ACT.Copy).then_inc(S["bbc_done"], 1)
            if n == 0:
                act.wait_ge(S["delta_ready"], b + 1)
            if k >= 2:
                act.wait_ge(S["scanned"], k - 1)
            act.activation(decay[:, k % 2, :, :], delta[:, b % 2, :, :], ACT.Exp, scale=-float(n + 1)).then_inc(S["decay_done"], 1)

        def state_pool(pool, b, n):
            k = NS1 * b + n
            pool.wait_ge(S["bbc_done"], k + 1)
            if n == 0:
                pool.wait_ge(S["delta_ready"], b + 1)
            if k >= 2:
                pool.wait_ge(S["scanned"], k - 1)
            pool.tensor_tensor(drive[:, k % 2, :, :], du[:, b % 2, :, :], b_bc[:, k % 2, :].unsqueeze(1).broadcast_to([P, 2, BLK]),
                               ALU.mult).then_inc(S["drive_done"], 1)

        def state_dve(o, dve, b, n):
            k = NS1 * b + n
            dve.wait_ge(S["decay_done"], k + 1)
            dve.wait_ge(S["drive_done"], k + 1)
            if k >= HBUF:
                dve.wait_ge(S["summed"], k - HBUF + 1)
                dve.wait_ge(S["hlast_done"], k - HBUF + 1)
            for j in range(2):
                init = 0.0 if b == 0 else hlast[:, n, j:j + 1]
                ins = dve.tensor_tensor_scan(hst[:, k % HBUF, j, :], decay[:, k % 2, j, :], drive[:, k % 2, j, :], init,
                                             ALU.mult, ALU.add)
            ins.then_inc(S["scanned"], 1)

        def state_last_dve(dve, b, n):
            k = NS1 * b + n
            dve.wait_ge(S["scanned"], k + 1)
            dve.tensor_copy(hlast[:, n, :], hst[:, k % HBUF, :, BLK - 1]).then_inc(S["hlast_done"], 1)

        def scan_y_dve(o, dve, b):
            dve.wait_ge(S["summed"], NS1 * (b + 1))
            u = u1[:, b % 2, :, :]
            for j in range(2):
                ins = dve.scalar_tensor_tensor(u[:, j, :], u[:, j, :], C("d1", j), bank[j][:, :], ALU.mult, ALU.add)
            ins.then_inc(S["y1_read"], 1)
            dve.wait_ge(S["y1_read"], b + 1)
            o.did(dve.tensor_tensor(u, u, sz1[b % 2][:, :, :], ALU.mult))
            o.wait()
            if b >= 1:
                dve.wait_ge(S["c_out_filled"], b)
            o.did(dve.tensor_copy(y1s[0][:, :, :], u))
            o.wait()
            lo_part(dve, y1s[1][:, :, :], u, y1s[0][:, :, :]).then_inc(S["y1_split"], 1)

        def scan_post_pe(pe, b):
            pe.wait_ge(S["y1_split"], b + 1)
            out = scan_fill.take(pe, "out", b, 0)
            for i in range(TPB):
                tt = slice(i * P, (i + 1) * P)
                for k in range(2):
                    ins = mm3(pe, out[:, tt], [y[:, k, tt] for y in y1s], sweights(W_OUT + k), start=(i == 0 and k == 0), stop=(k == 1))
            ins.then_inc(S["c_out_filled"], 1)

        def scan_post_dve(dve, b):
            dve.wait_ge(S["c_out_filled"], b + 1)
            xb = x_tok[:, b * TPB:(b + 1) * TPB, :]
            dve.tensor_tensor(xb, scan_fill.bank("out", b, 0)[:, :].rearrange("p (i d) -> p i d", i=TPB), xb,
                              ALU.add).then_inc(S["c_mixed"], 1)

        def scan_pe(pe):
            pe.wait_ge(S["sw_split"], 2)
            pe.wait_ge(S["moe_added"], NB)
            for _, part in FRONT_PE:
                scan_front_pe(pe, 0, part)
            pe.wait_ge(S["sel16_done"], 1)
            for k in range(B_AHEAD):
                state_b_pe(pe, 0, k)
            for k in range(NB * NS1 + SUM_AFTER):
                b, n = divmod(k, NS1)
                if k + B_AHEAD < NB * NS1:
                    state_b_pe(pe, *divmod(k + B_AHEAD, NS1))
                if k >= SUM_AFTER:
                    state_sum_pe(pe, *divmod(k - SUM_AFTER, NS1))
                if b == NB:
                    continue
                if n == POST_PE and b >= 1:
                    scan_post_pe(pe, b - 1)
                for nb, part in front_parts(FRONT_PE, k):
                    scan_front_pe(pe, nb, part)
            scan_post_pe(pe, NB - 1)

        def scan_act(o, act):
            act.wait_ge(S["moe_added"], NB)
            for _, part in FRONT_ACT:
                scan_front_act(o, act, 0, part)
            for b in range(NB):
                for n in range(NS1):
                    state_act(act, b, n)
                    for nb, part in front_parts(FRONT_ACT, NS1 * b + n):
                        scan_front_act(o, act, nb, part)
                    if n in FW_ACT and 3 * b + FW_ACT[n] < 11:
                        fweights_act(act, 3 * b + FW_ACT[n])

        def scan_dve(o, dve):
            dve.wait_ge(S["moe_added"], NB)
            for _, part in FRONT_DVE[2:]:
                scan_front_dve(o, dve, 0, part)
                if part == "conv1":
                    dve.tensor_copy(sel16[:, :, :], ident[:, NS1:2 * NS1].unsqueeze(2).broadcast_to([P, NS1, P])).then_inc(S["sel16_done"], 1)
            for k in range(EARLIEST, 0):
                for nb, part in front_parts(FRONT_DVE, k):
                    scan_front_dve(o, dve, nb, part)
            for b in range(NB):
                for n in range(NS1):
                    if n == POST_Y and b >= 1:
                        scan_y_dve(o, dve, b - 1)
                    state_dve(o, dve, b, n)
                    if b or n:
                        state_last_dve(dve, *divmod(NS1 * b + n - 1, NS1))
                    if n == POST_DVE and b >= 1:
                        scan_post_dve(dve, b - 1)
                    for nb, part in front_parts(FRONT_DVE, NS1 * b + n):
                        scan_front_dve(o, dve, nb, part)
            state_last_dve(dve, NB - 1, NS1 - 1)
            scan_y_dve(o, dve, NB - 1)
            net_norm_dve(o, dve, 0)
            scan_post_dve(dve, NB - 1)

        def scan_bias_pool(pool, b):
            pool.wait_ge(S["c_mixed"], b + 1)
            xb = x_tok[:, b * TPB:(b + 1) * TPB, :]
            pool.tensor_tensor(xb, xb, out1_b[:, :].unsqueeze(1).broadcast_to([P, TPB, D]), ALU.add).then_inc(S["x1_done"], 1)

        def scan_pool(o, pool):
            ln_pool(pool, LN_C)
            pool.wait_ge(S["in_sw"], 32)
            for k in range(EARLIEST, 0):
                for nb, _ in front_parts(FRONT_POOL, k):
                    ln_pool(pool, LN_C + nb)
            for b in range(NB):
                for n in range(NS1):
                    state_pool(pool, b, n)
                    for nb, _ in front_parts(FRONT_POOL, NS1 * b + n):
                        ln_pool(pool, LN_C + nb)
                    if n == POST_POOL and b >= 1:
                        scan_bias_pool(pool, b - 1)
                    if n in FW_POOL and 3 * b + FW_POOL[n] < 11:
                        fweights_pool(pool, 3 * b + FW_POOL[n])
            ln_pool(pool, LN_D)
            scan_bias_pool(pool, NB - 1)
            for b in range(1, NB):
                ln_pool(pool, LN_D + b)

        W_1, W_2, W_H1, W_H2, W_3 = 0, HC, 2 * HC, 2 * HC + HC * HC, 2 * HC + 2 * HC * HC
        LN_D = 4 * NB

        def net_names(b):
            return [(w, b, m) for m in range(HC) for w in ("w1", "w2")] + ([("turn", b - 1, 0)] if b else []) + \
                   [(w, b, m) for w in ("h1", "h2") for m in range(HC)] + ([("x", b + 1, 0)] if b + 1 < NB else []) + [("w3", b, 0)]

        def net_emptied(kind, b, m):
            return {"x": (S["xT_lo"], 2 * NB + b + 1), "w1": (S["f_a_done"], HC * b + m + 1), "w2": (S["f_prod"], HC * b + m + 1),
                    "h1": (S["f_g_hi"], 2 * HC * b + m + 1), "h2": (S["f_g_hi"], 2 * HC * b + HC + m + 1),
                    "w3": (S["f_o_done"], b + 1), "turn": (S["f_added"], b + 1)}[kind]

        net_fill = Fillings(bank, [("x", 0, 0)] + [x for b in range(NB) for x in net_names(b)] + [("turn", NB - 1, 0)], net_emptied)

        def fweights(j):
            return [w[:, j, :] for w in fw]

        def net_turn_pe(pe, b):
            out = net_fill.take(pe, "turn", b, 0)
            pe.wait_ge(S["f_o_done"], b + 1)
            for i in range(TPB):
                ins = pe.transpose(out[:, i * P:(i + 1) * P], fo[:, b % 2, i * P:(i + 1) * P], ident[:, :])
            ins.then_inc(S["f_turned"], 1)

        def net_pe(pe):
            pe.wait_ge(S["c_mixed"], NB)
            pe.wait_ge(S["fw_split"], 2 * 11)
            ln_pe(pe, LN_D, net_fill.take(pe, "x", 0, 0))
            for b in range(NB):
                pe.wait_ge(S["xT_lo"], 2 * NB + b + 1)
                for m in range(HC):
                    for name, w0 in (("w1", W_1), ("w2", W_2)):
                        mm3(pe, net_fill.take(pe, name, b, m)[:, :], fweights(w0 + m), [x[:, :] for x in xT]).then_inc(S["f_filled"], 1)
                if b >= 1:
                    net_turn_pe(pe, b - 1)
                for l, (name, w0) in enumerate((("h1", W_H1), ("h2", W_H2))):
                    for m in range(HC):
                        out = net_fill.take(pe, name, b, m)
                        for k in range(HC):
                            if m == 0:
                                pe.wait_ge(S["f_split"], 3 * HC * b + HC * l + k + 1)
                            ins = mm3(pe, out[:, :], fweights(w0 + HC * k + m), [h[:, l, k, :] for h in fhs],
                                      start=(k == 0), stop=(k == HC - 1))
                        ins.then_inc(S["f_filled"], 1)
                if b + 1 < NB:
                    ln_pe(pe, LN_D + b + 1, net_fill.take(pe, "x", b + 1, 0))
                out = net_fill.take(pe, "w3", b, 0)
                for k in range(HC):
                    pe.wait_ge(S["f_split"], 3 * HC * b + 2 * HC + k + 1)
                    ins = mm3(pe, out[:, :], fweights(W_3 + k), [h[:, 2, k, :] for h in fhs], start=(k == 0), stop=(k == HC - 1))
                ins.then_inc(S["f_filled"], 1)
            net_turn_pe(pe, NB - 1)

        FPB = 4 * HC + 1

        def net_hi_act(act, b):
            act.wait_ge(S["ln_turned"], LN_D + b + 1)
            act.activation(xT[0][:, :], net_fill.bank("x", b, 0)[:, :], ACT.Copy).then_inc(S["xT_hi"], 1)

        def net_act(act):
            act.wait_ge(S["c_mixed"], NB)
            net_hi_act(act, 0)
            for b in range(NB):
                for m in range(HC):
                    act.wait_ge(S["f_filled"], FPB * b + 2 * m + 1)
                    if HC * b + m >= 2:
                        act.wait_ge(S["f_prod"], HC * b + m - 1)
                    act.activation(fa[:, m % 2, :], net_fill.bank("w1", b, m)[:, :], ACT.Silu,
                                   scale=C("w1_s", m)).then_inc(S["f_a_done"], 1)
                for m in range(HC):
                    act.wait_ge(S["f_prod"], HC * b + m + 1)
                    act.activation(fhs[0][:, 0, m, :], fh[:, m, :], ACT.Copy).then_inc(S["f_hi"], 1)
                for l, scale in enumerate(("h1_s", "h2_s")):
                    for m in range(HC):
                        act.wait_ge(S["f_filled"], FPB * b + 2 * HC + HC * l + m + 1)
                        act.wait_ge(S["f_split"], 3 * HC * b + HC * l + m + 1)
                        src = net_fill.bank("h1" if l == 0 else "h2", b, m)[:, :]
                        act.activation(fh[:, m, :], src, ACT.Gelu, scale=C(scale, m))
                        act.activation(fhs[0][:, l + 1, m, :], src, ACT.Gelu, scale=C(scale, m)).then_inc(S["f_g_hi"], 1)
                if b + 1 < NB:
                    net_hi_act(act, b + 1)
                act.wait_ge(S["f_filled"], FPB * (b + 1))
                if b >= 2:
                    act.wait_ge(S["f_turned"], b - 1)
                act.activation(fo[:, b % 2, :], net_fill.bank("w3", b, 0)[:, :], ACT.Identity, scale=C("w3_s")).then_inc(S["f_o_done"], 1)

        def net_norm_dve(o, dve, b):
            src = x_tok[:, b * TPB:(b + 1) * TPB, :]
            dve.wait_ge(S["x1_done"], b + 1)
            ln_stats_dve(o, dve, LN_D + b, src)
            ln_apply_dve(dve, LN_D + b, src, xn, 0)

        def net_lo_dve(dve, b):
            dve.wait_ge(S["xT_hi"], 2 * NB + b + 1)
            lo_part(dve, xT[1][:, :], net_fill.bank("x", b, 0)[:, :], xT[0][:, :]).then_inc(S["xT_lo"], 1)

        def net_add_dve(dve, b):
            src = x_tok[:, b * TPB:(b + 1) * TPB, :]
            dve.wait_ge(S["f_turned"], b + 1)
            dve.tensor_tensor(src, net_fill.bank("turn", b, 0)[:, :].rearrange("p (i d) -> p i d", i=TPB), src,
                              ALU.add).then_inc(S["f_added"], 1)

        def net_dve(o, dve):
            net_lo_dve(dve, 0)
            for b in range(NB):
                for m in range(HC):
                    dve.wait_ge(S["f_filled"], FPB * b + 2 * m + 2)
                    dve.wait_ge(S["f_a_done"], HC * b + m + 1)
                    if b >= 1:
                        dve.wait_ge(S["f_split"], 3 * HC * b)
                    dve.scalar_tensor_tensor(fh[:, m, :], net_fill.bank("w2", b, m)[:, :], C("w2_s", m), fa[:, m % 2, :],
                                             ALU.mult, ALU.mult).then_inc(S["f_prod"], 1)
                for l in range(3):
                    for m in range(HC):
                        if l == 0:
                            dve.wait_ge(S["f_hi"], HC * b + m + 1)
                        else:
                            dve.wait_ge(S["f_g_hi"], 2 * HC * b + HC * (l - 1) + m + 1)
                        lo_part(dve, fhs[1][:, l, m, :], fh[:, m, :], fhs[0][:, l, m, :]).then_inc(S["f_split"], 1)
                    if l == 0 and b >= 1:
                        net_add_dve(dve, b - 1)
                    if l == 1 and b + 1 < NB:
                        net_norm_dve(o, dve, b + 1)
                if b + 1 < NB:
                    net_lo_dve(dve, b + 1)
            net_add_dve(dve, NB - 1)

        def fweights_sp(sp):
            for c in range(11):
                if c >= 2:
                    sp.wait_ge(S["fw_split"], 2 * (c - 1))
                sp.dma_start(fw_raw[:, c % 2, :, :], a["net"][:, c * 4 * P:(c + 1) * 4 * P].rearrange("p (j m) -> p j m", m=P)
                             ).then_inc(fw_in[c % 2], 16)

        fw_in = [sem("fw_in0"), sem("fw_in1")]

        def fweights_act(act, c):
            act.wait_ge(fw_in[c % 2], 16 * (c // 2 + 1))
            act.activation(fw[0][:, 4 * c:4 * c + 4, :], fw_raw[:, c % 2, :, :], ACT.Copy).then_inc(S["fw_hi"], 1)

        def fweights_pool(pool, c):
            pool.wait_ge(S["fw_hi"], c + 1)
            lo_part(pool, fw[1][:, 4 * c:4 * c + 4, :], fw_raw[:, c % 2, :, :], fw[0][:, 4 * c:4 * c + 4, :]).then_inc(S["fw_split"], 2)

        block = ctx.enter_context(nc.Block())

        @block.sync
        def _(sp):
            sp.dma_start(x_tok[:, :, :], a["x"].rearrange("b (i p) d -> p (b i) d", p=P)).then_inc(S["in_x"], 16)
            sp.dma_start(cols[:, :], a["cols"]).then_inc(S["in_x"], 16)
            sp.dma_start(w_raw[:, :], a["win"]).then_inc(S["in_win"], 16)
            sp.dma_start(wg_raw[:, :, :], a["wgo"].rearrange("p (j m) -> p j m", m=P)).then_inc(S["in_wg"], 16)
            sp.dma_start(wqkv_raw[:, :, :], a["wqkv"].rearrange("p (j m) -> p j m", m=P)).then_inc(S["in_wo"], 16)
            sp.dma_start(wo[:, :], a["wo"]).then_inc(S["in_wo"], 16)
            sp.dma_start(bv[:, :], a["bv"].partition_broadcast(P)).then_inc(S["in_wo"], 16)
            sp.dma_start(bo[:, :], a["bo"].partition_broadcast(P)).then_inc(S["in_wo"], 16)
            sp.wait_ge(S["x_mixed"], NB)
            for b in range(NB):
                qkv_sp(sp, b)
                if b in (1, 2):
                    mrow_sp(sp, b - 1)
            attention_sp(sp)
            sp.wait_ge(S["moe_pool_consts"], 1)
            sp.dma_start(b2_raw[0:NE, :], a["fc2_b"]).then_inc(S["in_moe"], 16)
            sp.dma_start(gw[:, :], a["gate_w"]).then_inc(S["in_moe"], 16)
            experts_sp(sp)
            sp.dma_start(sw_raw[:, :, :], a["scan"].rearrange("p (j m) -> p j m", m=P)).then_inc(S["in_sw"], 16)
            sp.dma_start(out1_b[:, :], a["out1_b"].partition_broadcast(P)).then_inc(S["in_sw"], 16)
            sp.wait_ge(S["moe_added"], NB)
            fweights_sp(sp)
            for b in range(NB):
                sp.wait_ge(S["f_added"], b + 1)
                tiles = slice(b * TPB, (b + 1) * TPB)
                sp.dma_start(a["out"].rearrange("b (i p) d -> p (b i) d", p=P)[:, tiles, :], x_tok[:, tiles, :]).then_inc(S["stored"], 16)
            sp.wait_ge(S["stored"], 16 * NB)

        @block.gpsimd
        def _(pool):
            o = Order(pool, S["pool_order"])
            o.did(pool.memset(ident[:, :], 0.0))
            o.did(pool.memset(tri[:, :], 1.0))
            o.did(pool.memset(headmask[:, :, :], 1.0))
            o.did(pool.memset(maskneg[:, :], 0.0))
            o.did(pool.memset(mhalf[:, :], -0.5))
            o.did(pool.memset(one[:, :], 1.0))
            o.wait()
            o.did(pool.affine_select(out=ident[:, :], in_=ident[:, :], compare_op=ALU.not_equal, fill=1.0, base=0,
                                     pattern=[[-1, P]], channel_multiplier=1))
            o.did(pool.affine_select(out=tri[:, :], in_=tri[:, :], compare_op=ALU.is_ge, fill=0.0, base=0,
                                     pattern=[[1, P]], channel_multiplier=-1))
            o.did(pool.affine_select(out=maskneg[:, :], in_=maskneg[:, :], compare_op=ALU.is_ge, fill=NEG, base=0,
                                     pattern=[[1, P]], channel_multiplier=-1))
            o.did(pool.affine_select(out=headmask[:, :, :], in_=headmask[:, :, :], compare_op=ALU.is_ge, fill=0.0, base=0,
                                     pattern=[[-NS0, H0], [0, HD0]], channel_multiplier=1))
            o.wait()
            pool.affine_select(out=headmask[:, :, :], in_=headmask[:, :, :], compare_op=ALU.is_ge, fill=0.0, base=NS0 - 1,
                               pattern=[[NS0, H0], [0, HD0]], channel_multiplier=-1).then_inc(S["consts"], 1)
            pool.wait_ge(S["w_split"], 1)
            lo_part(pool, win[1][:, :, :], w_raw[:, :].rearrange("p (j m) -> p j m", m=P), win[0][:, :, :]).then_inc(S["w_split"], 1)
            for n in range(5):
                front_pool(o, pool, 0, n)
            pool.wait_ge(S["w_split"], 3)
            lo_part(pool, wgo[1][:, :, :], wg_raw[:, :, :], wgo[0][:, :, :]).then_inc(S["w_split"], 1)
            for g in range(G_END):
                for what, b, n in sorted(mixer_parts(g), key=lambda part: part[2] != 0):
                    if what == "front":
                        front_pool(o, pool, b, n)
                    else:
                        end_pool(o, pool, b, n)
            pool.wait_ge(S["qkv_split"], 1)
            lo_part(pool, wqkv[1][:, :, :], wqkv_raw[:, :, :], wqkv[0][:, :, :]).then_inc(S["qkv_split"], 1)
            pool.wait_ge(S["x_mixed"], NB)
            ln_pool(pool, NB, double=True)
            o.did(pool.memset(kz[:, 0::2, :].bitcast(mybir.dt.uint32), 0))
            o.wait()
            o.did(pool.memset(kz[32:64, 0::2, :].bitcast(mybir.dt.uint32), 0x3F803F80))
            o.wait()
            pool.wait_ge(S["in_wo"], 64)
            for b in range(NB):
                if b:
                    ln_pool(pool, NB + b, double=True)
                pool.wait_ge(S["inner_ready"], b + 1)
                ib = inner[:, b * TPB:(b + 1) * TPB, :]
                pool.tensor_tensor(ib, ib, bo[:, :].unsqueeze(1).broadcast_to([P, TPB, D]), ALU.add).then_inc(S["bo_added"], 1)
            moe_pool(o, pool)

        @block.scalar
        def _(act):
            o = Order(act, S["act_order"])
            act.wait_ge(S["in_x"], 32)
            act.activation(a_neg[:, :], C("a_log"), ACT.Exp).then_inc(S["a_ready"], 1)
            act.wait_ge(S["in_win"], 16)
            act.activation(win[0][:, :, :], w_raw[:, :].rearrange("p (j m) -> p j m", m=P), ACT.Copy).then_inc(S["w_split"], 1)
            for n in range(5):
                front_act(o, act, 0, n)
            act.wait_ge(S["in_wg"], 16)
            act.wait_ge(S["w_split"], 2)
            act.activation(wgo[0][:, :, :], wg_raw[:, :, :], ACT.Copy).then_inc(S["w_split"], 1)
            for g in range(G_END):
                if g < G:
                    chunk_act(act, g)
                for what, b, n in mixer_parts(g):
                    if what == "front":
                        front_act(o, act, b, n)
                    else:
                        end_act(act, b, n)
            act.wait_ge(S["in_wo"], 64)
            act.activation(wqkv[0][:, :, :], wqkv_raw[:, :, :], ACT.Copy).then_inc(S["qkv_split"], 1)
            act.wait_ge(S["x_mixed"], NB)
            act.activation(v9[:, :], one[:, 0:1].broadcast_to([P, NT * VW + 32]), ACT.Copy).then_inc(S["v_ones"], 1)
            act.activation(qa[:, :, :].bitcast(F32), one[:, 0:1].unsqueeze(2).broadcast_to([P, HA // 2, T // 2]), ACT.Copy,
                           scale=0.0).then_inc(S["qk_cleared"], 1)
            for b in range(NB):
                qkv_act(act, b)
                if b == 0:
                    o.did(act.activation(kz[:, 1::2, :].bitcast(F32), one[:, 0:1].unsqueeze(2).broadcast_to([P, HA // 2, T // 2]),
                                         ACT.Copy, scale=0.0))
                    o.wait()
                    act.activation(kz[96:128, 1::2, :], one[96:128, 0:1].unsqueeze(2).broadcast_to([32, HA // 2, T]),
                                   ACT.Copy).then_inc(S["qk_cleared"], 1)
            attention_act(act)
            moe_act(act)
            scan_act(o, act)
            net_act(act)

        @block.vector
        def _(dve):
            o = Order(dve, S["dve_order"])
            dve.memset(state[:, 0, :], 0.0).then_inc(S["state_done"], 1)
            dve.wait_ge(S["consts"], 1)
            o.did(dve.tensor_copy(tri_r[:, :], tri[:, :]))
            o.did(dve.tensor_scalar(negtri_r[:, :], tri[:, :], -1.0, None, ALU.mult))
            o.did(dve.tensor_copy(identb[:, :], ident[:, :]))
            dve.wait_ge(S["a_ready"], 1)
            dve.tensor_scalar(a_neg[:, :], a_neg[:, :], -1.0, None, ALU.mult).then_inc(S["consts_r"], 1)
            dve.wait_ge(S["consts_r"], 1)
            dve.wait_ge(S["in_x"], 32)
            for n in range(5):
                front_early_dve(o, dve, 0, n)
                front_late_dve(o, dve, 0, n)
            for g in range(G_END):
                if g < G:
                    chunk_front_dve(dve, g)
                for what, b, n in mixer_parts(g):
                    if what == "front":
                        front_early_dve(o, dve, b, n)
                    else:
                        end_early_dve(o, dve, b, n)
                if 1 <= g <= G:
                    chunk_back_dve(o, dve, g - 1)
                if g < G:
                    chunk_mid_dve(dve, g)
                for what, b, n in mixer_parts(g):
                    if what == "front":
                        front_late_dve(o, dve, b, n)
                    else:
                        end_late_dve(o, dve, b, n)
            dve.wait_ge(S["x_mixed"], NB)
            dve.wait_ge(S["in_wo"], 64)
            for b in range(NB):
                qkv_dve(o, dve, b)
                if b in (1, 2):
                    first_maxima_dve(o, dve, b - 1)
            dve.wait_ge(S["bo_added"], NB)
            attention_dve(o, dve)
            moe_dve(o, dve)
            scan_dve(o, dve)
            net_dve(o, dve)

        @block.tensor
        def _(pe):
            pe.wait_ge(S["consts"], 1)
            pe.wait_ge(S["consts_r"], 1)
            for n in range(5):
                front_pe(pe, 0, n)
            for g in range(G_END):
                if g < G:
                    chunk_front_pe(pe, g)
                if 1 <= g <= G:
                    chunk_back_pe(pe, g - 1)
                for what, b, n in mixer_parts(g):
                    if what == "front":
                        front_pe(pe, b, n)
                    else:
                        end_pe(pe, b, n)
            pe.wait_ge(S["x_mixed"], NB)
            pe.wait_ge(S["in_wo"], 64)
            for b in range(NB):
                qkv_pe(pe, b)
                if b in (1, 2):
                    first_maxima_pe(pe, b - 1)
            pe.wait_ge(S["qk_evac"], 2 * NB)
            pe.wait_ge(S["v_done"], NB)
            attention_pe(pe)
            moe_pe(pe)
            scan_pe(pe)
            net_pe(pe)


def host_layout(x):
    import numpy as np

    win = x["L0_attn_W_in"]
    rows = [win[3 * DI:3 * DI + P], win[3 * DI + P:3 * DI + 2 * P],
            np.tile(win[4 * DI:4 * DI + NS0], (H0, 1)), np.tile(win[4 * DI + NS0:4 * DI + 2 * NS0], (H0, 1)),
            np.repeat(win[4 * DI + 2 * NS0:], NS0, axis=0),
            win[0:P], win[P:2 * P], win[DI:DI + P], win[DI + P:2 * DI]]
    out = {"x": x["L0_attn_u"], "win": np.concatenate(rows, 0).T}

    def kxm(w, k, m):
        return w.reshape(k, P, m, P).transpose(1, 0, 2, 3).reshape(P, k * m * P)

    out["wgo"] = np.concatenate([kxm(x["L0_attn_W_gate"].T, 2, 2), kxm(x["L0_attn_W_out"].T, 4, 1)], 1)

    wqkv = x["L0_ffn_Wqkv"]
    out["wqkv"] = wqkv
    out["wo"] = x["L0_ffn_Wo"]
    out["bv"], out["bo"] = x["L0_ffn_bqkv"][2 * P:], x["L0_ffn_bo"]
    out["experts"] = np.concatenate(
        [x["L0_ffn_fc1_w"].transpose(0, 2, 1), np.stack([kxm(w.T, FC, 1) for w in x["L0_ffn_fc2_w"]])], 2)
    out["fc2_b"], out["gate_w"] = x["L0_ffn_fc2_b"], x["L0_ffn_gate_W"]
    xw, dw = x["L1_attn_x_proj_w"], x["L1_attn_dt_proj_w"]
    xdb = np.zeros((DI, P), np.float32)
    xdb[:, 0:2 * NS1] = xw[:, 0:2 * NS1]
    dtw = np.zeros((P, DI), np.float32)
    dtw[0:NS1] = dw
    out["scan"] = np.concatenate([x["L1_attn_in_proj_w"], kxm(xw[:, 2 * NS1:], 2, 2), kxm(xdb, 2, 1), dtw,
                                  kxm(x["L1_attn_out_proj_w"], 2, 1)], 1)
    out["out1_b"] = x["L1_attn_out_proj_b"]
    out["net"] = np.concatenate([x["L1_ffn_w1_w"].T, x["L1_ffn_w2_w"].T, kxm(x["L1_ffn_h1_w"].T, HC, HC),
                                 kxm(x["L1_ffn_h2_w"].T, HC, HC), kxm(x["L1_ffn_w3_w"].T, HC, 1)], 1)

    def vec(v, n):
        return np.asarray(v).reshape(n, P).T

    cw = x["L0_attn_conv_w"][:, 0, :]
    cb = x["L0_attn_conv_b"]
    conv = [cw[0:P], cw[P:DI], np.tile(cw[DI:DI + NS0], (H0, 1)), np.tile(cw[DI + NS0:], (H0, 1))]
    convb = [cb[0:P], cb[P:DI], np.tile(cb[DI:DI + NS0], H0), np.tile(cb[DI + NS0:], H0)]
    c1 = x["L1_attn_conv_w"][:, 0, :]
    xpb = x["L1_attn_x_proj_b"]
    pad = np.zeros(P - 2 * NS1, np.float32)
    put = {
        "conv0_w": np.concatenate(conv, 1), "conv0_b": np.stack(convb, 1),
        "dt_bias": np.repeat(x["L0_attn_dt_bias"], NS0)[:, None], "a_log": np.repeat(x["L0_attn_A_log"], NS0)[:, None],
        "d0": vec(np.repeat(x["L0_attn_D_param"], HD0), 2), "gamma": vec(x["L0_attn_ln_gamma"], 2),
        "beta": vec(x["L0_attn_ln_beta"], 2), "b_gate": vec(x["L0_attn_b_gate"], 2),
        "ln1_w": vec(x["L0_ffn_ln1_w"], 1), "ln1_b": vec(x["L0_ffn_ln1_b"], 1),
        "ln2_w": vec(x["L0_ffn_ln2_w"], 1), "ln2_b": vec(x["L0_ffn_ln2_b"], 1),
        "bq": vec(x["L0_ffn_bqkv"][0:P], 1), "bk": vec(x["L0_ffn_bqkv"][P:2 * P], 1),
        "fc1_b": vec(x["L0_ffn_fc1_b"], NE * FC), "in1_b": vec(x["L1_attn_in_proj_b"], 4),
        "conv1_w": np.concatenate([c1[0:P], c1[P:]], 1), "conv1_b": vec(x["L1_attn_conv_b"], 2),
        "xu_b": vec(xpb[2 * NS1:], 2), "xdB_b": vec(np.concatenate([xpb[0:2 * NS1], pad]), 1),
        "dt1_b": vec(x["L1_attn_dt_proj_b"], 2),
        "d1": vec(x["L1_attn_D"], 2), "w1_s": vec(x["L1_ffn_w1_s"], HC), "w2_s": vec(x["L1_ffn_w2_s"], HC),
        "h1_s": vec(x["L1_ffn_h1_s"], HC), "h2_s": vec(x["L1_ffn_h2_s"], HC), "w3_s": vec(x["L1_ffn_w3_s"], 1),
        "out1_b": vec(x["L1_attn_out_proj_b"], 1),
    }
    out["cols"] = np.concatenate([put[n] for n, _ in _COLS], 1)
    return {k: np.ascontiguousarray(v) for k, v in out.items()}


def kernel(**inputs):
    import numpy as np
    import concourse.bacc as bacc
    from concourse.bass_utils import run_bass_kernel_spmd

    arrays = host_layout({name: np.asarray(v) for name, v in inputs.items()})
    nc = bacc.Bacc("TRN2", target_bir_lowering=False, num_devices=1)
    tensors = {name: nc.dram_tensor(name + "_dram", v.shape, mybir.dt.from_np(v.dtype), kind="ExternalInput").ap()
               for name, v in arrays.items()}
    tensors["out"] = nc.dram_tensor("out_dram", (1, T, D), F32, kind="ExternalOutput").ap()
    build(nc, tensors)
    r = run_bass_kernel_spmd(nc, [{name + "_dram": v for name, v in arrays.items()}], core_ids=[0])
    return r.results[0]["out_dram"]
```
